# Optimizing a Trainium2 kernel written in Bass

```python
import numpy as np
import jax
import jax.numpy as jnp

def _softmax(x, axis=-1):
    return jax.nn.softmax(x, axis=axis)

def _gelu(x):
    return jax.nn.gelu(x, approximate=True)

def _silu(x):
    return jax.nn.silu(x)

def _sigmoid(x):
    return jax.nn.sigmoid(x)

def _layernorm(x, axis=-1, eps=1e-05):
    m = jnp.mean(x, axis=axis, keepdims=True)
    v = jnp.var(x, axis=axis, keepdims=True)
    return (x - m) / jnp.sqrt(v + eps)

def _scatter_add(tgt, idx, src, axis=0):
    return tgt.at[idx].add(src)

def _segment_sum(src, seg, n):
    return jax.ops.segment_sum(src, seg, n)
kernel_name = 'mk_gnn_resnorm_d4_gnn_r32_4dd994'

def setup_inputs(seed: int=0):
    np.random.seed(seed)
    _w = jnp.asarray

    def _rec_inputs():
        import jax
        import jax.numpy as jnp
        _gk = jax.random.key(seed)
        x = -0.000202 + 1 * jax.random.normal(jax.random.fold_in(_gk, 1), (3125, 64), jnp.float32)
        _s = jax.random.randint(jax.random.fold_in(_gk, 2), (50000,), 0, 3125, jnp.int32)
        _d = jax.random.randint(jax.random.fold_in(_gk, 3), (50000,), 0, 3125, jnp.int32)
        _loop = jnp.arange(3125, dtype=jnp.int32)
        src = jnp.concatenate([_s, _d, _loop])
        dst = jnp.concatenate([_d, _s, _loop])
        _o = jnp.argsort(dst, stable=True)
        src = src[_o]
        dst = dst[_o]
        edge_attr_3 = jax.random.uniform(jax.random.fold_in(_gk, 13), (103125, 3), jnp.float32, 0.0, 1)
        edge_attr_64 = -8.16379e-05 + 0.999858 * jax.random.normal(jax.random.fold_in(_gk, 14), (103125, 64), jnp.float32)
        return (x, src, dst, edge_attr_3, edge_attr_64)
    x, src, dst, edge_attr_3, edge_attr_64 = _rec_inputs()

    def _L0_gnn_setup():
        import jax, jax.numpy as jnp
        import numpy as np
        N_NODES = 3125
        N_EDGES = 50000
        IN_SIZE = 64
        OUT_SIZE = 64
        N_HEADS = 2
        NEG_SLOPE = 0.2
        BN_EPS = 1e-05
        key = jax.random.key(seed)
        ks = jax.random.split(key, 8)
        atom = jax.random.normal(ks[0], (N_NODES, IN_SIZE), dtype=jnp.float32)
        bond = jax.random.normal(ks[1], (N_EDGES, IN_SIZE), dtype=jnp.float32)
        W = jax.random.normal(ks[2], (IN_SIZE, OUT_SIZE * N_HEADS), dtype=jnp.float32) * 0.1
        attn_l = jax.random.normal(ks[3], (N_HEADS, OUT_SIZE), dtype=jnp.float32) * 0.1
        attn_r = jax.random.normal(ks[4], (N_HEADS, OUT_SIZE), dtype=jnp.float32) * 0.1
        bn_gamma = jnp.ones((OUT_SIZE,), dtype=jnp.float32)
        bn_beta = jnp.zeros((OUT_SIZE,), dtype=jnp.float32)
        src = jax.random.randint(ks[5], (N_EDGES,), 0, N_NODES, dtype=jnp.int32)
        dst = jax.random.randint(ks[6], (N_EDGES,), 0, N_NODES, dtype=jnp.int32)
        return {'atom': atom, 'bond': bond, 'W': W, 'attn_l': attn_l, 'attn_r': attn_r, 'bn_gamma': bn_gamma, 'bn_beta': bn_beta, 'src': src, 'dst': dst}
    _L0_gnn_all = _L0_gnn_setup()
    _L0_gnn_in = {k: v for k, v in _L0_gnn_all.items() if k in ('W', 'attn_l', 'attn_r', 'bn_gamma', 'bn_beta')}
    del _L0_gnn_all

    def _L1_gnn_setup():
        import jax, jax.numpy as jnp
        import numpy as np
        N_NODES = 3125
        N_EDGES = 50000
        IN_FEATS = 64
        OUT_FEATS = 64
        DIM = 3
        N_KERNELS = 4
        key = jax.random.key(seed)
        ks = jax.random.split(key, 8)
        feat = jax.random.normal(ks[0], (N_NODES, IN_FEATS), dtype=jnp.float32)
        pseudo = jax.random.uniform(ks[1], (N_EDGES, DIM), dtype=jnp.float32)
        src = jax.random.randint(ks[2], (N_EDGES,), 0, N_NODES, dtype=jnp.int32)
        dst = jax.random.randint(ks[3], (N_EDGES,), 0, N_NODES, dtype=jnp.int32)
        W_fc = jax.random.normal(ks[4], (N_KERNELS * OUT_FEATS, IN_FEATS), dtype=jnp.float32) * 0.1
        mu = jax.random.normal(ks[5], (N_KERNELS, DIM), dtype=jnp.float32)
        inv_sigma = jax.random.uniform(ks[6], (N_KERNELS, DIM), dtype=jnp.float32) + 0.5
        bias = jnp.zeros((OUT_FEATS,), dtype=jnp.float32)
        return {'feat': feat, 'pseudo': pseudo, 'src': src, 'dst': dst, 'W_fc': W_fc, 'mu': mu, 'inv_sigma': inv_sigma, 'bias': bias}
    _L1_gnn_all = _L1_gnn_setup()
    _L1_gnn_in = {k: v for k, v in _L1_gnn_all.items() if k in ('W_fc', 'mu', 'inv_sigma', 'bias')}
    del _L1_gnn_all

    def _L2_gnn_setup():
        import jax, jax.numpy as jnp
        import numpy as np
        N = 50000
        D = 64
        E = 25000
        key = jax.random.key(seed)
        k1, k2, k3, k4 = jax.random.split(key, 4)
        f = jax.random.normal(k1, (N, D), dtype=jnp.float32)
        norm = jax.random.uniform(k2, (N, 1), dtype=jnp.float32)
        src = jax.random.randint(k3, (E,), 0, N, dtype=jnp.int64)
        dst = jax.random.randint(k4, (E,), 0, N, dtype=jnp.int64)
        return {'f': f, 'norm': norm, 'src': src, 'dst': dst, 'num_nodes': N}
    _L2_gnn_all = _L2_gnn_setup()
    _L2_gnn_in = {k: v for k, v in _L2_gnn_all.items() if k in ()}
    del _L2_gnn_all

    def _L3_gnn_setup():
        import jax, jax.numpy as jnp
        import numpy as np
        N_NODES = 3125
        N_EDGES = 25000
        D = 64
        NEG_SLOPE = 0.2
        key = jax.random.key(seed)
        k1, k2, k3, k4, k5 = jax.random.split(key, 5)
        x = jax.random.normal(k1, (N_NODES, D), dtype=jnp.float32)
        edge_index = jax.random.randint(k2, (2, N_EDGES), 0, N_NODES, dtype=jnp.int64)
        W = jax.random.normal(k3, (D, D), dtype=jnp.float32) * (1.0 / np.sqrt(D))
        att_src = jax.random.normal(k4, (D,), dtype=jnp.float32) * 0.1
        att_dst = jax.random.normal(k5, (D,), dtype=jnp.float32) * 0.1
        bias = jnp.zeros((D,), dtype=jnp.float32)
        return {'x': x, 'edge_index': edge_index, 'W': W, 'att_src': att_src, 'att_dst': att_dst, 'bias': bias}
    _L3_gnn_all = _L3_gnn_setup()
    _L3_gnn_in = {k: v for k, v in _L3_gnn_all.items() if k in ('W', 'att_src', 'att_dst', 'bias')}
    del _L3_gnn_all
    return {'x': x, 'src': src, 'dst': dst, 'edge_attr_3': edge_attr_3, 'edge_attr_64': edge_attr_64, 'L0_gnn_W': _L0_gnn_in['W'], 'L0_gnn_attn_l': _L0_gnn_in['attn_l'], 'L0_gnn_attn_r': _L0_gnn_in['attn_r'], 'L0_gnn_bn_gamma': _L0_gnn_in['bn_gamma'], 'L0_gnn_bn_beta': _L0_gnn_in['bn_beta'], 'L1_gnn_W_fc': _L1_gnn_in['W_fc'], 'L1_gnn_mu': _L1_gnn_in['mu'], 'L1_gnn_inv_sigma': _L1_gnn_in['inv_sigma'], 'L1_gnn_bias': _L1_gnn_in['bias'], 'L3_gnn_W': _L3_gnn_in['W'], 'L3_gnn_att_src': _L3_gnn_in['att_src'], 'L3_gnn_att_dst': _L3_gnn_in['att_dst'], 'L3_gnn_bias': _L3_gnn_in['bias']}

def reference(x, src, dst, edge_attr_3, edge_attr_64, L0_gnn_W, L0_gnn_attn_l, L0_gnn_attn_r, L0_gnn_bn_gamma, L0_gnn_bn_beta, L1_gnn_W_fc, L1_gnn_mu, L1_gnn_inv_sigma, L1_gnn_bias, L3_gnn_W, L3_gnn_att_src, L3_gnn_att_dst, L3_gnn_bias):
    import jax
    import jax.numpy as jnp

    def _L0_gnn_ref(atom, bond, W, attn_l, attn_r, bn_gamma, bn_beta, src, dst):
        import jax, jax.numpy as jnp
        import numpy as np
        N_NODES = 3125
        N_EDGES = 50000
        IN_SIZE = 64
        OUT_SIZE = 64
        N_HEADS = 2
        NEG_SLOPE = 0.2
        BN_EPS = 1e-05
        N = atom.shape[0]
        H, D = attn_l.shape
        h_edge = ((atom[src] + bond) @ W).reshape(-1, H, D)
        h_node = (atom @ W).reshape(-1, H, D)
        el = jnp.einsum('ehd,hd->eh', h_edge, attn_l)
        er = jnp.einsum('nhd,hd->nh', h_node, attn_r)
        s = el + er[dst]
        s = jnp.where(s > 0, s, NEG_SLOPE * s)
        smax = jax.ops.segment_max(s, dst, num_segments=N)
        ex = jnp.exp(s - smax[dst])
        denom = jax.ops.segment_sum(ex, dst, num_segments=N)
        alpha = ex / denom[dst]
        ft = jax.ops.segment_sum(h_edge * alpha[..., None], dst, num_segments=N)
        h = ft.mean(axis=1)
        mu = h.mean(axis=0)
        var = h.var(axis=0)
        h = (h - mu) / jnp.sqrt(var + BN_EPS) * bn_gamma + bn_beta
        h = jax.nn.relu(h)
        return h

    def _L1_gnn_ref(feat, pseudo, src, dst, W_fc, mu, inv_sigma, bias):
        import jax, jax.numpy as jnp
        import numpy as np
        N_NODES = 3125
        N_EDGES = 50000
        IN_FEATS = 64
        OUT_FEATS = 64
        DIM = 3
        N_KERNELS = 4
        N = feat.shape[0]
        K, out = (N_KERNELS, OUT_FEATS)
        h = (feat @ W_fc.T).reshape(N, K, out)
        diff = pseudo[:, None, :] - mu[None, :, :]
        g = jnp.exp(jnp.sum(-0.5 * diff * diff * inv_sigma[None] ** 2, axis=-1))
        rst = jnp.zeros((N, out), dtype=feat.dtype)
        for k in range(K):
            msg = h[:, k, :][src] * g[:, k:k + 1]
            rst = rst + jax.ops.segment_sum(msg, dst, num_segments=N)
        rst = rst + feat + bias
        return rst

    def _L2_gnn_ref(f, norm, src, dst, num_nodes):
        import jax, jax.numpy as jnp
        import numpy as np
        N = 50000
        D = 64
        E = 25000
        w = norm[src] * norm[dst]
        h = f[src] * w
        s = jax.ops.segment_max(h, dst, num_segments=num_nodes)
        has_in = jax.ops.segment_sum(jnp.ones_like(dst, dtype=jnp.float32), dst, num_segments=num_nodes) > 0
        return jnp.where(has_in[:, None], s, 0.0)

    def _L3_gnn_ref(x, edge_index, W, att_src, att_dst, bias):
        import jax, jax.numpy as jnp
        import numpy as np
        N_NODES = 3125
        N_EDGES = 25000
        D = 64
        NEG_SLOPE = 0.2
        n = x.shape[0]
        loops = jnp.arange(n, dtype=edge_index.dtype)
        src = jnp.concatenate([edge_index[0], loops])
        dst = jnp.concatenate([edge_index[1], loops])
        h = x @ W
        a_src = h @ att_src
        a_dst = h @ att_dst
        e = jax.nn.leaky_relu(a_src[src] + a_dst[dst], NEG_SLOPE)
        m = jax.lax.stop_gradient(jax.ops.segment_max(e, dst, num_segments=n))
        ex = jnp.exp(e - m[dst])
        denom = jax.ops.segment_sum(ex, dst, num_segments=n)
        alpha = ex / (denom[dst] + 1e-16)
        out = jax.ops.segment_sum(alpha[:, None] * h[src], dst, num_segments=n)
        return out + bias
    edge_index = jnp.stack([src, dst])
    deg = jnp.maximum(jax.ops.segment_sum(jnp.ones(dst.shape, jnp.float32), dst, num_segments=3125), 1.0)
    deg_isqrt = deg ** (-0.5)
    x = _layernorm(x + _L0_gnn_ref(x, edge_attr_64, L0_gnn_W, L0_gnn_attn_l, L0_gnn_attn_r, L0_gnn_bn_gamma, L0_gnn_bn_beta, src, dst), axis=-1)
    x = _layernorm(x + _L1_gnn_ref(x, edge_attr_3, src, dst, L1_gnn_W_fc, L1_gnn_mu, L1_gnn_inv_sigma, L1_gnn_bias), axis=-1)
    x = _layernorm(x + _L2_gnn_ref(x, deg_isqrt[:, None], src, dst, 3125), axis=-1)
    x = _layernorm(x + _L3_gnn_ref(x, edge_index, L3_gnn_W, L3_gnn_att_src, L3_gnn_att_dst, L3_gnn_bias), axis=-1)
    return x

_drawn_inputs = setup_inputs


def setup_inputs(seed=0):
    import zlib

    import numpy as np

    out = dict(_drawn_inputs(seed))
    spreads = {'L0_gnn_bn_gamma': (1.0, 0.2),
     'L0_gnn_bn_beta': (0.0, 0.1),
     'L1_gnn_bias': (0.0, 0.337),
     'L3_gnn_bias': (0.0, 0.1)}
    factors = {}
    for name, (base, spread) in spreads.items():
        noise = np.random.default_rng([zlib.crc32(name.encode()), seed]).standard_normal(out[name].shape)
        drawn = base * np.exp(spread * noise) if base else spread * noise
        out[name] = jnp.asarray(drawn.astype(out[name].dtype))
    for name, factor in factors.items():
        out[name] = (out[name] * factor).astype(out[name].dtype)
    return out
```

```python
from contextlib import ExitStack

import concourse.bass as bass
from concourse import mybir

F32 = mybir.dt.float32
I32 = mybir.dt.int32
ALU = mybir.AluOpType
ACT = mybir.ActivationFunctionType
AX = mybir.AxisListType.X

N = 3125
E = 103125
D = 64
P = 128
J = 810
EP = P * J
NP = 125
NK = N // NP
G = 18
U = 5
NG = J // G
IT = NG // U
BIG = 1e37
EPS = 1e-5
SLOPE = 0.2
ROWW = [132, 256, 64, 66]
UNITS = [2, 4, 1, 1]
CH = [65, 64, 64, 65]
DRING = 5


class Step:

    def __init__(self, eng, sem):
        self.eng, self.sem, self.total, self.local, self.it, self.per = eng, sem, 0, 0, None, 0

    def link(self, ins):
        ins.then_inc(self.sem, 1)
        self.local += 1
        if self.it is None:
            self.total, self.local = self.total + 1, 0
            self.eng.wait_ge(self.sem, self.total)
        else:
            self.eng.wait_ge(self.sem, self.it * self.per + (self.total + self.local))

    def enter(self, it, per):
        self.it, self.per, self.local = it, per, 0

    def leave(self, iterations):
        assert self.local == self.per, (self.local, self.per)
        self.total += iterations * self.per
        self.it, self.local = None, 0


def gnn(nc, x, src, dst, attr3, attr64, w0, attn_l, attn_r, gamma, beta,
        w1, mu, inv_sigma, bias1, w3, att_src, att_dst, bias3, out):
    with ExitStack() as ctx:
        def sb(name, shape, dt=F32):
            return ctx.enter_context(nc.sbuf_tensor(name, shape, dt))

        def dram(name, shape, dt=F32):
            return nc.dram_tensor(name, shape, dt, kind="Internal").ap()

        def sem(name):
            return ctx.enter_context(nc.semaphore(name))

        dst_rows = dram("dst_rows", [P, J])
        start_tab = dram("start_tab", [N + 1, 1], I32)
        er_tab = dram("er_tab", [N, 2])
        er_edges = dram("er_edges", [EP + N, 2])
        x_tab = [x] + [dram(f"x_tab{l}", [N, D]) for l in (1, 2, 3)]
        run_tab = [dram(f"run_tab{l}", [EP, ROWW[l]]) for l in range(4)]

        ring_big = sb("ring_big", [P, U * G * 65 + 2 * G * D])
        ring = ring_big[:, 0:U * G * 65].rearrange("p (s j f) -> p s j f", s=U, j=G)
        prod = ring_big[:, U * G * 65:].rearrange("p (h j f) -> p h j f", h=2, j=G)
        corr = ring_big[0:NP, 0:NK * 256]
        wz = sb("wz", [P, 4, 65 * (G + 1)])
        pseudo = wz[:, :, :].rearrange("p a c -> p (a c)")[:, 0:3 * J].rearrange("p (j d) -> p j d", d=3)
        before_loops = ring_big[:, U * G * 65:]
        dst_f = before_loops[:, 0:J + 1]
        attb = before_loops[:, J + 1:J + 1 + 6 * P].rearrange("p (v c) -> p v c", v=6)
        dec_run = sb("dec_run", [P, 4, 65 * (G + 1)])
        dec = dec_run[:, 0:2, :]
        run = dec_run[:, 2:4, :]
        squares = dec_run[:, :, :].rearrange("p a c -> p (a c)")[:, 0:6 * J].rearrange(
            "p (b d j) -> p b d j", b=2, d=3)
        RROW = 2 * G * 132
        rows_big = sb("rows_big", [P, max(RROW + U * G * D, 2 * G * 256)])
        bond = rows_big[:, RROW:RROW + U * G * D].rearrange("p (s c) -> p s c", s=U)
        drows = rows_big[0:NP, 0:DRING * J].rearrange("p (s c) -> p s c", s=DRING)
        ends = rows_big[0:NP, 0:NK * 256]
        er = sb("er", [P, 2, J])
        mx = sb("mx", [P, 2 * (J + 1)])
        mxv = mx[:, :].rearrange("p (h j) -> p h j", h=2)
        er_raw = mx[:, 0:2 * J].rearrange("p (j h) -> p j h", h=2)
        neg = sb("neg", [P, J])
        keep = sb("keep", [P, J])
        gauss = sb("gauss", [P, 4, J])
        dot = sb("dot", [P, 2, G])
        logit = sb("logit", [P, 2, G])
        wexp_in = sb("wexp_in", [P, U, 2, 2, G])
        wexp = sb("wexp", [P, U, 2, 2, G])
        idx = sb("idx", [P, U, G], I32)
        dst_i = sb("dst_i", [P, J + 1], I32)
        nxt_i = sb("nxt_i", [P, 1], I32)
        nxt_f = sb("nxt_f", [P, 1])
        flags = sb("flags", [P, 8])
        sel = sb("sel", [P, N])
        ident = sb("ident", [P, P])
        ones = sb("ones", [P, P])
        diag = sb("diag", [P, 2, P])
        last_row = sb("last_row", [P, P])
        pass_b = sb("pass_b", [P, P])
        negpass_b = sb("negpass_b", [P, P])
        xs = sb("xs", [NP, NK, D])
        xw = sb("xw", [NP, NK, D])
        xt = sb("xt", [NP, NK, D])
        nid = sb("nid", [NP, NK])
        cross = sb("cross", [NP, NK])
        below = sb("below", [NP, NK])
        start_i = sb("start_i", [NP, NK], I32)
        next_i = sb("next_i", [NP, NK], I32)
        bound_i = sb("bound_i", [NP, NK], I32)
        startf = sb("startf", [NP, NK])
        nextf = sb("nextf", [NP, NK])
        has = sb("has", [NP, NK])
        norm = sb("norm", [NP, NK])
        end_i = sb("end_i", [NP, NK], I32)
        put_i = sb("put_i", [NP, NK], I32)
        negc = sb("negc", [NP, NK])
        er_n = sb("er_n", [NP, NK, 2])
        er_first = sb("er_first", [P, 2])
        total_i = sb("total_i", [1, 1], I32)
        w03 = sb("w03", [D, 192])
        wst0 = sb("wst0", [P, D])
        wst0h = sb("wst0h", [P, D])
        w1a = sb("w1a", [D, 4 * D])
        wst1 = sb("wst1", [P, 2, D])
        w0t = sb("w0t", [P, D])
        w3t = sb("w3t", [D, D])
        att0 = sb("att0", [P, 2])
        att3 = sb("att3", [D, 2])
        vecs = sb("vecs", [P, 6, D])
        feat_b = sb("feat_b", [NP, 4, D])
        mu_b = sb("mu_b", [P, 12])
        inv_b = sb("inv_b", [P, 12])
        mi_b = sb("mi_b", [P, 12])
        carry_t = sb("carry_t", [P, 4, P + 1])
        mc = sb("mc", [P, 2, P + 1])
        cexp_in = sb("cexp_in", [P, 2, 2, P])
        cexp = sb("cexp", [P, 2, 2, P])
        tail_s = sb("tail_s", [P, 2, P])
        carry = sb("carry", [P, 256])
        proj_t = sb("proj_t", [P, 2, P])
        st = sb("st", [NP, 12, NK])
        bn = sb("bn", [NP, 4, D])
        nexp_in = sb("nexp_in", [NP, 3, 2, NK])
        nexp = sb("nexp", [NP, 3, 2, NK])
        loop_logit = sb("loop_logit", [NP, NK])

        pt = [ctx.enter_context(nc.psum_tensor(f"pt{i}", [P, 512], F32)) for i in range(2)]
        pa = [ctx.enter_context(nc.psum_tensor(f"pa{i}", [P, 512], F32)) for i in range(4)]
        pb = [ctx.enter_context(nc.psum_tensor(f"pb{i}", [P, 512], F32)) for i in range(2)]

        dve_step = sem("dve_step")
        preset, dst_loaded, w_loaded, x_loaded, attr3_loaded = (sem(n) for n in (
            "preset", "dst_loaded", "w_loaded", "x_loaded", "attr3_loaded"))
        iota_done, total_ready, ident_ready = sem("iota_done"), sem("total_ready"), sem("ident_ready")
        dstf_ready, dst_stored, cross_ready = sem("dstf_ready"), sem("dst_stored"), sem("cross_ready")
        drow = [sem(f"drow{i}") for i in range(DRING)]
        drow_used, starts_ready, starts_stored, next_loaded, put_ready = (sem(n) for n in (
            "drow_used", "starts_ready", "starts_stored", "next_loaded", "put_ready"))
        zero_ready, zeroed, diag_ready, rows_bcast = (sem(n) for n in (
            "zero_ready", "zeroed", "diag_ready", "rows_bcast"))
        wt_psum, wt_copied, att_ready, vec_psum, vec_ready = (sem(n) for n in (
            "wt_psum", "wt_copied", "att_ready", "vec_psum", "vec_ready"))
        gauss_in, gauss_sq, gauss_sum, gauss_ready = (sem(n) for n in (
            "gauss_in", "gauss_sq", "gauss_sum", "gauss_ready"))
        ern_ready, ern_stored, er_first_in, er_put, er_loaded = (sem(n) for n in (
            "ern_ready", "ern_stored", "er_first_in", "er_put", "er_loaded"))
        x_ready, x_stored, sel_ready, negc_psum = (sem(n) for n in (
            "x_ready", "x_stored", "sel_ready", "negc_psum"))
        idx_loaded = [[sem(f"idx_loaded{l}_{s}") for s in range(U)] for l in range(4)]
        gathered = [[sem(f"gathered{l}_{s}") for s in range(U)] for l in range(4)]
        bond_loaded = [sem(f"bond_loaded{s}") for s in range(U)]
        slot_free = [sem(f"slot_free{l}") for l in range(4)]
        logits_ready = {l: sem(f"logits_ready{l}") for l in (0, 3)}
        w_ready = {l: sem(f"w_ready{l}") for l in (0, 3)}
        dec_ready = [sem(f"dec_ready{l}") for l in range(4)]
        scanned = [sem(f"scanned{l}") for l in range(4)]
        rows_copied = [sem(f"rows_copied{l}") for l in range(4)]
        row_free = [[sem(f"row_free{l}_{r}") for r in range(2)] for l in range(4)]
        tail_ready, tails_t, exp_in, exp_ready, carry_scanned, carry_back, carry_ready = (sem(n) for n in (
            "tail_ready", "tails_t", "exp_in", "exp_ready", "carry_scanned", "carry_back", "carry_ready"))
        corr_psum, corr_copied, ends_in = sem("corr_psum"), sem("corr_copied"), sem("ends_in")
        agg_ready, agg_t, agg_tc, proj_done, stat_ready, stat_sum, sqrt_in, sqrt_out = (sem(n) for n in (
            "agg_ready", "agg_t", "agg_tc", "proj_done", "stat_ready", "stat_sum", "sqrt_in", "sqrt_out"))
        out_stored = sem("out_stored")

        assert NG == U * IT and J == G * NG

        def wz3(k, ch=65):
            return wz[:, k, :].rearrange("p (f j) -> p f j", f=65)[:, 0:ch, :]

        def dec3(k, ch=65):
            return dec[:, k, :].rearrange("p (f j) -> p f j", f=65)[:, 0:ch, :]

        def run3(k, ch=65):
            return run[:, k, :].rearrange("p (f j) -> p f j", f=65)[:, 0:ch, :]

        def row_slot(l, r):
            w = ROWW[l]
            return rows_big[:, r * G * w:(r + 1) * G * w].rearrange("p (j c) -> p j c", c=w)

        def run_store(l, g):
            return run_tab[l].rearrange("(p j) c -> p j c", j=J)[:, bass.ds(g * G, G), :]

        def bank_blocks(l):
            per = min(512 // ROWW[l], NK)
            return [(b, min(b + per, NK)) for b in range(0, NK, per)]

        ROUNDS = [sum(len(bank_blocks(m)) for m in range(l)) for l in range(5)]
        NPROJ = [1, 2, 0, 1]
        PIECE0 = [0, NK, 3 * NK, 3 * NK, 4 * NK]
        SOFT = (0, 3)
        COPIES = [2, 1, 1, 2]
        CREDIT = [4, 2, 1, 2]
        ROW_USES = [(0, 3), (0, 2), (1, 3), (1, 2), (2, 3)]

        def agg_of(l):
            if l == 1:
                return ends[:, :].rearrange("p (k c) -> p k c", k=NK)
            w = 128 if l == 0 else 64
            return wz[0:NP, :, :].rearrange("p a c -> p (a c)")[:, 0:NK * w].rearrange("p (k c) -> p k c", k=NK)

        block = ctx.enter_context(nc.Block())

        @block.sync
        def _(sp):
            dst2 = dst.rearrange("(p j) -> p j", j=J)
            sp.dma_start(dst_i[:, 1:J + 1], dst2).then_inc(dst_loaded, 16)
            sp.wait_ge(preset, 1)
            sp.dma_start(dst_i[1:P, 0:1], dst2[0:P - 1, J - 1:J],
                         allow_slow_non_contiguous=True).then_inc(dst_loaded, 16)
            sp.dma_start(nxt_i[0:P - 1, :], dst2[1:P, 0:1], allow_slow_non_contiguous=True).then_inc(dst_loaded, 16)
            sp.dma_start(xs[:, :, :], x.rearrange("(p k) f -> p k f", k=NK)).then_inc(x_loaded, 16)
            for t, a in ((w03[:, 0:128], w0), (w03[:, 128:192], w3),
                         (att0[:, 0:1], attn_l.rearrange("h (d a) -> (h d) a", a=1)),
                         (att0[:, 1:2], attn_r.rearrange("h (d a) -> (h d) a", a=1)),
                         (att3[:, 0:1], att_src.rearrange("(d a) -> d a", a=1)),
                         (att3[:, 1:2], att_dst.rearrange("(d a) -> d a", a=1)),
                         (wst0[0:D, :], w0[:, 0:D]), (wst0[D:P, :], w0[:, D:2 * D]),
                         (w1a[:, :].rearrange("o (k i) -> o k i", k=4), w1.rearrange("(k o) i -> o k i", k=4)),
                         (mu_b[:, :], mu.rearrange("k d -> (k d)").partition_broadcast(P)),
                         (inv_b[:, :], inv_sigma.rearrange("k d -> (k d)").partition_broadcast(P)),
                         (feat_b[:, 0, :], gamma.partition_broadcast(NP)),
                         (feat_b[:, 1, :], beta.partition_broadcast(NP)),
                         (feat_b[:, 2, :], bias1.partition_broadcast(NP)),
                         (feat_b[:, 3, :], bias3.partition_broadcast(NP))):
                sp.dma_start(t, a).then_inc(w_loaded, 16)
            sp.wait_ge(dstf_ready, 1)
            sp.dma_start(dst_rows, dst_f[:, 1:J + 1]).then_inc(dst_stored, 16)
            sp.wait_ge(zero_ready, 1)
            sp.dma_start(er_edges[0:EP, :].rearrange("(p j) h -> p (j h)", j=J),
                         mx[:, 0:2 * J]).then_inc(zeroed, 16)
            sp.wait_ge(cross_ready, 1)
            sp.dma_start(pseudo[:, :, :], attr3.rearrange("(p j) d -> p j d", j=J)).then_inc(attr3_loaded, 16)
            sp.wait_ge(total_ready, 1)
            sp.dma_start(start_tab[N:N + 1, :], total_i[:, :]).then_inc(starts_stored, 16)

            def load_indices(l, g, s):
                sp.wait_ge(slot_free[l], g + 1)
                sp.dma_start(idx[:, s, :], src.rearrange("(p j) -> p j", j=J)[:, bass.ds(g * G, G)]
                             ).then_inc(idx_loaded[l][s], 16)
                if l == 0:
                    sp.dma_start(bond[:, s, :],
                                 attr64.rearrange("(p j) f -> p (j f)", j=J)[:, bass.ds(g * (G * D), G * D)]
                                 ).then_inc(bond_loaded[s], 16)

            def store_er():
                sp.dma_start(er_tab.rearrange("(p k) h -> p k h", k=NK), er_n[:, :, :]).then_inc(ern_stored, 16)

            def load_er(n):
                sp.wait_ge(er_put, 16 * NK * n)
                sp.dma_start(er_raw, er_edges[0:EP, :].rearrange("(p j) h -> p j h", j=J)).then_inc(er_loaded, 16)

            for s in range(U):
                load_indices(0, s, s)
            sp.wait_ge(ern_ready, 1)
            store_er()
            sp.wait_ge(starts_ready, 1)
            sp.dma_start(start_tab[0:N, :].rearrange("(p k) a -> p (k a)", k=NK), start_i[:, :]
                         ).then_inc(starts_stored, 16)
            sp.wait_ge(starts_stored, 32)
            sp.dma_start(next_i[:, :], start_tab[1:N + 1, :].rearrange("(p k) a -> p (k a)", k=NK)
                         ).then_inc(next_loaded, 16)
            load_er(1)
            for l in range(4):
                if l == 3:
                    for s in range(U):
                        load_indices(l, s, s)
                    sp.wait_ge(ern_ready, 2)
                    store_er()
                    load_er(2)
                with nc.sync.Fori(1 if l in SOFT else 0, IT) as it:
                    for s in range(U):
                        load_indices(l, it * U + s, s)
                if l < 3:
                    sp.wait_ge(x_ready, l + 1)
                    sp.dma_start(x_tab[l + 1].rearrange("(p k) f -> p k f", k=NK),
                                 (xw if l == 1 else xs)[:, :, :]).then_inc(x_stored, 16)
            sp.wait_ge(x_ready, 4)
            sp.dma_start(out.rearrange("(p k) f -> p k f", k=NK), xs[:, :, :]).then_inc(out_stored, 16)
            sp.wait_ge(out_stored, 16)
            sp.wait_ge(x_stored, 48)
            sp.wait_ge(dst_stored, 16)
            sp.wait_ge(zeroed, 16)
            sp.wait_ge(ern_stored, 32)
            sp.wait_ge(starts_stored, 32)
            sp.wait_ge(er_put, 32 * NK)
            for l in range(4):
                sp.wait_ge(row_free[l][0], 16 * (3 * IT + 1))
                sp.wait_ge(row_free[l][1], 16 * (2 * IT + 1))

        @block.gpsimd
        def _(pool):
            nc.gpsimd.iota(nid[:, :], [[1, NK]], base=0, channel_multiplier=NK,
                           allow_small_or_imprecise_dtypes=True).then_inc(iota_done, 1)
            nc.gpsimd.iota(ident[:, :], [[1, P]], base=0, channel_multiplier=-1,
                           allow_small_or_imprecise_dtypes=True).then_inc(iota_done, 1)
            nc.gpsimd.iota(total_i[:, :], [[1, 1]], base=E, channel_multiplier=0).then_inc(total_ready, 1)
            nc.gpsimd.iota(sel[:, :], [[1, N]], base=0, channel_multiplier=0,
                           allow_small_or_imprecise_dtypes=True).then_inc(iota_done, 1)

            pool.wait_ge(dst_stored, 16)
            pool.wait_ge(cross_ready, 1)
            for k in range(NK):
                if k >= DRING:
                    pool.wait_ge(drow_used, k - DRING + 1)
                nc.gpsimd.indirect_dma_start(
                    drows[:, k % DRING, :], None, dst_rows,
                    bass.IndirectOffsetOnAxis(ap=bound_i[:, k:k + 1], axis=0)).then_inc(drow[k % DRING], 16)

            def gather_group(l, loads, s):
                pool.wait_ge(idx_loaded[l][s], loads)
                nc.gpsimd.nop(nofuse=True)
                for j in range(G):
                    nc.gpsimd.indirect_dma_start(
                        ring[:, s, j, 0:D], None, x_tab[l],
                        bass.IndirectOffsetOnAxis(ap=idx[:, s, j:j + 1], axis=0)).then_inc(gathered[l][s], 16)

            def scatter_er(n):
                pool.wait_ge(ern_stored, 16 * n)
                if n == 1:
                    pool.wait_ge(put_ready, 1)
                    pool.wait_ge(zeroed, 16)
                for k in range(NK):
                    nc.gpsimd.indirect_dma_start(
                        er_edges, bass.IndirectOffsetOnAxis(ap=put_i[:, k:k + 1], axis=0),
                        er_n[:, k, :], None).then_inc(er_put, 16)
                nc.gpsimd.indirect_dma_start(
                    er_first[:, :], None, er_tab,
                    bass.IndirectOffsetOnAxis(ap=dst_i[:, 1:2], axis=0)).then_inc(er_first_in, 16)

            for l in range(4):
                if l > 0:
                    pool.wait_ge(x_stored, 16 * l)
                if l in SOFT:
                    gather_group(l, 16, 0)
                    scatter_er(1 if l == 0 else 2)
                    for s in range(1, U):
                        gather_group(l, 16, s)
                with nc.gpsimd.Fori(1 if l in SOFT else 0, IT) as it:
                    for s in range(U):
                        gather_group(l, it * 16 + 16, s)
                pool.wait_ge(row_free[l][0], 16 * (3 * IT + 1))
                pool.wait_ge(row_free[l][1], 16 * (2 * IT + 1))
                for k in range(NK):
                    nc.gpsimd.indirect_dma_start(
                        ends[:, k * ROWW[l]:(k + 1) * ROWW[l]], None, run_tab[l],
                        bass.IndirectOffsetOnAxis(ap=end_i[:, k:k + 1], axis=0)).then_inc(ends_in, 16)

        @block.scalar
        def _(act):
            act.wait_ge(w_loaded, 16 * 15)
            nc.scalar.mul(wst0h[:, :], wst0[:, :], 0.5).then_inc(wt_copied, 1)
            act.wait_ge(wt_psum, 1)
            nc.scalar.copy(w0t[:, :], pb[0][:, 0:D]).then_inc(wt_copied, 1)
            nc.scalar.copy(w3t[:, :], pb[0][0:D, D:2 * D]).then_inc(wt_copied, 1)
            nc.scalar.copy(wst1[:, :, :], pb[0][:, 2 * D:4 * D].rearrange("p (a o) -> p a o", a=2)
                           ).then_inc(wt_copied, 1)
            act.wait_ge(vec_psum, 1)
            nc.scalar.copy(vecs[:, :, :], pb[1][:, 0:6 * D].rearrange("p (v f) -> p v f", v=6)).then_inc(vec_ready, 1)

            act.wait_ge(gauss_in, 1)
            act.wait_ge(attr3_loaded, 16)
            for k in range(4):
                if k >= 2:
                    act.wait_ge(gauss_sum, k - 1)
                for d in range(3):
                    nc.scalar.activation(squares[:, k % 2, d, :], pseudo[:, :, d], ACT.Square,
                                         bias=mi_b[:, 3 * k + d:3 * k + d + 1],
                                         scale=inv_b[:, 3 * k + d:3 * k + d + 1]).then_inc(gauss_sq, 1)
            act.wait_ge(gauss_sum, 4)
            nc.scalar.activation(gauss[:, :, :], gauss[:, :, :], ACT.Exp, scale=-0.5).then_inc(gauss_ready, 1)

            def decays(l, g, s):
                act.wait_ge(scanned[l], g * UNITS[l] + 1)
                if l in SOFT:
                    for h in range(UNITS[l]):
                        nc.scalar.copy(dec3(h)[:, :, 1:G + 1],
                                       wexp[:, s, 1, h:h + 1, :].broadcast_to([P, 65, G])).then_inc(dec_ready[l], 1)
                else:
                    flag = keep if l == 1 else neg
                    nc.scalar.copy(dec3(s % 2, D)[:, :, 1:G + 1],
                                   flag[:, bass.ds(g * G, G)].rearrange("p (a j) -> p a j", a=1)
                                   .broadcast_to([P, D, G])).then_inc(dec_ready[l], 1)

            def store_rows(l, g, it, s):
                before, per = ROW_USES[s]
                units, ch, stride = UNITS[l], CH[l], ROWW[l] // UNITS[l]
                slot = row_slot(l, s % 2)
                act.wait_ge(row_free[l][s % 2], it * (16 * per) + 16 * (before + 1))
                for k in range(units):
                    act.wait_ge(scanned[l], g * units + (k + 2))
                    nc.scalar.copy(slot[:, :, k * stride:k * stride + ch],
                                   run3(k % 2, ch)[:, :, 1:G + 1].rearrange("p f j -> p j f")
                                   ).then_inc(rows_copied[l], 1)
                    if l in SOFT:
                        nc.scalar.copy(slot[:, :, k * stride + 65:k * stride + 66],
                                       mxv[:, k, bass.ds(g * G + 1, G)].rearrange("p (j a) -> p j a", a=1)
                                       ).then_inc(rows_copied[l], 1)
                act.wait_ge(rows_copied[l], g * (units * COPIES[l]) + (units * COPIES[l] + CREDIT[l]))
                act.dma_start(run_store(l, g), slot).then_inc(row_free[l][s % 2], 16)

            rounds = exps = roots = 0

            def node_exp(t, shape_in):
                act.wait_ge(exp_in, exps + 1)
                nc.scalar.activation(t, shape_in, ACT.Exp).then_inc(exp_ready, 1)

            def node_sqrt(t):
                act.wait_ge(sqrt_in, roots + 1)
                nc.scalar.activation(t, t, ACT.Sqrt).then_inc(sqrt_out, 1)

            for l in range(4):
                units = UNITS[l]
                nc.scalar.sem_inc(row_free[l][0], 16)
                nc.scalar.sem_inc(row_free[l][1], 16)
                nc.scalar.sem_inc(rows_copied[l], CREDIT[l])
                with nc.scalar.Fori(0, IT) as it:
                    for s in range(U):
                        g = it * U + s
                        if l in SOFT:
                            act.wait_ge(logits_ready[l], g + 1)
                            nc.scalar.activation(wexp[:, s, :, 0:units, :], wexp_in[:, s, :, 0:units, :],
                                                 ACT.Exp).then_inc(w_ready[l], 1)
                            act.wait_ge(w_ready[l], g + 1)
                        decays(l, g, s)
                        if l == 2:
                            act.wait_ge(gathered[2][s], it * (16 * G) + 16 * G)
                            nc.scalar.copy(wz3(s % 2, D)[:, :, 1:G + 1],
                                           ring[:, s, :, 0:D].rearrange("p j f -> p f j")).then_inc(slot_free[2], 1)
                        store_rows(l, g, it, s)

                if l in SOFT:
                    node_exp(cexp[:, :, 0:units, :], cexp_in[:, :, 0:units, :])
                    exps += 1
                act.wait_ge(carry_back, l + 1)
                nc.scalar.copy(carry[:, 0:ROWW[l]], pb[1][:, 0:ROWW[l]]).then_inc(carry_ready, 1)
                for b0, b1 in bank_blocks(l):
                    act.wait_ge(corr_psum, rounds + 1)
                    nc.scalar.copy(corr[:, b0 * ROWW[l]:b1 * ROWW[l]],
                                   pa[rounds % 4][0:NP, 0:(b1 - b0) * ROWW[l]]).then_inc(corr_copied, 1)
                    rounds += 1
                if l in SOFT:
                    parts = 2 if l == 0 else 3
                    node_exp(nexp[:, 0:parts, 0:units, :], nexp_in[:, 0:parts, 0:units, :])
                    exps += 1
                width = 64 if l == 3 else 128
                for n in range(PIECE0[l], PIECE0[l + 1]):
                    act.wait_ge(agg_t, n + 1)
                    if n >= 2:
                        act.wait_ge(proj_done, n - 1)
                    nc.scalar.copy(proj_t[0:width, n % 2, 0:NP], pt[n % 2][0:width, 0:NP]).then_inc(agg_tc, 1)
                for t in ([norm[:, :], bn[:, 2, :]] if l == 0 else []) + [st[:, 1, :]]:
                    node_sqrt(t)
                    roots += 1

        @block.tensor
        def _(pe):
            pe.wait_ge(diag_ready, 1)
            nc.tensor.matmul(pa[0][:, 0:256], ones[:, :], diag[:, 0:2, :].rearrange("p a b -> p (a b)"),
                             start=True, stop=True).then_inc(rows_bcast, 1)
            pe.wait_ge(w_loaded, 16 * 15)
            nc.tensor.transpose(pb[0][:, 0:D], w03[:, 0:128], ident[0:D, 0:D])
            nc.tensor.transpose(pb[0][0:D, D:2 * D], w03[:, 128:192], ident[0:D, 0:D])
            for a in range(2):
                last = nc.tensor.transpose(pb[0][:, (2 + a) * D:(3 + a) * D], w1a[:, a * 128:(a + 1) * 128],
                                           ident[0:D, 0:D])
            last.then_inc(wt_psum, 1)
            pe.wait_ge(wt_copied, 4)
            pe.wait_ge(att_ready, 1)
            for v in range(4):
                nc.tensor.matmul(pb[1][:, v * D:(v + 1) * D], attb[:, v, :], w0t[:, :], start=True, stop=True)
            for v in range(4, 6):
                last = nc.tensor.matmul(pb[1][:, v * D:(v + 1) * D], attb[0:D, v, :], w3t[:, :], start=True, stop=True)
            last.then_inc(vec_psum, 1)

            rounds = stats = 0
            for l in range(4):
                units, ch, w = UNITS[l], CH[l], ROWW[l]
                stride = w // units
                pe.wait_ge(tail_ready, l + 1)
                if l in SOFT:
                    nc.tensor.matmul(pt[0][:, 0:units * P], ones[:, :],
                                     diag[:, 0:units, :].rearrange("p a b -> p (a b)"), start=True, stop=True)
                for k in range(units):
                    last = nc.tensor.transpose(pb[0][0:ch, k * P:(k + 1) * P],
                                               wz3(k, ch)[:, :, 0:1].rearrange("p f a -> p (f a)"), ident[:, :])
                last.then_inc(tails_t, 1)
                pe.wait_ge(carry_scanned, l + 1)
                for k in range(units):
                    last = nc.tensor.transpose(pb[1][:, k * stride:k * stride + ch], carry_t[0:ch, k, 0:P],
                                               ident[0:ch, 0:ch])
                    if l in SOFT:
                        last = nc.tensor.transpose(pb[1][:, k * stride + 65:k * stride + 66], mc[0:1, k, 0:P],
                                                   ident[0:1, 0:1])
                last.then_inc(carry_back, 1)
                if l == 0:
                    pe.wait_ge(sel_ready, 1)
                    for b in range(NK):
                        last = nc.tensor.matmul(pt[1][0:NP, b:b + 1], sel[:, b::NK], ones[:, 0:1],
                                                start=True, stop=True)
                    last.then_inc(negc_psum, 1)
                pe.wait_ge(carry_ready, l + 1)
                for b0, b1 in bank_blocks(l):
                    if rounds >= 4:
                        pe.wait_ge(corr_copied, rounds - 3)
                    for b in range(b0, b1):
                        last = nc.tensor.matmul(pa[rounds % 4][0:NP, (b - b0) * w:(b - b0 + 1) * w],
                                                sel[:, b::NK], carry[:, 0:w], start=True, stop=True)
                    last.then_inc(corr_psum, 1)
                    rounds += 1
                if not NPROJ[l]:
                    continue
                width = 64 if l == 3 else 128
                agg = agg_of(l)
                pe.wait_ge(agg_ready, l + 1 if l < 3 else 3)
                pe.wait_ge(corr_copied, ROUNDS[l + 1])

                def turn(n):
                    m = n - PIECE0[l]
                    b, c = m // NPROJ[l], m % NPROJ[l]
                    if n >= 2:
                        pe.wait_ge(agg_tc, n - 1)
                    nc.tensor.transpose(pt[n % 2][0:width, 0:NP], agg[:, b, c * 128:c * 128 + width],
                                        ident[0:NP, 0:NP]).then_inc(agg_t, 1)

                turn(PIECE0[l])
                for n in range(PIECE0[l], PIECE0[l + 1]):
                    if n + 1 < PIECE0[l + 1]:
                        turn(n + 1)
                    m = n - PIECE0[l]
                    b, c = m // NPROJ[l], m % NPROJ[l]
                    rhs = wst0h[:, :] if l == 0 else wst1[:, c, :] if l == 1 else w03[:, 128:192]
                    pe.wait_ge(agg_tc, n + 1)
                    nc.tensor.matmul(pa[b // 8][0:NP, (b % 8) * D:(b % 8 + 1) * D], proj_t[0:width, n % 2, 0:NP],
                                     rhs, start=(c == 0), stop=(c == NPROJ[l] - 1)).then_inc(proj_done, 1)
                if l == 0:
                    for r in range(2):
                        pe.wait_ge(stat_ready, r + 1)
                        nc.tensor.matmul(pb[0][0:NP, 0:D], ones[0:NP, 0:NP], bn[:, 0, :],
                                         start=True, stop=True).then_inc(stat_sum, 1)

        @block.vector
        def _(dve):
            v = nc.vector
            step = Step(dve, dve_step)
            link = step.link

            v.memset(dst_i[:, 0:1], -1)
            v.memset(nxt_i[:, :], -1).then_inc(preset, 1)
            v.memset(ones[:, :], 1.0)
            v.memset(carry_t[:, :, 0:1], 0.0)
            v.memset(mc[:, :, 0:1], -BIG)
            v.memset(ring[:, :, :, D:D + 1], 1.0)
            v.memset(attb[:, :, :], 0.0)
            link(v.memset(mx[:, :], 0.0))
            v.sem_inc(zero_ready, 1)
            v.sem_inc(slot_free[0], U)
            dve.wait_ge(iota_done, 2)
            link(v.tensor_scalar(ident[:, :], ident[:, :], 0.0, None, ALU.is_equal))
            dve.wait_ge(dst_loaded, 48)
            v.tensor_copy(nxt_f[:, :], nxt_i[:, :])
            link(v.tensor_copy(dst_f[:, :], dst_i[:, :]))
            v.sem_inc(dstf_ready, 1)
            first, last = dst_f[:, 1:2], dst_f[:, J:J + 1]
            CONT, SINGLE, NEXT, PASS, STOP, TAKE = range(6)

            def fl(i):
                return flags[:, i:i + 1]
            v.tensor_tensor(keep[:, :], dst_f[:, 1:J + 1], dst_f[:, 0:J], ALU.is_equal)
            v.tensor_tensor(fl(CONT), first, dst_f[:, 0:1], ALU.is_equal)
            v.tensor_tensor(fl(SINGLE), first, last, ALU.is_equal)
            link(v.tensor_tensor(fl(NEXT), nxt_f[:, :], last, ALU.is_equal))
            v.tensor_tensor(fl(PASS), fl(CONT), fl(SINGLE), ALU.mult)
            link(v.tensor_tensor(fl(STOP), fl(SINGLE), fl(NEXT), ALU.mult))
            v.tensor_scalar(neg[:, :], keep[:, :], -1.0, BIG, ALU.add, ALU.mult)
            v.tensor_scalar(diag[:, 0, :], ident[:, :], last, None, ALU.mult)
            link(v.tensor_scalar(diag[:, 1, :], ident[:, :], fl(PASS), None, ALU.mult))
            v.sem_inc(diag_ready, 1)
            link(v.tensor_scalar(fl(TAKE), fl(STOP), -1.0, 1.0, ALU.mult, ALU.add))
            link(v.tensor_tensor(fl(TAKE), fl(TAKE), fl(CONT), ALU.mult))
            dve.wait_ge(rows_bcast, 1)
            v.tensor_copy(pass_b[:, :], pa[0][:, P:2 * P])
            v.tensor_scalar(negpass_b[:, :], pa[0][:, P:2 * P], -1.0, BIG, ALU.add, ALU.mult)
            link(v.tensor_copy(last_row[:, :], pa[0][:, 0:P]))
            less = wz[0:NP, :, :].rearrange("p a c -> p (a c)")[:, 0:NK * P].rearrange("p (k b) -> p k b", k=NK)
            dve.wait_ge(iota_done, 3)
            link(v.tensor_tensor(less, last_row[0:NP, :].rearrange("p (a b) -> p a b", a=1).broadcast_to([NP, NK, P]),
                                 nid[:, :].rearrange("p (k a) -> p k a", a=1).broadcast_to([NP, NK, P]), ALU.is_lt))
            link(v.tensor_reduce(cross[:, :], less, AX, ALU.add))
            link(v.tensor_scalar(cross[:, :], cross[:, :], float(P - 1), None, ALU.min))
            link(v.tensor_copy(bound_i[:, :], cross[:, :]))
            v.sem_inc(cross_ready, 1)
            dve.wait_ge(w_loaded, 16 * 15)
            for a, (p0, p1) in ((0, (0, D)), (1, (D, P))):
                v.tensor_scalar(attb[p0:p1, a, :], ones[p0:p1, :], att0[p0:p1, 0:1], None, ALU.mult)
                v.tensor_scalar(attb[p0:p1, 2 + a, :], ones[p0:p1, :], att0[p0:p1, 1:2], None, ALU.mult)
            v.tensor_scalar(attb[0:D, 4, :], ones[0:D, :], att3[:, 0:1], None, ALU.mult)
            link(v.tensor_scalar(attb[0:D, 5, :], ones[0:D, :], att3[:, 1:2], None, ALU.mult))
            v.sem_inc(att_ready, 1)
            link(v.scalar_tensor_tensor(mi_b[:, :], mu_b[:, :], -1.0, inv_b[:, :], ALU.mult, ALU.mult))
            v.sem_inc(gauss_in, 1)
            link(v.tensor_scalar(sel[:, :], sel[:, :], first, fl(TAKE), ALU.is_equal, ALU.mult))
            v.sem_inc(sel_ready, 1)

            def node_dot(dst_ap, vec):
                link(v.tensor_tensor(xt[:, :, :], xs[:, :, :], vec.rearrange("p (a f) -> p a f", a=1)
                                     .broadcast_to([NP, NK, D]), ALU.mult))
                link(v.tensor_reduce(dst_ap, xt[:, :, :], AX, ALU.add))

            dve.wait_ge(vec_ready, 1)
            dve.wait_ge(x_loaded, 16)
            node_dot(er_n[:, :, 0], vecs[0:NP, 2, :])
            node_dot(er_n[:, :, 1], vecs[0:NP, 3, :])
            v.sem_inc(ern_ready, 1)
            for k in range(NK):
                dve.wait_ge(drow[k % DRING], 16 * (k // DRING + 1))
                v.tensor_scalar(drows[:, k % DRING, :], drows[:, k % DRING, :], nid[:, k:k + 1], None,
                                ALU.is_lt, ALU.add, accum_out=below[:, k:k + 1]).then_inc(drow_used, 1)
            dve.wait_ge(drow_used, NK)
            link(v.scalar_tensor_tensor(startf[:, :], cross[:, :], float(J), below[:, :], ALU.mult, ALU.add))
            link(v.tensor_copy(start_i[:, :], startf[:, :]))
            v.sem_inc(starts_ready, 1)
            dve.wait_ge(next_loaded, 16)
            link(v.tensor_copy(nextf[:, :], next_i[:, :]))
            deg, t0, t1 = st[:, 2, :], st[:, 3, :], st[:, 4, :]
            v.tensor_scalar(t1, nextf[:, :], -1.0, 0.0, ALU.add, ALU.max)
            link(v.tensor_tensor(deg, nextf[:, :], startf[:, :], ALU.subtract))
            v.tensor_copy(end_i[:, :], t1)
            v.tensor_scalar(norm[:, :], deg, 1.0, None, ALU.max)
            link(v.tensor_scalar(has[:, :], deg, 1.0, None, ALU.min))
            link(v.tensor_scalar(t0, nid[:, :], float(EP), None, ALU.add))
            link(v.tensor_tensor(t1, startf[:, :], t0, ALU.subtract))
            link(v.tensor_tensor(t1, t1, has[:, :], ALU.mult))
            link(v.tensor_tensor(t0, t0, t1, ALU.add))
            link(v.tensor_copy(put_i[:, :], t0))
            v.sem_inc(put_ready, 1)
            for k in range(4):
                dve.wait_ge(gauss_sq, 3 * (k + 1))
                link(v.tensor_tensor(gauss[:, k, :], squares[:, k % 2, 0, :], squares[:, k % 2, 1, :], ALU.add))
                link(v.tensor_tensor(gauss[:, k, :], gauss[:, k, :], squares[:, k % 2, 2, :], ALU.add))
                v.sem_inc(gauss_sum, 1)

            def expand_er(n, heads):
                dve.wait_ge(er_loaded, 16 * n)
                dve.wait_ge(er_first_in, 16 * n)
                for h in range(heads):
                    last_scan = v.tensor_tensor_scan(er[:, h, :], keep[:, :], er_raw[:, :, h], er_first[:, h:h + 1],
                                                     ALU.mult, ALU.add)
                link(last_scan)
                link(v.memset(mxv[:, :, 0:1], -BIG))

            def prepare(l):
                op_max = l == 2
                for k in range(4):
                    v.memset(wz3(k)[:, :, 0:1], -BIG if op_max else 0.0)
                for k in range(2):
                    ins = v.memset(dec3(k)[:, :, 0:1], -BIG if op_max else 0.0)
                link(ins)
                v.sem_inc(scanned[l], 1)

            def logits(l, g, it, s):
                heads = UNITS[l]
                vec0 = 0 if l == 0 else 4
                dve.wait_ge(gathered[l][s], it * (16 * G) + 16 * G)
                if l == 0:
                    dve.wait_ge(bond_loaded[s], it * 16 + 16)
                    link(v.tensor_tensor(ring[:, s, :, 0:D], ring[:, s, :, 0:D],
                                         bond[:, s, :].rearrange("p (j f) -> p j f", j=G), ALU.add))
                for h in range(heads):
                    ins = v.tensor_tensor(prod[:, h, :, :], ring[:, s, :, 0:D],
                                          vecs[:, vec0 + h:vec0 + h + 1, :].broadcast_to([P, G, D]), ALU.mult)
                link(ins)
                link(v.tensor_reduce(dot[:, 0:heads, :], prod[:, 0:heads, :, :], AX, ALU.add))
                link(v.tensor_tensor(dot[:, 0:heads, :], dot[:, 0:heads, :], er[:, 0:heads, bass.ds(g * G, G)], ALU.add))
                link(v.scalar_tensor_tensor(logit[:, 0:heads, :], dot[:, 0:heads, :], SLOPE, dot[:, 0:heads, :],
                                            ALU.mult, ALU.max))
                for h in range(heads):
                    ins = v.tensor_tensor_scan(mxv[:, h, bass.ds(g * G + 1, G)], neg[:, bass.ds(g * G, G)],
                                               logit[:, h, :], mxv[:, h, bass.ds(g * G, 1)], ALU.add, ALU.max)
                link(ins)
                now, before = mxv[:, 0:heads, bass.ds(g * G + 1, G)], mxv[:, 0:heads, bass.ds(g * G, G)]
                link(v.tensor_tensor(wexp_in[:, s, 1, 0:heads, :], before,
                                     neg[:, bass.ds(g * G, G)].rearrange("p (a j) -> p a j", a=1)
                                     .broadcast_to([P, heads, G]), ALU.add))
                v.tensor_tensor(wexp_in[:, s, 0, 0:heads, :], logit[:, 0:heads, :], now, ALU.subtract)
                v.tensor_tensor(wexp_in[:, s, 1, 0:heads, :], wexp_in[:, s, 1, 0:heads, :], now,
                                ALU.subtract).then_inc(logits_ready[l], 1)

            def scans(l, g, s):
                units, ch = UNITS[l], CH[l]
                if l in SOFT:
                    dve.wait_ge(w_ready[l], g + 1)
                if l != 2:
                    for k in range(units):
                        weight = wexp[:, s, 0, k:k + 1, :] if l in SOFT else gauss[:, k:k + 1, bass.ds(g * G, G)]
                        ins = v.tensor_tensor(wz3(k, ch)[:, :, 1:G + 1], ring[:, s, :, 0:ch].rearrange("p j f -> p f j"),
                                              weight.broadcast_to([P, ch, G]), ALU.mult)
                    link(ins)
                    v.sem_inc(slot_free[l], 1)
                else:
                    dve.wait_ge(slot_free[2], g + (U + 1))

                def keep_last(k):
                    to = wz3((s + 1) % U % 2 if l == 2 else k, ch)
                    dve.wait_ge(scanned[l], g * units + (k + 2))
                    return v.tensor_copy(to[:, :, 0:1], run3(k % 2, ch)[:, :, G:G + 1])

                for k in range(units):
                    if l in SOFT or k == 0:
                        dve.wait_ge(dec_ready[l], g * (units if l in SOFT else 1) + ((k if l in SOFT else 0) + 1))
                    dve.wait_ge(rows_copied[l], g * (units * COPIES[l]) + (k * COPIES[l] + 1))
                    d = dec[:, k if l in SOFT else s % 2, 0:ch * (G + 1)]
                    z = wz[:, s % 2 if l == 2 else k, 0:ch * (G + 1)]
                    ops = (ALU.add, ALU.max) if l == 2 else (ALU.mult, ALU.add)
                    v.tensor_tensor_scan(run[:, k % 2, 0:ch * (G + 1)], d, z, 0.0, *ops).then_inc(scanned[l], 1)
                    if 0 < k < units - 1:
                        link(keep_last(k - 1))
                    elif k > 0:
                        keep_last(k - 1)
                link(keep_last(units - 1))

            def loop_soft(l):
                a, f = (7, 2) if l == 0 else (6, 2)
                logits(l, 0, 0, 0)
                with nc.vector.Fori(0, IT - 1) as it:
                    step.enter(it, U * (a + f))
                    for s in range(U):
                        nxt = it + 1 if s == U - 1 else it
                        logits(l, it * U + (s + 1), nxt, (s + 1) % U)
                        scans(l, it * U + s, s)
                step.leave(IT - 1)
                for s in range(U):
                    g = (IT - 1) * U + s
                    if s < U - 1:
                        logits(l, g + 1, IT - 1, s + 1)
                    scans(l, g, s)

            def loop_plain(l):
                with nc.vector.Fori(0, IT) as it:
                    step.enter(it, U * (1 if l == 2 else 4))
                    for s in range(U):
                        if l == 1:
                            dve.wait_ge(gathered[l][s], it * (16 * G) + 16 * G)
                        scans(l, it * U + s, s)
                step.leave(IT)

            n_exp = n_root = 0

            def carries(l):
                nonlocal n_exp
                units, ch = UNITS[l], CH[l]
                if l in SOFT:
                    for h in range(units):
                        ins = v.tensor_scalar(diag[:, h, :], ident[:, :], mxv[:, h, J:J + 1], None, ALU.mult)
                    link(ins)
                v.sem_inc(tail_ready, 1)
                dve.wait_ge(tails_t, l + 1)
                tails = pb[0]
                if l in SOFT:
                    mrow = pt[0][:, 0:units * P].rearrange("p (h b) -> p h b", h=units)
                    for h in range(units):
                        ins = v.tensor_tensor_scan(mc[:, h, 1:P + 1], negpass_b[:, :], mrow[:, h, :], -BIG,
                                                   ALU.add, ALU.max)
                    link(ins)
                    v.tensor_tensor(cexp_in[:, 1, 0:units, :], mrow, mc[:, 0:units, 1:P + 1], ALU.subtract)
                    link(v.tensor_tensor(cexp_in[:, 0, 0:units, :], mc[:, 0:units, 0:P],
                                         negpass_b[:, :].rearrange("p (a b) -> p a b", a=1)
                                         .broadcast_to([P, units, P]), ALU.add))
                    v.tensor_tensor(cexp_in[:, 0, 0:units, :], cexp_in[:, 0, 0:units, :], mc[:, 0:units, 1:P + 1],
                                    ALU.subtract).then_inc(exp_in, 1)
                    n_exp += 1
                    dve.wait_ge(exp_ready, n_exp)
                    for h in range(units):
                        ins = v.tensor_tensor(tail_s[0:ch, h, :], tails[0:ch, h * P:(h + 1) * P], cexp[0:ch, 1, h, :],
                                              ALU.mult)
                    link(ins)
                    for h in range(units):
                        ins = v.tensor_tensor_scan(carry_t[0:ch, h, 1:P + 1], cexp[0:ch, 0, h, :], tail_s[0:ch, h, :],
                                                   0.0, ALU.mult, ALU.add)
                else:
                    for k in range(units):
                        ins = v.tensor_tensor_scan(
                            carry_t[0:ch, k, 1:P + 1], (negpass_b if l == 2 else pass_b)[0:ch, :],
                            tails[0:ch, k * P:(k + 1) * P], -BIG if l == 2 else 0.0,
                            *((ALU.add, ALU.max) if l == 2 else (ALU.mult, ALU.add)))
                ins.then_inc(carry_scanned, 1)

            def bk(ap, n):
                return ap.rearrange("p (k a) -> p k a", a=1).broadcast_to([NP, NK, n])

            def bf(ap):
                return ap.rearrange("p (a f) -> p a f", a=1).broadcast_to([NP, NK, D])

            def merge_soft(l):
                nonlocal n_exp
                heads = UNITS[l]
                e4 = ends[:, 0:NK * ROWW[l]].rearrange("p (k h c) -> p k h c", k=NK, h=heads)
                c4 = corr[:, 0:NK * ROWW[l]].rearrange("p (k h c) -> p k h c", k=NK, h=heads)
                agg = agg_of(l)
                for h in range(heads):
                    m_ends, m_corr, m_all = st[:, 9, :], st[:, 5 + h, :], st[:, 7 + h, :]
                    link(v.tensor_tensor(m_corr, c4[:, :, h, 65], negc[:, :], ALU.add))
                    if l == 3:
                        link(v.tensor_scalar(m_ends, has[:, :], -1.0, BIG, ALU.add, ALU.mult))
                        link(v.tensor_tensor(m_ends, m_ends, e4[:, :, h, 65], ALU.add))
                        link(v.tensor_tensor(m_all, m_ends, loop_logit[:, :], ALU.max))
                        link(v.tensor_tensor(m_all, m_all, m_corr, ALU.max))
                        v.tensor_tensor(nexp_in[:, 2, h, :], loop_logit[:, :], m_all, ALU.subtract)
                    else:
                        m_ends = e4[:, :, h, 65]
                        link(v.tensor_tensor(m_all, m_ends, m_corr, ALU.max))
                    v.tensor_tensor(nexp_in[:, 0, h, :], m_ends, m_all, ALU.subtract)
                    link(v.tensor_tensor(nexp_in[:, 1, h, :], m_corr, m_all, ALU.subtract))
                v.sem_inc(exp_in, 1)
                n_exp += 1
                dve.wait_ge(exp_ready, n_exp)
                for h in range(heads):
                    v.tensor_tensor(e4[:, :, h, 0:65], e4[:, :, h, 0:65], bk(nexp[:, 0, h, :], 65), ALU.mult)
                    link(v.tensor_tensor(c4[:, :, h, 0:65], c4[:, :, h, 0:65], bk(nexp[:, 1, h, :], 65), ALU.mult))
                for h in range(heads):
                    link(v.tensor_tensor(e4[:, :, h, 0:65], e4[:, :, h, 0:65], c4[:, :, h, 0:65], ALU.add))
                    if l == 3:
                        link(v.tensor_tensor(xt[:, :, :], xs[:, :, :], bk(nexp[:, 2, h, :], D), ALU.mult))
                        v.tensor_tensor(e4[:, :, h, 0:D], e4[:, :, h, 0:D], xt[:, :, :], ALU.add)
                        link(v.tensor_tensor(e4[:, :, h, 64], e4[:, :, h, 64], nexp[:, 2, h, :], ALU.add))
                    link(v.tensor_scalar(st[:, 9, :], e4[:, :, h, 64], 1e-16 if l == 3 else 0.0, 1e-30,
                                         ALU.add, ALU.max))
                    link(v.reciprocal(st[:, 9, :], st[:, 9, :]))
                    if l == 0:
                        link(v.tensor_tensor(st[:, 9, :], st[:, 9, :], has[:, :], ALU.mult))
                    link(v.tensor_tensor(agg[:, :, h * D:(h + 1) * D], e4[:, :, h, 0:D], bk(st[:, 9, :], D), ALU.mult))

            def root(t):
                nonlocal n_root
                v.sem_inc(sqrt_in, 1)
                n_root += 1
                dve.wait_ge(sqrt_out, n_root)
                link(v.reciprocal(t, t))

            def free_slots(l):
                if l == 3:
                    link(v.memset(ring[:, :, :, D:D + 1], 1.0))
                v.sem_inc(slot_free[l], U)

            def projected(l):
                dve.wait_ge(proj_done, PIECE0[l + 1])
                for b in range(0, NK, 8):
                    n = min(8, NK - b)
                    p = pa[b // 8][0:NP, 0:n * D].rearrange("p (k f) -> p k f", f=D)
                    if l == 0:
                        ins = v.tensor_copy(xw[:, b:b + n, :], p)
                    else:
                        ins = v.tensor_tensor(xw[:, b:b + n, :], xw[:, b:b + n, :], p, ALU.add)
                link(ins)

            def layer_norm():
                mean, var = st[:, 0, :], st[:, 1, :]
                link(v.tensor_reduce(mean, xw[:, :, :], AX, ALU.add))
                link(v.tensor_scalar(mean, mean, 1.0 / D, None, ALU.mult))
                link(v.tensor_tensor(xw[:, :, :], xw[:, :, :], bk(mean, D), ALU.subtract))
                link(v.tensor_tensor(xt[:, :, :], xw[:, :, :], xw[:, :, :], ALU.mult))
                link(v.tensor_reduce(var, xt[:, :, :], AX, ALU.add))
                link(v.tensor_scalar(var, var, 1.0 / D, EPS, ALU.mult, ALU.add))
                root(var)
                link(v.tensor_tensor(xs[:, :, :], xw[:, :, :], bk(var, D), ALU.mult))

            expand_er(1, 2)
            prepare(0)
            loop_soft(0)
            carries(0)
            dve.wait_ge(negc_psum, 1)
            link(v.tensor_scalar(negc[:, :], pt[1][0:NP, 0:NK], -1.0, BIG, ALU.add, ALU.mult))
            dve.wait_ge(corr_copied, ROUNDS[1])
            dve.wait_ge(ends_in, 16 * NK)
            merge_soft(0)
            v.sem_inc(agg_ready, 1)
            free_slots(1)
            root(norm[:, :])
            projected(0)
            by_f = "p k f -> p f k"
            link(v.tensor_reduce(bn[:, 0, :], xw[:, :, :].rearrange(by_f), AX, ALU.add))
            v.sem_inc(stat_ready, 1)
            dve.wait_ge(stat_sum, 1)
            link(v.tensor_scalar(bn[:, 1, :], pb[0][0:NP, 0:D], 1.0 / N, None, ALU.mult))
            link(v.tensor_tensor(xw[:, :, :], xw[:, :, :], bf(bn[:, 1, :]), ALU.subtract))
            link(v.tensor_tensor(xt[:, :, :], xw[:, :, :], xw[:, :, :], ALU.mult))
            link(v.tensor_reduce(bn[:, 0, :], xt[:, :, :].rearrange(by_f), AX, ALU.add))
            v.sem_inc(stat_ready, 1)
            dve.wait_ge(stat_sum, 2)
            link(v.tensor_scalar(bn[:, 2, :], pb[0][0:NP, 0:D], 1.0 / N, EPS, ALU.mult, ALU.add))
            root(bn[:, 2, :])
            link(v.tensor_tensor(bn[:, 2, :], bn[:, 2, :], feat_b[:, 0, :], ALU.mult))
            link(v.tensor_tensor(xw[:, :, :], xw[:, :, :], bf(bn[:, 2, :]), ALU.mult))
            link(v.tensor_tensor(xw[:, :, :], xw[:, :, :], bf(feat_b[:, 1, :]), ALU.add))
            link(v.scalar_tensor_tensor(xw[:, :, :], xw[:, :, :], 0.0, xs[:, :, :], ALU.max, ALU.add))
            layer_norm()
            v.sem_inc(x_ready, 1)

            prepare(1)
            dve.wait_ge(gauss_ready, 1)
            loop_plain(1)
            carries(1)
            dve.wait_ge(x_stored, 16)
            link(v.tensor_scalar(xw[:, :, :], xs[:, :, :], 2.0, None, ALU.mult))
            link(v.tensor_tensor(xw[:, :, :], xw[:, :, :], bf(feat_b[:, 2, :]), ALU.add))
            dve.wait_ge(corr_copied, ROUNDS[2])
            dve.wait_ge(ends_in, 32 * NK)
            agg1 = agg_of(1)
            corr1 = corr[:, :].rearrange("p (k c) -> p k c", k=NK)
            link(v.tensor_tensor(agg1, agg1, corr1, ALU.add))
            link(v.tensor_tensor(agg1, agg1, bk(has[:, :], 256), ALU.mult))
            v.sem_inc(agg_ready, 1)
            free_slots(2)
            projected(1)
            layer_norm()
            link(v.tensor_tensor(xw[:, :, :], xs[:, :, :], bk(norm[:, :], D), ALU.mult))
            v.sem_inc(x_ready, 1)

            prepare(2)
            loop_plain(2)
            carries(2)
            corr2 = corr[:, 0:NK * D].rearrange("p (k f) -> p k f", k=NK)
            ends2 = ends[:, 0:NK * D].rearrange("p (k f) -> p k f", k=NK)
            dve.wait_ge(corr_copied, ROUNDS[3])
            link(v.tensor_tensor(corr2, corr2, bk(negc[:, :], D), ALU.add))
            link(v.tensor_tensor(st[:, 10, :], norm[:, :], has[:, :], ALU.mult))
            dve.wait_ge(ends_in, 48 * NK)
            link(v.tensor_tensor(corr2, corr2, ends2, ALU.max))
            dve.wait_ge(x_stored, 32)
            link(v.tensor_tensor(xw[:, :, :], corr2, bk(st[:, 10, :], D), ALU.mult))
            free_slots(3)
            link(v.tensor_tensor(xw[:, :, :], xw[:, :, :], xs[:, :, :], ALU.add))
            layer_norm()
            v.sem_inc(x_ready, 1)

            node_dot(er_n[:, :, 0], vecs[0:NP, 5, :])
            v.sem_inc(ern_ready, 1)
            node_dot(st[:, 2, :], vecs[0:NP, 4, :])
            link(v.tensor_tensor(st[:, 2, :], st[:, 2, :], er_n[:, :, 0], ALU.add))
            link(v.scalar_tensor_tensor(loop_logit[:, :], st[:, 2, :], SLOPE, st[:, 2, :], ALU.mult, ALU.max))
            expand_er(2, 1)
            prepare(3)
            loop_soft(3)
            carries(3)
            dve.wait_ge(corr_copied, ROUNDS[4])
            dve.wait_ge(ends_in, 64 * NK)
            merge_soft(3)
            v.sem_inc(agg_ready, 1)
            dve.wait_ge(x_stored, 48)
            link(v.tensor_tensor(xw[:, :, :], xs[:, :, :], bf(feat_b[:, 3, :]), ALU.add))
            projected(3)
            layer_norm()
            v.sem_inc(x_ready, 1)


_INS = ["x", "src", "dst", "edge_attr_3", "edge_attr_64", "L0_gnn_W", "L0_gnn_attn_l", "L0_gnn_attn_r",
        "L0_gnn_bn_gamma", "L0_gnn_bn_beta", "L1_gnn_W_fc", "L1_gnn_mu", "L1_gnn_inv_sigma", "L1_gnn_bias",
        "L3_gnn_W", "L3_gnn_att_src", "L3_gnn_att_dst", "L3_gnn_bias"]


def kernel(**inputs):
    import numpy as _np
    import concourse.bacc as _bacc
    from concourse.bass_utils import run_bass_kernel_spmd as _run

    nc = _bacc.Bacc("TRN2", target_bir_lowering=False, num_devices=1)
    arrays, args = {}, []
    for name in _INS:
        a = _np.ascontiguousarray(inputs[name])
        if a.shape[0] == E:
            padded = _np.full((EP,) + a.shape[1:], N if name == "dst" else 0, a.dtype)
            padded[:E] = a
            a = padded
        arrays[f"in_{name}"] = a
        args.append(nc.dram_tensor(f"in_{name}", a.shape, mybir.dt.from_np(a.dtype), kind="ExternalInput").ap())
    args.append(nc.dram_tensor("out_0", (N, D), F32, kind="ExternalOutput").ap())
    gnn(nc, *args)
    return _run(nc, [arrays], core_ids=[0]).results[0]["out_0"]
```

```python
from contextlib import ExitStack

import concourse.bass as bass
from concourse import mybir

F32 = mybir.dt.float32
I32 = mybir.dt.int32
ALU = mybir.AluOpType
ACT = mybir.ActivationFunctionType
AX = mybir.AxisListType.X

N = 3125
E = 103125
D = 64
P = 128
J = 810
EP = P * J
NP = 125
NK = N // NP
G = 18
U = 5
NG = J // G
IT = NG // U
BIG = 1e37
EPS = 1e-5
SLOPE = 0.2
ROWW = [132, 256, 64, 66]
UNITS = [2, 4, 1, 1]
CORRW = [132, 64, 64, 66]
CH = [65, 64, 64, 65]
CHUNKS = [(0, 8), (8, 16), (16, 21), (21, 25)]
DRING = 5


class Step:

    def __init__(self, eng, sem):
        self.eng, self.sem, self.total, self.local, self.it, self.per = eng, sem, 0, 0, None, 0

    def link(self, ins):
        ins.then_inc(self.sem, 1)
        self.local += 1
        if self.it is None:
            self.total, self.local = self.total + 1, 0
            self.eng.wait_ge(self.sem, self.total)
        else:
            self.eng.wait_ge(self.sem, self.it * self.per + (self.total + self.local))

    def enter(self, it, per):
        self.it, self.per, self.local = it, per, 0

    def leave(self, iterations):
        assert self.local == self.per, (self.local, self.per)
        self.total += iterations * self.per
        self.it, self.local = None, 0


def gnn(nc, x, src, dst, attr3, attr64, w0, attn_l, attn_r, gamma, beta,
        w1, mu, inv_sigma, bias1, w3, att_src, att_dst, bias3, out):
    with ExitStack() as ctx:
        def sb(name, shape, dt=F32):
            return ctx.enter_context(nc.sbuf_tensor(name, shape, dt))

        def dram(name, shape, dt=F32):
            return nc.dram_tensor(name, shape, dt, kind="Internal").ap()

        def sem(name):
            return ctx.enter_context(nc.semaphore(name))

        dst_rows = dram("dst_rows", [P, J])
        start_tab = dram("start_tab", [N + 1, 1], I32)
        er_tab = dram("er_tab", [N, 2])
        er_edges = dram("er_edges", [EP + N, 2])
        x_tab = [x] + [dram(f"x_tab{l}", [N, D]) for l in (1, 2, 3)]
        run_tab = [dram(f"run_tab{l}", [EP + 1, ROWW[l]]) for l in range(4)]

        ring_big = sb("ring_big", [P, U * G * 65 + 2 * G * D])
        ring = ring_big[:, 0:U * G * 65].rearrange("p (s j f) -> p s j f", s=U, j=G)
        prod = ring_big[:, U * G * 65:].rearrange("p (h j f) -> p h j f", h=2, j=G)
        corr = ring_big[0:NP, 0:NK * 132]
        proj_t = ring_big[:, NK * 256:NK * 256 + 8 * NP].rearrange("p (b n) -> p b n", b=2)
        wz = sb("wz", [P, 4, 65 * (G + 1)])
        pseudo = wz[:, :, :].rearrange("p a c -> p (a c)")[:, 0:3 * J].rearrange("p (j d) -> p j d", d=3)
        before_loops = ring_big[:, U * G * 65:]
        dst_f = before_loops[:, 0:J + 1]
        prod_tail = ring_big[:, NK * 256 + 8 * NP:NK * 256 + 8 * NP + 4 * D]
        attb = before_loops[:, J + 1:J + 1 + 6 * P].rearrange("p (v c) -> p v c", v=6)
        dec_run = sb("dec_run", [P, 4, 65 * (G + 1)])
        dec = dec_run[:, 0:2, :]
        run = dec_run[:, 2:4, :]
        squares = dec_run[:, :, :].rearrange("p a c -> p (a c)")[:, 0:6 * J].rearrange(
            "p (b d j) -> p b d j", b=2, d=3)
        RROW = 2 * G * 132
        rows_big = sb("rows_big", [P, max(RROW + U * G * D, 2 * G * 256)])
        bond = rows_big[:, RROW:RROW + U * G * D].rearrange("p (s c) -> p s c", s=U)
        drows = rows_big[0:NP, 0:DRING * J].rearrange("p (s c) -> p s c", s=DRING)
        ends = rows_big[0:NP, 0:NK * 256]
        er = sb("er", [P, 2, J])
        mx = sb("mx", [P, 2 * (J + 1)])
        mxv = mx[:, :].rearrange("p (h j) -> p h j", h=2)
        er_raw = mx[:, 0:2 * J].rearrange("p (j h) -> p j h", h=2)
        neg = sb("neg", [P, J])
        keep = sb("keep", [P, J])
        gauss = sb("gauss", [P, 4, J])
        dot = sb("dot", [P, 2, G])
        logit = sb("logit", [P, 2, G])
        wexp_in = sb("wexp_in", [P, U, 2, 2, G])
        wexp = sb("wexp", [P, U, 2, 2, G])
        idx = sb("idx", [P, U, G], I32)
        dst_i = sb("dst_i", [P, J + 1], I32)
        nxt_i = sb("nxt_i", [P, 1], I32)
        nxt_f = sb("nxt_f", [P, 1])
        flags = sb("flags", [P, 8])
        sel = sb("sel", [P, N])
        ident = sb("ident", [P, P])
        ones = sb("ones", [P, P])
        diag = sb("diag", [P, 2, P])
        last_row = sb("last_row", [P, P])
        pass_b = sb("pass_b", [P, P])
        negpass_b = sb("negpass_b", [P, P])
        xs = sb("xs", [NP, NK, D])
        xw = sb("xw", [NP, NK, D])
        xt = sb("xt", [NP, NK, D])
        nid = sb("nid", [NP, NK])
        cross = sb("cross", [NP, NK])
        below = sb("below", [NP, NK])
        start_i = sb("start_i", [NP, NK], I32)
        next_i = sb("next_i", [NP, NK], I32)
        bound_i = sb("bound_i", [NP, NK], I32)
        startf = sb("startf", [NP, NK])
        nextf = sb("nextf", [NP, NK])
        has = sb("has", [NP, NK])
        norm = sb("norm", [NP, NK])
        end_i = sb("end_i", [NP, NK], I32)
        put_i = sb("put_i", [NP, NK], I32)
        negc = sb("negc", [NP, NK])
        nege = sb("nege", [NP, NK])
        small = sb("small", [NP, 3, 2, NK])
        er_n = sb("er_n", [NP, NK, 2])
        er_first = sb("er_first", [P, 2])
        total_i = sb("total_i", [1, 1], I32)
        w03 = sb("w03", [D, 192])
        wst0 = sb("wst0", [P, D])
        wst0h = sb("wst0h", [P, D])
        w1a = sb("w1a", [D, 4 * D])
        wst1 = sb("wst1", [P, 2, D])
        w1t = sb("w1t", [D, 4, D])
        w0t = sb("w0t", [P, D])
        w3t = sb("w3t", [D, D])
        att0 = sb("att0", [P, 2])
        att3 = sb("att3", [D, 2])
        vecs = sb("vecs", [P, 6, D])
        feat_b = sb("feat_b", [NP, 4, D])
        mu_b = sb("mu_b", [P, 12])
        inv_b = sb("inv_b", [P, 12])
        mi_b = sb("mi_b", [P, 12])
        carry_t = sb("carry_t", [P, 4, P + 1])
        mc = sb("mc", [P, 2, P + 1])
        cexp_in = sb("cexp_in", [P, 2, 2, P])
        cexp = sb("cexp", [P, 2, 2, P])
        tail_s = sb("tail_s", [P, 2, P])
        carry = sb("carry", [P, 256])
        st = sb("st", [NP, 12, NK])
        bn = sb("bn", [NP, 3, D])
        parts = prod_tail[0:NP, :].rearrange("p (c f) -> p c f", f=D)
        eps = sb("eps", [P, 1])
        zero = sb("zero", [P, 1])
        nexp_in = sb("nexp_in", [NP, 3, 2, NK])
        nexp = sb("nexp", [NP, 3, 2, NK])
        loop_logit = sb("loop_logit", [NP, NK])

        pt = [ctx.enter_context(nc.psum_tensor(f"pt{i}", [P, 512], F32)) for i in range(2)]
        pa = [ctx.enter_context(nc.psum_tensor(f"pa{i}", [P, 512], F32)) for i in range(4)]
        pb = [ctx.enter_context(nc.psum_tensor(f"pb{i}", [P, 512], F32)) for i in range(2)]

        dve_step = sem("dve_step")
        preset, dst_loaded, w_loaded, x_loaded, attr3_loaded = (sem(n) for n in (
            "preset", "dst_loaded", "w_loaded", "x_loaded", "attr3_loaded"))
        iota_done, total_ready, ident_ready = sem("iota_done"), sem("total_ready"), sem("ident_ready")
        dstf_ready, dst_stored, cross_ready = sem("dstf_ready"), sem("dst_stored"), sem("cross_ready")
        drow = [sem(f"drow{i}") for i in range(DRING)]
        drow_used, starts_ready, starts_stored, next_loaded, put_ready = (sem(n) for n in (
            "drow_used", "starts_ready", "starts_stored", "next_loaded", "put_ready"))
        zero_ready, zeroed, diag_ready, rows_bcast = (sem(n) for n in (
            "zero_ready", "zeroed", "diag_ready", "rows_bcast"))
        wt_psum, wt_copied, att_ready, vec_psum, vec_ready = (sem(n) for n in (
            "wt_psum", "wt_copied", "att_ready", "vec_psum", "vec_ready"))
        gauss_in, gauss_sq, gauss_sum, gauss_ready = (sem(n) for n in (
            "gauss_in", "gauss_sq", "gauss_sum", "gauss_ready"))
        ern_ready, ern_stored, er_first_in, er_put, er_loaded = (sem(n) for n in (
            "ern_ready", "ern_stored", "er_first_in", "er_put", "er_loaded"))
        x_ready, x_stored, sel_ready, negc_psum = (sem(n) for n in (
            "x_ready", "x_stored", "sel_ready", "negc_psum"))
        idx_loaded = [[sem(f"idx_loaded{l}_{s}") for s in range(U)] for l in range(4)]
        gathered = [[sem(f"gathered{l}_{s}") for s in range(U)] for l in range(4)]
        bond_loaded = [sem(f"bond_loaded{s}") for s in range(U)]
        slot_free = [sem(f"slot_free{l}") for l in range(4)]
        logits_ready = {l: sem(f"logits_ready{l}") for l in (0, 3)}
        w_ready = {l: sem(f"w_ready{l}") for l in (0, 3)}
        dec_ready = [sem(f"dec_ready{l}") for l in range(4)]
        scanned = [sem(f"scanned{l}") for l in range(4)]
        rows_copied = [sem(f"rows_copied{l}") for l in range(4)]
        row_free = [[sem(f"row_free{l}_{r}") for r in range(2)] for l in range(4)]
        tail_ready, tails_t, exp_in, exp_ready, carry_scanned, carry_back, carry_ready = (sem(n) for n in (
            "tail_ready", "tails_t", "exp_in", "exp_ready", "carry_scanned", "carry_back", "carry_ready"))
        corr_psum, corr_copied = sem("corr_psum"), sem("corr_copied")
        ends_in = [[sem(f"ends_in{l}_{c}") for c in range(len(CHUNKS))] for l in range(4)]
        proj_read = sem("proj_read")
        agg_ready, agg_t, agg_tc, proj_done, stat_ready, stat_sum, sqrt_in, sqrt_out = (sem(n) for n in (
            "agg_ready", "agg_t", "agg_tc", "proj_done", "stat_ready", "stat_sum", "sqrt_in", "sqrt_out"))
        out_stored = sem("out_stored")

        assert NG == U * IT and J == G * NG

        def wz3(k, ch=65):
            return wz[:, k, :].rearrange("p (f j) -> p f j", f=65)[:, 0:ch, :]

        def dec3(k, ch=65):
            return dec[:, k, :].rearrange("p (f j) -> p f j", f=65)[:, 0:ch, :]

        def run3(k, ch=65):
            return run[:, k, :].rearrange("p (f j) -> p f j", f=65)[:, 0:ch, :]

        def row_slot(l, r):
            w = ROWW[l]
            return rows_big[:, r * G * w:(r + 1) * G * w].rearrange("p (j c) -> p j c", c=w)

        def run_store(l, g):
            return run_tab[l][0:EP, :].rearrange("(p j) c -> p j c", j=J)[:, bass.ds(g * G, G), :]

        def bank_blocks(l):
            per = 512 // CORRW[l]
            return [(b, min(b + per, NK)) for b in range(0, NK, per)]

        def chunk_of(k):
            return next(c for c, (b0, b1) in enumerate(CHUNKS) if b0 <= k < b1)

        ROUNDS = [sum(len(bank_blocks(m)) for m in range(l)) for l in range(5)]
        NPROJ = [1, 2, 0, 1]
        PROJ_READS = [0, len(CHUNKS), 2 * len(CHUNKS), 2 * len(CHUNKS)]
        SOFT = (0, 3)
        BATCHES, BATCH0 = [], []
        for l in range(4):
            BATCH0.append(BATCHES[-1][-1][1] if BATCHES else 0)
            BATCHES.append([])
            n = BATCH0[-1]
            for b0, b1 in CHUNKS:
                pieces = [(b, c) for b in range(b0, b1) for c in range(NPROJ[l])]
                lots = [pieces[i:i + 4] for i in range(0, len(pieces), 4)]
                BATCHES[-1].append((lots, n + len(lots)))
                n += len(lots)
        COPIES = [2, 1, 1, 2]
        CREDIT = [4, 2, 1, 2]
        ROW_USES = [(0, 3), (0, 2), (1, 3), (1, 2), (2, 3)]

        def agg_of(l):
            if l == 1:
                return ends[:, :].rearrange("p (k c) -> p k c", k=NK)
            w = 128 if l == 0 else 64
            return wz[0:NP, :, :].rearrange("p a c -> p (a c)")[:, 0:NK * w].rearrange("p (k c) -> p k c", k=NK)

        block = ctx.enter_context(nc.Block())

        @block.sync
        def _(sp):
            def load_indices(l, g, s):
                sp.wait_ge(slot_free[l], g + 1)
                sp.dma_start(idx[:, s, :], src.rearrange("(p j) -> p j", j=J)[:, bass.ds(g * G, G)]
                             ).then_inc(idx_loaded[l][s], 16)
                if l == 0:
                    sp.dma_start(bond[:, s, :],
                                 attr64.rearrange("(p j) f -> p (j f)", j=J)[:, bass.ds(g * (G * D), G * D)]
                                 ).then_inc(bond_loaded[s], 16)

            dst2 = dst.rearrange("(p j) -> p j", j=J)
            sp.dma_start(dst_i[:, 1:J + 1], dst2).then_inc(dst_loaded, 16)
            sp.wait_ge(preset, 1)
            sp.dma_start(dst_i[1:P, 0:1], dst2[0:P - 1, J - 1:J],
                         allow_slow_non_contiguous=True).then_inc(dst_loaded, 16)
            sp.dma_start(nxt_i[0:P - 1, :], dst2[1:P, 0:1], allow_slow_non_contiguous=True).then_inc(dst_loaded, 16)
            load_indices(0, 0, 0)
            load_indices(0, 1, 1)
            sp.dma_start(xs[:, :, :], x.rearrange("(p k) f -> p k f", k=NK)).then_inc(x_loaded, 16)
            for t, a in ((w03[:, 0:128], w0), (w03[:, 128:192], w3),
                         (att0[:, 0:1], attn_l.rearrange("h (d a) -> (h d) a", a=1)),
                         (att0[:, 1:2], attn_r.rearrange("h (d a) -> (h d) a", a=1)),
                         (att3[:, 0:1], att_src.rearrange("(d a) -> d a", a=1)),
                         (att3[:, 1:2], att_dst.rearrange("(d a) -> d a", a=1)),
                         (wst0[0:D, :], w0[:, 0:D]), (wst0[D:P, :], w0[:, D:2 * D]),
                         (w1a[:, :].rearrange("o (k i) -> o k i", k=4), w1.rearrange("(k o) i -> o k i", k=4)),
                         (mu_b[:, :], mu.rearrange("k d -> (k d)").partition_broadcast(P)),
                         (inv_b[:, :], inv_sigma.rearrange("k d -> (k d)").partition_broadcast(P)),
                         (feat_b[:, 0, :], gamma.partition_broadcast(NP)),
                         (feat_b[:, 1, :], beta.partition_broadcast(NP)),
                         (feat_b[:, 2, :], bias1.partition_broadcast(NP)),
                         (feat_b[:, 3, :], bias3.partition_broadcast(NP))):
                sp.dma_start(t, a).then_inc(w_loaded, 16)
            sp.wait_ge(dstf_ready, 1)
            sp.dma_start(dst_rows, dst_f[:, 1:J + 1]).then_inc(dst_stored, 16)
            sp.wait_ge(zero_ready, 1)
            sp.dma_start(er_edges[0:EP, :].rearrange("(p j) h -> p (j h)", j=J),
                         mx[:, 0:2 * J]).then_inc(zeroed, 16)
            for l in range(4):
                sp.dma_start(run_tab[l][EP:EP + 1, :], mx[0:1, 0:ROWW[l]]).then_inc(zeroed, 16)
            sp.wait_ge(cross_ready, 1)
            sp.dma_start(pseudo[:, :, :], attr3.rearrange("(p j) d -> p j d", j=J)).then_inc(attr3_loaded, 16)
            sp.wait_ge(total_ready, 1)
            sp.dma_start(start_tab[N:N + 1, :], total_i[:, :]).then_inc(starts_stored, 16)

            def store_er():
                sp.dma_start(er_tab.rearrange("(p k) h -> p k h", k=NK), er_n[:, :, :]).then_inc(ern_stored, 16)

            def load_er(n):
                sp.wait_ge(er_put, 16 * NK * n)
                sp.dma_start(er_raw, er_edges[0:EP, :].rearrange("(p j) h -> p j h", j=J)).then_inc(er_loaded, 16)

            for s in range(2, U):
                load_indices(0, s, s)
            sp.wait_ge(ern_ready, 1)
            store_er()
            sp.wait_ge(starts_ready, 1)
            sp.dma_start(start_tab[0:N, :].rearrange("(p k) a -> p (k a)", k=NK), start_i[:, :]
                         ).then_inc(starts_stored, 16)
            sp.wait_ge(starts_stored, 32)
            sp.dma_start(next_i[:, :], start_tab[1:N + 1, :].rearrange("(p k) a -> p (k a)", k=NK)
                         ).then_inc(next_loaded, 16)
            load_er(1)
            for l in range(4):
                if l == 3:
                    for s in range(U):
                        load_indices(l, s, s)
                    sp.wait_ge(ern_ready, 2)
                    store_er()
                    load_er(2)
                with nc.sync.Fori(1 if l in SOFT else 0, IT) as it:
                    for s in range(U):
                        load_indices(l, it * U + s, s)
                if l < 3:
                    sp.wait_ge(x_ready, l + 1)
                    sp.dma_start(x_tab[l + 1].rearrange("(p k) f -> p k f", k=NK),
                                 (xt if l == 1 else xs)[:, :, :]).then_inc(x_stored, 16)
            sp.wait_ge(x_ready, 4)
            sp.dma_start(out.rearrange("(p k) f -> p k f", k=NK), xs[:, :, :]).then_inc(out_stored, 16)
            sp.wait_ge(out_stored, 16)
            sp.wait_ge(x_stored, 48)
            sp.wait_ge(dst_stored, 16)
            sp.wait_ge(zeroed, 80)
            sp.wait_ge(ern_stored, 32)
            sp.wait_ge(starts_stored, 32)
            sp.wait_ge(er_put, 32 * NK)
            for l in range(4):
                sp.wait_ge(row_free[l][0], 16 * (3 * IT + 1))
                sp.wait_ge(row_free[l][1], 16 * (2 * IT + 1))

        @block.gpsimd
        def _(pool):
            nc.gpsimd.iota(nid[:, :], [[1, NK]], base=0, channel_multiplier=NK,
                           allow_small_or_imprecise_dtypes=True).then_inc(iota_done, 1)
            nc.gpsimd.iota(ident[:, :], [[1, P]], base=0, channel_multiplier=-1,
                           allow_small_or_imprecise_dtypes=True).then_inc(iota_done, 1)
            nc.gpsimd.iota(total_i[:, :], [[1, 1]], base=E, channel_multiplier=0).then_inc(total_ready, 1)
            nc.gpsimd.iota(sel[:, :], [[1, N]], base=0, channel_multiplier=0,
                           allow_small_or_imprecise_dtypes=True).then_inc(iota_done, 1)

            def fetch_dst_rows():
                pool.wait_ge(dst_stored, 16)
                pool.wait_ge(cross_ready, 1)
                for k in range(NK):
                    if k >= DRING:
                        pool.wait_ge(drow_used, k - DRING + 1)
                    nc.gpsimd.indirect_dma_start(
                        drows[:, k % DRING, :], None, dst_rows,
                        bass.IndirectOffsetOnAxis(ap=bound_i[:, k:k + 1], axis=0)).then_inc(drow[k % DRING], 16)

            def gather_group(l, loads, s):
                pool.wait_ge(idx_loaded[l][s], loads)
                nc.gpsimd.nop(nofuse=True)
                for j in range(G):
                    nc.gpsimd.indirect_dma_start(
                        ring[:, s, j, 0:D], None, x_tab[l],
                        bass.IndirectOffsetOnAxis(ap=idx[:, s, j:j + 1], axis=0)).then_inc(gathered[l][s], 16)

            def scatter_er(n):
                pool.wait_ge(ern_stored, 16 * n)
                if n == 1:
                    pool.wait_ge(put_ready, 1)
                    pool.wait_ge(zeroed, 80)
                for k in range(NK):
                    nc.gpsimd.indirect_dma_start(
                        er_edges, bass.IndirectOffsetOnAxis(ap=put_i[:, k:k + 1], axis=0),
                        er_n[:, k, :], None).then_inc(er_put, 16)
                nc.gpsimd.indirect_dma_start(
                    er_first[:, :], None, er_tab,
                    bass.IndirectOffsetOnAxis(ap=dst_i[:, 1:2], axis=0)).then_inc(er_first_in, 16)

            for l in range(4):
                if l > 0:
                    pool.wait_ge(x_stored, 16 * l)
                if l in SOFT:
                    gather_group(l, 16, 0)
                    if l == 0:
                        fetch_dst_rows()
                        gather_group(l, 16, 1)
                    scatter_er(1 if l == 0 else 2)
                    for s in range(2 if l == 0 else 1, U):
                        gather_group(l, 16, s)
                with nc.gpsimd.Fori(1 if l in SOFT else 0, IT) as it:
                    for s in range(U):
                        gather_group(l, it * 16 + 16, s)
                pool.wait_ge(row_free[l][0], 16 * (3 * IT + 1))
                pool.wait_ge(row_free[l][1], 16 * (2 * IT + 1))
                for k in range(NK):
                    nc.gpsimd.indirect_dma_start(
                        ends[:, k * ROWW[l]:(k + 1) * ROWW[l]], None, run_tab[l],
                        bass.IndirectOffsetOnAxis(ap=end_i[:, k:k + 1], axis=0)).then_inc(ends_in[l][chunk_of(k)], 16)

        @block.scalar
        def _(act):
            act.wait_ge(w_loaded, 16 * 15)
            nc.scalar.mul(wst0h[:, :], wst0[:, :], 0.5).then_inc(wt_copied, 1)
            act.wait_ge(wt_psum, 1)
            nc.scalar.copy(w0t[:, :], pb[0][:, 0:D]).then_inc(wt_copied, 1)
            nc.scalar.copy(w3t[:, :], pb[0][0:D, D:2 * D]).then_inc(wt_copied, 1)
            nc.scalar.copy(wst1[:, :, :], pb[0][:, 2 * D:4 * D].rearrange("p (a o) -> p a o", a=2)
                           ).then_inc(wt_copied, 1)
            nc.scalar.copy(w1t[:, :, :], pb[0][0:D, 4 * D:8 * D].rearrange("p (k o) -> p k o", k=4)).then_inc(wt_copied, 1)
            act.wait_ge(vec_psum, 1)
            nc.scalar.copy(vecs[:, :, :], pb[1][:, 0:6 * D].rearrange("p (v f) -> p v f", v=6)).then_inc(vec_ready, 1)

            act.wait_ge(gauss_in, 1)
            act.wait_ge(attr3_loaded, 16)
            for k in range(4):
                if k >= 2:
                    act.wait_ge(gauss_sum, k - 1)
                for d in range(3):
                    nc.scalar.activation(squares[:, k % 2, d, :], pseudo[:, :, d], ACT.Square,
                                         bias=mi_b[:, 3 * k + d:3 * k + d + 1],
                                         scale=inv_b[:, 3 * k + d:3 * k + d + 1]).then_inc(gauss_sq, 1)
            act.wait_ge(gauss_sum, 4)
            nc.scalar.activation(gauss[:, :, :], gauss[:, :, :], ACT.Exp, scale=-0.5).then_inc(gauss_ready, 1)

            def decays(l, g, s):
                act.wait_ge(scanned[l], g * UNITS[l] + 1)
                if l in SOFT:
                    for h in range(UNITS[l]):
                        nc.scalar.copy(dec3(h)[:, :, 1:G + 1],
                                       wexp[:, s, 1, h:h + 1, :].broadcast_to([P, 65, G])).then_inc(dec_ready[l], 1)
                else:
                    flag = keep if l == 1 else neg
                    nc.scalar.copy(dec3(s % 2, D)[:, :, 1:G + 1],
                                   flag[:, bass.ds(g * G, G)].rearrange("p (a j) -> p a j", a=1)
                                   .broadcast_to([P, D, G])).then_inc(dec_ready[l], 1)

            def store_rows(l, g, it, s):
                before, per = ROW_USES[s]
                units, ch, stride = UNITS[l], CH[l], ROWW[l] // UNITS[l]
                slot = row_slot(l, s % 2)
                act.wait_ge(row_free[l][s % 2], it * (16 * per) + 16 * (before + 1))
                for k in range(units):
                    act.wait_ge(scanned[l], g * units + (k + 2))
                    nc.scalar.copy(slot[:, :, k * stride:k * stride + ch],
                                   run3(k % 2, ch)[:, :, 1:G + 1].rearrange("p f j -> p j f")
                                   ).then_inc(rows_copied[l], 1)
                    if l in SOFT:
                        nc.scalar.copy(slot[:, :, k * stride + 65:k * stride + 66],
                                       mxv[:, k, bass.ds(g * G + 1, G)].rearrange("p (j a) -> p j a", a=1)
                                       ).then_inc(rows_copied[l], 1)
                act.wait_ge(rows_copied[l], g * (units * COPIES[l]) + (units * COPIES[l] + CREDIT[l]))
                act.dma_start(run_store(l, g), slot).then_inc(row_free[l][s % 2], 16)

            rounds = exps = roots = batch = 0

            def node_exp(t, shape_in):
                act.wait_ge(exp_in, exps + 1)
                nc.scalar.activation(t, shape_in, ACT.Exp).then_inc(exp_ready, 1)

            def node_sqrt(t, sums=None, scale=1.0 / D, bias=eps):
                act.wait_ge(sqrt_in, roots + 1)
                nc.scalar.activation(t, t if sums is None else sums, ACT.Sqrt, scale=scale,
                                     bias=bias[0:NP, :]).then_inc(sqrt_out, 1)

            for l in range(4):
                units = UNITS[l]
                nc.scalar.sem_inc(row_free[l][0], 16)
                nc.scalar.sem_inc(row_free[l][1], 16)
                nc.scalar.sem_inc(rows_copied[l], CREDIT[l])
                with nc.scalar.Fori(0, IT) as it:
                    for s in range(U):
                        g = it * U + s
                        if l in SOFT:
                            act.wait_ge(logits_ready[l], g + 1)
                            nc.scalar.activation(wexp[:, s, :, 0:units, :], wexp_in[:, s, :, 0:units, :],
                                                 ACT.Exp).then_inc(w_ready[l], 1)
                            act.wait_ge(w_ready[l], g + 1)
                        decays(l, g, s)
                        if l == 2:
                            act.wait_ge(gathered[2][s], it * (16 * G) + 16 * G)
                            nc.scalar.copy(wz3(s % 2, D)[:, :, 1:G + 1],
                                           ring[:, s, :, 0:D].rearrange("p j f -> p f j")).then_inc(slot_free[2], 1)
                        store_rows(l, g, it, s)

                if l in SOFT:
                    node_exp(cexp[:, :, 0:units, :], cexp_in[:, :, 0:units, :])
                    exps += 1
                act.wait_ge(carry_back, l + 1)
                width = CORRW[l]
                nc.scalar.copy(carry[:, 0:width], pb[1][:, 0:width]).then_inc(carry_ready, 1)
                for b0, b1 in bank_blocks(l):
                    act.wait_ge(corr_psum, rounds + 1)
                    nc.scalar.copy(corr[:, b0 * width:b1 * width],
                                   pa[rounds % 4][0:NP, 0:(b1 - b0) * width]).then_inc(corr_copied, 1)
                    rounds += 1
                width = 64 if l == 3 else 128
                for b0, b1 in CHUNKS:
                    if l in SOFT:
                        parts = 2 if l == 0 else 3
                        node_exp(nexp[:, 0:parts, 0:units, b0:b1], nexp_in[:, 0:parts, 0:units, b0:b1])
                        exps += 1
                    for lot in BATCHES[l][chunk_of(b0)][0]:
                        act.wait_ge(agg_t, batch + 1)
                        if batch >= 2:
                            act.wait_ge(proj_done, batch - 1)
                        nc.scalar.copy(proj_t[0:width, batch % 2, 0:len(lot) * NP],
                                       pt[batch % 2][0:width, 0:len(lot) * NP]).then_inc(agg_tc, 1)
                        batch += 1
                    if l in (1, 3) and b0:
                        node_sqrt(st[:, 1, last[0]:last[1]])
                        roots += 1
                    elif l == 2:
                        node_sqrt(st[:, 1, b0:b1])
                        roots += 1
                    last = b0, b1
                if l in (1, 3):
                    node_sqrt(st[:, 1, last[0]:last[1]])
                    roots += 1
                if l == 0:
                    node_sqrt(norm[:, :], scale=1.0, bias=zero)
                    roots += 1
                    act.wait_ge(stat_sum, 2)
                    node_sqrt(bn[:, 2, :], pb[0][0:NP, 0:D], 1.0 / N)
                    roots += 1
                    node_sqrt(st[:, 1, :])
                    roots += 1

        @block.tensor
        def _(pe):
            pe.wait_ge(diag_ready, 1)
            nc.tensor.matmul(pa[0][:, 0:256], ones[:, :], diag[:, 0:2, :].rearrange("p a b -> p (a b)"),
                             start=True, stop=True).then_inc(rows_bcast, 1)
            pe.wait_ge(w_loaded, 16 * 15)
            nc.tensor.transpose(pb[0][:, 0:D], w03[:, 0:128], ident[0:D, 0:D])
            nc.tensor.transpose(pb[0][0:D, D:2 * D], w03[:, 128:192], ident[0:D, 0:D])
            for a in range(2):
                last = nc.tensor.transpose(pb[0][:, (2 + a) * D:(3 + a) * D], w1a[:, a * 128:(a + 1) * 128],
                                           ident[0:D, 0:D])
            for k in range(4):
                last = nc.tensor.transpose(pb[0][0:D, (4 + k) * D:(5 + k) * D], w1a[:, k * D:(k + 1) * D], ident[0:D, 0:D])
            last.then_inc(wt_psum, 1)
            pe.wait_ge(wt_copied, 5)
            pe.wait_ge(att_ready, 1)
            for v in range(4):
                nc.tensor.matmul(pb[1][:, v * D:(v + 1) * D], attb[:, v, :], w0t[:, :], start=True, stop=True)
            for v in range(4, 6):
                last = nc.tensor.matmul(pb[1][:, v * D:(v + 1) * D], attb[0:D, v, :], w3t[:, :], start=True, stop=True)
            last.then_inc(vec_psum, 1)

            rounds = stats = 0
            for l in range(4):
                units, ch, w = UNITS[l], CH[l], CORRW[l]
                stride = ROWW[l] // units
                pe.wait_ge(tail_ready, l + 1)
                if l in SOFT:
                    nc.tensor.matmul(pt[0][:, 0:units * P], ones[:, :],
                                     diag[:, 0:units, :].rearrange("p a b -> p (a b)"), start=True, stop=True)
                for k in range(units):
                    last = nc.tensor.transpose(pb[0][0:ch, k * P:(k + 1) * P],
                                               wz3(k, ch)[:, :, 0:1].rearrange("p f a -> p (f a)"), ident[:, :])
                last.then_inc(tails_t, 1)
                pe.wait_ge(carry_scanned, l + 1)
                if l == 1:
                    for k in range(4):
                        last = nc.tensor.matmul(pb[1][:, 0:D], carry_t[0:D, k, 0:P], w1t[:, k, :],
                                                start=(k == 0), stop=(k == 3))
                else:
                    for k in range(units):
                        last = nc.tensor.transpose(pb[1][:, k * stride:k * stride + ch], carry_t[0:ch, k, 0:P],
                                                   ident[0:ch, 0:ch])
                        if l in SOFT:
                            last = nc.tensor.transpose(pb[1][:, k * stride + 65:k * stride + 66], mc[0:1, k, 0:P],
                                                       ident[0:1, 0:1])
                last.then_inc(carry_back, 1)
                if l == 0:
                    pe.wait_ge(sel_ready, 1)
                    for b in range(NK):
                        last = nc.tensor.matmul(pt[1][0:NP, b:b + 1], sel[:, b::NK], ones[:, 0:1],
                                                start=True, stop=True)
                    last.then_inc(negc_psum, 1)
                pe.wait_ge(carry_ready, l + 1)
                for b0, b1 in bank_blocks(l):
                    if rounds >= 4:
                        pe.wait_ge(corr_copied, rounds - 3)
                    for b in range(b0, b1):
                        last = nc.tensor.matmul(pa[rounds % 4][0:NP, (b - b0) * w:(b - b0 + 1) * w],
                                                sel[:, b::NK], carry[:, 0:w], start=True, stop=True)
                    last.then_inc(corr_psum, 1)
                    rounds += 1
                if not NPROJ[l]:
                    continue
                width = 64 if l == 3 else 128
                agg = agg_of(l)
                if l > 0:
                    pe.wait_ge(proj_read, PROJ_READS[l])
                pe.wait_ge(corr_copied, ROUNDS[l + 1])

                def arrived(c):
                    if l == 1:
                        b0, b1 = CHUNKS[c]
                        pe.wait_ge(ends_in[1][c], 16 * (b1 - b0))
                    else:
                        pe.wait_ge(agg_ready, (0 if l == 0 else len(CHUNKS)) + c + 1)

                def turn(n, lot):
                    if n >= 2:
                        pe.wait_ge(agg_tc, n - 1)
                    for i, (b, c) in enumerate(lot):
                        last = nc.tensor.transpose(pt[n % 2][0:width, i * NP:(i + 1) * NP],
                                                   agg[:, b, c * 128:c * 128 + width], ident[0:NP, 0:NP])
                    last.then_inc(agg_t, 1)

                for chunk, (b0, b1) in enumerate(CHUNKS):
                    lots = BATCHES[l][chunk][0]
                    n0 = BATCHES[l][chunk][1] - len(lots)
                    arrived(chunk)
                    turn(n0, lots[0])
                    for n, lot in enumerate(lots, n0):
                        if n - n0 + 1 < len(lots):
                            turn(n + 1, lots[n - n0 + 1])
                        pe.wait_ge(agg_tc, n + 1)
                        for i, (b, c) in enumerate(lot):
                            rhs = wst0h[:, :] if l == 0 else wst1[:, c, :] if l == 1 else w03[:, 128:192]
                            product = pa[chunk][0:NP, (b - b0) * D:(b - b0 + 1) * D]
                            last = nc.tensor.matmul(product, proj_t[0:width, n % 2, i * NP:(i + 1) * NP], rhs,
                                                    start=(c == 0), stop=(c == NPROJ[l] - 1))
                        last.then_inc(proj_done, 1)
                if l == 0:
                    for c in range(len(CHUNKS)):
                        pe.wait_ge(stat_ready, c + 1)
                        last = nc.tensor.matmul(pb[0][0:NP, 0:D], ones[0:NP, 0:NP], parts[:, c, :],
                                                start=(c == 0), stop=(c == len(CHUNKS) - 1))
                    last.then_inc(stat_sum, 1)
                    pe.wait_ge(stat_ready, len(CHUNKS) + 1)
                    nc.tensor.matmul(pb[0][0:NP, 0:D], ones[0:NP, 0:NP], bn[:, 0, :],
                                     start=True, stop=True).then_inc(stat_sum, 1)

        @block.vector
        def _(dve):
            v = nc.vector
            step = Step(dve, dve_step)
            link = step.link

            v.memset(dst_i[:, 0:1], -1)
            v.memset(nxt_i[:, :], -1).then_inc(preset, 1)
            v.sem_inc(slot_free[0], U)
            v.memset(ones[:, :], 1.0)
            v.memset(eps[:, :], EPS)
            v.memset(zero[:, :], 0.0)
            v.memset(carry_t[:, :, 0:1], 0.0)
            v.memset(mc[:, :, 0:1], -BIG)
            v.memset(ring[:, :, :, D:D + 1], 1.0)
            v.memset(attb[:, :, :], 0.0)
            link(v.memset(mx[:, :], 0.0))
            v.sem_inc(zero_ready, 1)
            dve.wait_ge(iota_done, 2)
            link(v.tensor_scalar(ident[:, :], ident[:, :], 0.0, None, ALU.is_equal))
            dve.wait_ge(dst_loaded, 48)
            v.tensor_copy(nxt_f[:, :], nxt_i[:, :])
            link(v.tensor_copy(dst_f[:, :], dst_i[:, :]))
            v.sem_inc(dstf_ready, 1)
            first, last = dst_f[:, 1:2], dst_f[:, J:J + 1]
            CONT, SINGLE, NEXT, PASS, STOP, TAKE = range(6)

            def fl(i):
                return flags[:, i:i + 1]
            v.tensor_tensor(keep[:, :], dst_f[:, 1:J + 1], dst_f[:, 0:J], ALU.is_equal)
            v.tensor_tensor(fl(CONT), first, dst_f[:, 0:1], ALU.is_equal)
            v.tensor_tensor(fl(SINGLE), first, last, ALU.is_equal)
            link(v.tensor_tensor(fl(NEXT), nxt_f[:, :], last, ALU.is_equal))
            v.tensor_tensor(fl(PASS), fl(CONT), fl(SINGLE), ALU.mult)
            link(v.tensor_tensor(fl(STOP), fl(SINGLE), fl(NEXT), ALU.mult))
            v.tensor_scalar(neg[:, :], keep[:, :], -1.0, BIG, ALU.add, ALU.mult)
            v.tensor_scalar(diag[:, 0, :], ident[:, :], last, None, ALU.mult)
            link(v.tensor_scalar(diag[:, 1, :], ident[:, :], fl(PASS), None, ALU.mult))
            v.sem_inc(diag_ready, 1)
            link(v.tensor_scalar(fl(TAKE), fl(STOP), -1.0, 1.0, ALU.mult, ALU.add))
            link(v.tensor_tensor(fl(TAKE), fl(TAKE), fl(CONT), ALU.mult))
            dve.wait_ge(rows_bcast, 1)
            v.tensor_copy(pass_b[:, :], pa[0][:, P:2 * P])
            v.tensor_scalar(negpass_b[:, :], pa[0][:, P:2 * P], -1.0, BIG, ALU.add, ALU.mult)
            link(v.tensor_copy(last_row[:, :], pa[0][:, 0:P]))
            less = wz[0:NP, :, :].rearrange("p a c -> p (a c)")[:, 0:NK * P].rearrange("p (k b) -> p k b", k=NK)
            dve.wait_ge(iota_done, 3)
            link(v.tensor_tensor(less, last_row[0:NP, :].rearrange("p (a b) -> p a b", a=1).broadcast_to([NP, NK, P]),
                                 nid[:, :].rearrange("p (k a) -> p k a", a=1).broadcast_to([NP, NK, P]), ALU.is_lt))
            link(v.tensor_reduce(cross[:, :], less, AX, ALU.add))
            link(v.tensor_scalar(cross[:, :], cross[:, :], float(P - 1), None, ALU.min))
            link(v.tensor_copy(bound_i[:, :], cross[:, :]))
            v.sem_inc(cross_ready, 1)
            dve.wait_ge(w_loaded, 16 * 15)
            for a, (p0, p1) in ((0, (0, D)), (1, (D, P))):
                v.tensor_scalar(attb[p0:p1, a, :], ones[p0:p1, :], att0[p0:p1, 0:1], None, ALU.mult)
                v.tensor_scalar(attb[p0:p1, 2 + a, :], ones[p0:p1, :], att0[p0:p1, 1:2], None, ALU.mult)
            v.tensor_scalar(attb[0:D, 4, :], ones[0:D, :], att3[:, 0:1], None, ALU.mult)
            link(v.tensor_scalar(attb[0:D, 5, :], ones[0:D, :], att3[:, 1:2], None, ALU.mult))
            v.sem_inc(att_ready, 1)
            link(v.scalar_tensor_tensor(mi_b[:, :], mu_b[:, :], -1.0, inv_b[:, :], ALU.mult, ALU.mult))
            v.sem_inc(gauss_in, 1)
            link(v.tensor_scalar(sel[:, :], sel[:, :], first, fl(TAKE), ALU.is_equal, ALU.mult))
            v.sem_inc(sel_ready, 1)

            def node_dot(dst_ap, vec):
                link(v.tensor_tensor(xt[:, :, :], xs[:, :, :], vec.rearrange("p (a f) -> p a f", a=1)
                                     .broadcast_to([NP, NK, D]), ALU.mult))
                link(v.tensor_reduce(dst_ap, xt[:, :, :], AX, ALU.add))

            dve.wait_ge(vec_ready, 1)
            dve.wait_ge(x_loaded, 16)
            node_dot(er_n[:, :, 0], vecs[0:NP, 2, :])
            node_dot(er_n[:, :, 1], vecs[0:NP, 3, :])
            v.sem_inc(ern_ready, 1)
            for k in range(NK):
                dve.wait_ge(drow[k % DRING], 16 * (k // DRING + 1))
                v.tensor_scalar(drows[:, k % DRING, :], drows[:, k % DRING, :], nid[:, k:k + 1], None,
                                ALU.is_lt, ALU.add, accum_out=below[:, k:k + 1]).then_inc(drow_used, 1)
            dve.wait_ge(drow_used, NK)
            link(v.scalar_tensor_tensor(startf[:, :], cross[:, :], float(J), below[:, :], ALU.mult, ALU.add))
            link(v.tensor_copy(start_i[:, :], startf[:, :]))
            v.sem_inc(starts_ready, 1)
            dve.wait_ge(next_loaded, 16)
            link(v.tensor_copy(nextf[:, :], next_i[:, :]))
            deg, t0, t1 = st[:, 2, :], st[:, 3, :], st[:, 4, :]
            v.tensor_scalar(t1, nextf[:, :], -1.0 - EP, None, ALU.add)
            link(v.tensor_tensor(deg, nextf[:, :], startf[:, :], ALU.subtract))
            v.tensor_scalar(norm[:, :], deg, 1.0, None, ALU.max)
            link(v.tensor_scalar(has[:, :], deg, 1.0, None, ALU.min))
            link(v.tensor_scalar(nege[:, :], has[:, :], -1.0, BIG, ALU.add, ALU.mult))
            link(v.tensor_tensor(t1, t1, has[:, :], ALU.mult))
            link(v.tensor_scalar(t1, t1, float(EP), None, ALU.add))
            v.tensor_copy(end_i[:, :], t1)
            link(v.tensor_scalar(t0, nid[:, :], float(EP), None, ALU.add))
            link(v.tensor_tensor(t1, startf[:, :], t0, ALU.subtract))
            link(v.tensor_tensor(t1, t1, has[:, :], ALU.mult))
            link(v.tensor_tensor(t0, t0, t1, ALU.add))
            link(v.tensor_copy(put_i[:, :], t0))
            v.sem_inc(put_ready, 1)
            for k in range(4):
                dve.wait_ge(gauss_sq, 3 * (k + 1))
                link(v.tensor_tensor(gauss[:, k, :], squares[:, k % 2, 0, :], squares[:, k % 2, 1, :], ALU.add))
                link(v.tensor_tensor(gauss[:, k, :], gauss[:, k, :], squares[:, k % 2, 2, :], ALU.add))
                v.sem_inc(gauss_sum, 1)

            def expand_er(n, heads):
                dve.wait_ge(er_loaded, 16 * n)
                dve.wait_ge(er_first_in, 16 * n)
                for h in range(heads):
                    last_scan = v.tensor_tensor_scan(er[:, h, :], keep[:, :], er_raw[:, :, h], er_first[:, h:h + 1],
                                                     ALU.mult, ALU.add)
                link(last_scan)
                link(v.memset(mxv[:, :, 0:1], -BIG))

            def prepare(l):
                op_max = l == 2
                for k in range(4):
                    v.memset(wz3(k)[:, :, 0:1], -BIG if op_max else 0.0)
                for k in range(2):
                    ins = v.memset(dec3(k)[:, :, 0:1], -BIG if op_max else 0.0)
                link(ins)
                v.sem_inc(scanned[l], 1)

            def logits(l, g, it, s):
                heads = UNITS[l]
                vec0 = 0 if l == 0 else 4
                dve.wait_ge(gathered[l][s], it * (16 * G) + 16 * G)
                if l == 0:
                    dve.wait_ge(bond_loaded[s], it * 16 + 16)
                    link(v.tensor_tensor(ring[:, s, :, 0:D], ring[:, s, :, 0:D],
                                         bond[:, s, :].rearrange("p (j f) -> p j f", j=G), ALU.add))
                for h in range(heads):
                    ins = v.tensor_tensor(prod[:, h, :, :], ring[:, s, :, 0:D],
                                          vecs[:, vec0 + h:vec0 + h + 1, :].broadcast_to([P, G, D]), ALU.mult)
                link(ins)
                link(v.tensor_reduce(dot[:, 0:heads, :], prod[:, 0:heads, :, :], AX, ALU.add))
                link(v.tensor_tensor(dot[:, 0:heads, :], dot[:, 0:heads, :], er[:, 0:heads, bass.ds(g * G, G)], ALU.add))
                link(v.scalar_tensor_tensor(logit[:, 0:heads, :], dot[:, 0:heads, :], SLOPE, dot[:, 0:heads, :],
                                            ALU.mult, ALU.max))
                for h in range(heads):
                    ins = v.tensor_tensor_scan(mxv[:, h, bass.ds(g * G + 1, G)], neg[:, bass.ds(g * G, G)],
                                               logit[:, h, :], mxv[:, h, bass.ds(g * G, 1)], ALU.add, ALU.max)
                link(ins)
                now, before = mxv[:, 0:heads, bass.ds(g * G + 1, G)], mxv[:, 0:heads, bass.ds(g * G, G)]
                link(v.tensor_tensor(wexp_in[:, s, 1, 0:heads, :], before,
                                     neg[:, bass.ds(g * G, G)].rearrange("p (a j) -> p a j", a=1)
                                     .broadcast_to([P, heads, G]), ALU.add))
                v.tensor_tensor(wexp_in[:, s, 0, 0:heads, :], logit[:, 0:heads, :], now, ALU.subtract)
                v.tensor_tensor(wexp_in[:, s, 1, 0:heads, :], wexp_in[:, s, 1, 0:heads, :], now,
                                ALU.subtract).then_inc(logits_ready[l], 1)

            def scans(l, g, s):
                units, ch = UNITS[l], CH[l]
                if l in SOFT:
                    dve.wait_ge(w_ready[l], g + 1)
                if l != 2:
                    for k in range(units):
                        weight = wexp[:, s, 0, k:k + 1, :] if l in SOFT else gauss[:, k:k + 1, bass.ds(g * G, G)]
                        ins = v.tensor_tensor(wz3(k, ch)[:, :, 1:G + 1], ring[:, s, :, 0:ch].rearrange("p j f -> p f j"),
                                              weight.broadcast_to([P, ch, G]), ALU.mult)
                    link(ins)
                    v.sem_inc(slot_free[l], 1)
                else:
                    dve.wait_ge(slot_free[2], g + (U + 1))

                def keep_last(k):
                    to = wz3((s + 1) % U % 2 if l == 2 else k, ch)
                    dve.wait_ge(scanned[l], g * units + (k + 2))
                    return v.tensor_copy(to[:, :, 0:1], run3(k % 2, ch)[:, :, G:G + 1])

                for k in range(units):
                    if l in SOFT or k == 0:
                        dve.wait_ge(dec_ready[l], g * (units if l in SOFT else 1) + ((k if l in SOFT else 0) + 1))
                    dve.wait_ge(rows_copied[l], g * (units * COPIES[l]) + (k * COPIES[l] + 1))
                    d = dec[:, k if l in SOFT else s % 2, 0:ch * (G + 1)]
                    z = wz[:, s % 2 if l == 2 else k, 0:ch * (G + 1)]
                    ops = (ALU.add, ALU.max) if l == 2 else (ALU.mult, ALU.add)
                    v.tensor_tensor_scan(run[:, k % 2, 0:ch * (G + 1)], d, z, 0.0, *ops).then_inc(scanned[l], 1)
                    if 0 < k < units - 1:
                        link(keep_last(k - 1))
                    elif k > 0:
                        keep_last(k - 1)
                link(keep_last(units - 1))

            def loop_soft(l):
                a, f = (7, 2) if l == 0 else (6, 2)
                logits(l, 0, 0, 0)
                with nc.vector.Fori(0, IT - 1) as it:
                    step.enter(it, U * (a + f))
                    for s in range(U):
                        nxt = it + 1 if s == U - 1 else it
                        logits(l, it * U + (s + 1), nxt, (s + 1) % U)
                        scans(l, it * U + s, s)
                step.leave(IT - 1)
                for s in range(U):
                    g = (IT - 1) * U + s
                    if s < U - 1:
                        logits(l, g + 1, IT - 1, s + 1)
                    scans(l, g, s)

            def loop_plain(l):
                with nc.vector.Fori(0, IT) as it:
                    step.enter(it, U * (1 if l == 2 else 4))
                    for s in range(U):
                        if l == 1:
                            dve.wait_ge(gathered[l][s], it * (16 * G) + 16 * G)
                        scans(l, it * U + s, s)
                step.leave(IT)

            n_exp = n_root = 0

            def carries(l):
                nonlocal n_exp
                units, ch = UNITS[l], CH[l]
                if l in SOFT:
                    for h in range(units):
                        ins = v.tensor_scalar(diag[:, h, :], ident[:, :], mxv[:, h, J:J + 1], None, ALU.mult)
                    link(ins)
                v.sem_inc(tail_ready, 1)
                dve.wait_ge(tails_t, l + 1)
                tails = pb[0]
                if l in SOFT:
                    mrow = pt[0][:, 0:units * P].rearrange("p (h b) -> p h b", h=units)
                    for h in range(units):
                        ins = v.tensor_tensor_scan(mc[:, h, 1:P + 1], negpass_b[:, :], mrow[:, h, :], -BIG,
                                                   ALU.add, ALU.max)
                    link(ins)
                    v.tensor_tensor(cexp_in[:, 1, 0:units, :], mrow, mc[:, 0:units, 1:P + 1], ALU.subtract)
                    link(v.tensor_tensor(cexp_in[:, 0, 0:units, :], mc[:, 0:units, 0:P],
                                         negpass_b[:, :].rearrange("p (a b) -> p a b", a=1)
                                         .broadcast_to([P, units, P]), ALU.add))
                    v.tensor_tensor(cexp_in[:, 0, 0:units, :], cexp_in[:, 0, 0:units, :], mc[:, 0:units, 1:P + 1],
                                    ALU.subtract).then_inc(exp_in, 1)
                    n_exp += 1
                    dve.wait_ge(exp_ready, n_exp)
                    for h in range(units):
                        ins = v.tensor_tensor(tail_s[0:ch, h, :], tails[0:ch, h * P:(h + 1) * P], cexp[0:ch, 1, h, :],
                                              ALU.mult)
                    link(ins)
                    for h in range(units):
                        ins = v.tensor_tensor_scan(carry_t[0:ch, h, 1:P + 1], cexp[0:ch, 0, h, :], tail_s[0:ch, h, :],
                                                   0.0, ALU.mult, ALU.add)
                else:
                    for k in range(units):
                        ins = v.tensor_tensor_scan(
                            carry_t[0:ch, k, 1:P + 1], (negpass_b if l == 2 else pass_b)[0:ch, :],
                            tails[0:ch, k * P:(k + 1) * P], -BIG if l == 2 else 0.0,
                            *((ALU.add, ALU.max) if l == 2 else (ALU.mult, ALU.add)))
                ins.then_inc(carry_scanned, 1)

            def bk(ap, n):
                return ap.rearrange("p (k a) -> p k a", a=1).broadcast_to([NP, ap.shape[1], n])

            def bf(ap, n=NK):
                return ap.rearrange("p (a f) -> p a f", a=1).broadcast_to([NP, n, D])

            def merge_soft(l, b0, b1):
                nonlocal n_exp
                heads, nk = UNITS[l], b1 - b0
                e4 = ends[:, b0 * ROWW[l]:b1 * ROWW[l]].rearrange("p (k h c) -> p k h c", k=nk, h=heads)
                c4 = corr[:, b0 * ROWW[l]:b1 * ROWW[l]].rearrange("p (k h c) -> p k h c", k=nk, h=heads)
                agg = agg_of(l)[:, b0:b1, :]
                x0, x1, x2 = (nexp_in[:, i, :, b0:b1] for i in range(3))
                f0, f1, f2 = (nexp[:, i, :, b0:b1] for i in range(3))
                m_all, den = small[:, 0, :, b0:b1], small[:, 1, :, b0:b1]
                m_ends = e4[:, :, :, 65].rearrange("p k h -> p h k")
                m_corr = c4[:, :, :, 65].rearrange("p k h -> p h k")
                d_ends = e4[:, :, :, 64].rearrange("p k h -> p h k")
                d_corr = c4[:, :, :, 64].rearrange("p k h -> p h k")

                def both(ap):
                    return ap[:, b0:b1].rearrange("p (a k) -> p a k", a=1).broadcast_to([NP, heads, nk])
                s0, s1 = x0[:, 0:heads, :], x1[:, 0:heads, :]
                m_all, den = m_all[:, 0:heads, :], den[:, 0:heads, :]
                link(v.tensor_tensor(s0, m_ends, both(nege), ALU.add))
                link(v.tensor_tensor(s1, m_corr, both(negc), ALU.add))
                link(v.tensor_tensor(m_all, s0, s1, ALU.max))
                if l == 3:
                    link(v.tensor_tensor(m_all, m_all, both(loop_logit), ALU.max))
                    v.tensor_tensor(x2[:, 0:heads, :], both(loop_logit), m_all, ALU.subtract)
                v.tensor_tensor(s0, s0, m_all, ALU.subtract)
                link(v.tensor_tensor(s1, s1, m_all, ALU.subtract))
                v.sem_inc(exp_in, 1)
                n_exp += 1
                dve.wait_ge(exp_ready, n_exp)
                s0, s1, s2 = f0[:, 0:heads, :], f1[:, 0:heads, :], f2[:, 0:heads, :]
                tmp = small[:, 2, 0:heads, b0:b1]
                v.tensor_tensor(den, d_ends, s0, ALU.mult)
                link(v.tensor_tensor(tmp, d_corr, s1, ALU.mult))
                link(v.tensor_tensor(den, den, tmp, ALU.add))
                if l == 3:
                    link(v.tensor_tensor(den, den, s2, ALU.add))
                link(v.tensor_scalar(den, den, 1e-16 if l == 3 else 0.0, 1e-30, ALU.add, ALU.max))
                link(v.reciprocal(den, den))
                if l == 3:
                    v.tensor_tensor(s2, s2, den, ALU.mult)
                v.tensor_tensor(s0, s0, den, ALU.mult)
                link(v.tensor_tensor(s1, s1, den, ALU.mult))
                for h in range(heads):
                    to = agg[:, :, h * D:(h + 1) * D]
                    v.tensor_tensor(to, e4[:, :, h, 0:D], bk(f0[:, h, :], D), ALU.mult)
                    link(v.tensor_tensor(c4[:, :, h, 0:D], c4[:, :, h, 0:D], bk(f1[:, h, :], D), ALU.mult))
                    ins = v.tensor_tensor(to, to, c4[:, :, h, 0:D], ALU.add)
                    if l == 3:
                        link(ins)
                        link(v.tensor_tensor(xt[:, b0:b1, :], xs[:, b0:b1, :], bk(f2[:, h, :], D), ALU.mult))
                        ins = v.tensor_tensor(to, to, xt[:, b0:b1, :], ALU.add)
                link(ins)
                v.sem_inc(agg_ready, 1)

            def root(t):
                nonlocal n_root
                v.sem_inc(sqrt_in, 1)
                n_root += 1
                dve.wait_ge(sqrt_out, n_root)
                link(v.reciprocal(t, t))

            def free_slots(l):
                if l == 3:
                    link(v.memset(ring[:, :, :, D:D + 1], 1.0))
                v.sem_inc(slot_free[l], U)

            def projected(l, b0, b1):
                dve.wait_ge(proj_done, BATCHES[l][chunk_of(b0)][1])
                p = pa[chunk_of(b0)][0:NP, 0:(b1 - b0) * D].rearrange("p (k f) -> p k f", f=D)
                w = xw[:, b0:b1, :]
                if l == 0:
                    ins = v.tensor_copy(w, p)
                else:
                    ins = v.tensor_tensor(w, w, p, ALU.add)
                link(ins)
                v.sem_inc(proj_read, 1)

            def layer_norm(l, b0, b1):
                mean, var = st[:, 0, b0:b1], st[:, 1, b0:b1]
                w, t = xw[:, b0:b1, :], xt[:, b0:b1, :]
                link(v.tensor_reduce(mean, w, AX, ALU.add))
                link(v.scalar_tensor_tensor(w, bk(mean, D), -1.0 / D, w, ALU.mult, ALU.add))
                link(v.tensor_tensor(t, w, w, ALU.mult))
                link(v.tensor_reduce(var, t, AX, ALU.add))
                root(var)
                if l == 1:
                    link(v.tensor_tensor(mean, var, norm[:, b0:b1], ALU.mult))
                    link(v.tensor_tensor(t, w, bk(mean, D), ALU.mult))
                else:
                    link(v.tensor_tensor(xs[:, b0:b1, :], w, bk(var, D), ALU.mult))

            expand_er(1, 2)
            prepare(0)
            loop_soft(0)
            carries(0)
            dve.wait_ge(negc_psum, 1)
            link(v.tensor_scalar(negc[:, :], pt[1][0:NP, 0:NK], -1.0, BIG, ALU.add, ALU.mult))
            by_f = "p k f -> p f k"

            def part_sum(c):
                b0, b1 = CHUNKS[c]
                projected(0, b0, b1)
                link(v.tensor_reduce(parts[:, c, :], xw[:, b0:b1, :].rearrange(by_f), AX, ALU.add))
                v.sem_inc(stat_ready, 1)

            dve.wait_ge(corr_copied, ROUNDS[1])
            for c, (b0, b1) in enumerate(CHUNKS):
                dve.wait_ge(ends_in[0][c], 16 * (b1 - b0))
                merge_soft(0, b0, b1)
                if c:
                    part_sum(c - 1)
            free_slots(1)
            part_sum(len(CHUNKS) - 1)
            root(norm[:, :])
            dve.wait_ge(stat_sum, 1)
            link(v.scalar_tensor_tensor(xw[:, :, :], bf(pb[0][0:NP, 0:D]), -1.0 / N, xw[:, :, :], ALU.mult, ALU.add))
            link(v.tensor_tensor(xt[:, :, :], xw[:, :, :], xw[:, :, :], ALU.mult))
            link(v.tensor_reduce(bn[:, 0, :], xt[:, :, :].rearrange(by_f), AX, ALU.add))
            v.sem_inc(stat_ready, 1)
            root(bn[:, 2, :])
            link(v.tensor_tensor(bn[:, 2, :], bn[:, 2, :], feat_b[:, 0, :], ALU.mult))
            link(v.tensor_tensor(xw[:, :, :], xw[:, :, :], bf(bn[:, 2, :]), ALU.mult))
            link(v.tensor_tensor(xw[:, :, :], xw[:, :, :], bf(feat_b[:, 1, :]), ALU.add))
            link(v.scalar_tensor_tensor(xw[:, :, :], xw[:, :, :], 0.0, xs[:, :, :], ALU.max, ALU.add))
            layer_norm(0, 0, NK)
            v.sem_inc(x_ready, 1)

            prepare(1)
            dve.wait_ge(gauss_ready, 1)
            loop_plain(1)
            carries(1)
            dve.wait_ge(x_stored, 16)
            link(v.tensor_scalar(xw[:, :, :], xs[:, :, :], 2.0, None, ALU.mult))
            link(v.tensor_tensor(xw[:, :, :], xw[:, :, :], bf(feat_b[:, 2, :]), ALU.add))
            dve.wait_ge(corr_copied, ROUNDS[2])
            link(v.tensor_tensor(xw[:, :, :], xw[:, :, :], corr[:, 0:NK * D].rearrange("p (k f) -> p k f", k=NK),
                                 ALU.add))
            free_slots(2)
            for b0, b1 in CHUNKS:
                projected(1, b0, b1)
                layer_norm(1, b0, b1)
            v.sem_inc(x_ready, 1)
            link(v.tensor_tensor(xs[:, :, :], xw[:, :, :], bk(st[:, 1, :], D), ALU.mult))

            prepare(2)
            loop_plain(2)
            carries(2)
            corr2 = corr[:, 0:NK * D].rearrange("p (k f) -> p k f", k=NK)
            ends2 = ends[:, 0:NK * D].rearrange("p (k f) -> p k f", k=NK)
            dve.wait_ge(corr_copied, ROUNDS[3])
            link(v.tensor_tensor(corr2, corr2, bk(negc[:, :], D), ALU.add))
            dve.wait_ge(x_stored, 32)
            for c, (b0, b1) in enumerate(CHUNKS):
                dve.wait_ge(ends_in[2][c], 16 * (b1 - b0))
                w = xw[:, b0:b1, :]
                link(v.tensor_tensor(w, corr2[:, b0:b1, :], ends2[:, b0:b1, :], ALU.max))
                link(v.tensor_tensor(w, w, bk(norm[:, b0:b1], D), ALU.mult))
                link(v.tensor_tensor(w, w, xs[:, b0:b1, :], ALU.add))
                layer_norm(2, b0, b1)
            free_slots(3)
            v.sem_inc(x_ready, 1)

            node_dot(er_n[:, :, 0], vecs[0:NP, 5, :])
            v.sem_inc(ern_ready, 1)
            node_dot(st[:, 2, :], vecs[0:NP, 4, :])
            link(v.tensor_tensor(st[:, 2, :], st[:, 2, :], er_n[:, :, 0], ALU.add))
            link(v.scalar_tensor_tensor(loop_logit[:, :], st[:, 2, :], SLOPE, st[:, 2, :], ALU.mult, ALU.max))
            expand_er(2, 1)
            prepare(3)
            loop_soft(3)
            carries(3)
            dve.wait_ge(x_stored, 48)
            link(v.tensor_tensor(xw[:, :, :], xs[:, :, :], bf(feat_b[:, 3, :]), ALU.add))
            dve.wait_ge(corr_copied, ROUNDS[4])
            for c, (b0, b1) in enumerate(CHUNKS):
                dve.wait_ge(ends_in[3][c], 16 * (b1 - b0))
                merge_soft(3, b0, b1)
                if c:
                    projected(3, *CHUNKS[c - 1])
                    layer_norm(3, *CHUNKS[c - 1])
            projected(3, *CHUNKS[-1])
            layer_norm(3, *CHUNKS[-1])

            v.sem_inc(x_ready, 1)


_INS = ["x", "src", "dst", "edge_attr_3", "edge_attr_64", "L0_gnn_W", "L0_gnn_attn_l", "L0_gnn_attn_r",
        "L0_gnn_bn_gamma", "L0_gnn_bn_beta", "L1_gnn_W_fc", "L1_gnn_mu", "L1_gnn_inv_sigma", "L1_gnn_bias",
        "L3_gnn_W", "L3_gnn_att_src", "L3_gnn_att_dst", "L3_gnn_bias"]


def kernel(**inputs):
    import numpy as _np
    import concourse.bacc as _bacc
    from concourse.bass_utils import run_bass_kernel_spmd as _run

    nc = _bacc.Bacc("TRN2", target_bir_lowering=False, num_devices=1)
    arrays, args = {}, []
    for name in _INS:
        a = _np.ascontiguousarray(inputs[name])
        if a.shape[0] == E:
            padded = _np.full((EP,) + a.shape[1:], N if name == "dst" else 0, a.dtype)
            padded[:E] = a
            a = padded
        arrays[f"in_{name}"] = a
        args.append(nc.dram_tensor(f"in_{name}", a.shape, mybir.dt.from_np(a.dtype), kind="ExternalInput").ap())
    args.append(nc.dram_tensor("out_0", (N, D), F32, kind="ExternalOutput").ap())
    gnn(nc, *args)
    return _run(nc, [arrays], core_ids=[0]).results[0]["out_0"]
```

```python
from contextlib import ExitStack

import concourse.bass as bass
from concourse import mybir

F32 = mybir.dt.float32
I32 = mybir.dt.int32
I16 = mybir.dt.int16
BF16 = mybir.dt.bfloat16
ALU = mybir.AluOpType
ACT = mybir.ActivationFunctionType
AX = mybir.AxisListType.X

N = 3125
E = 103125
D = 64
P = 128
J = 810
EP = P * J
NP = 125
NK = N // NP
G = 18
U = 5
NG = J // G
IT = NG // U
BIG = 1e37
EPS = 1e-5
SLOPE = 0.2
ROWW = [132, 256, 64, 66]
UNITS = [2, 4, 1, 1]
CORRW = [132, 64, 64, 66]
CH = [65, 64, 64, 65]
CHUNKS = [(0, 6), (6, 13), (13, 19), (19, 25)]
C = [0, 2, 4, 4]
GP = [G - c for c in C]
AHEAD = [0, 1, 1, 2]
LOTS = 5
LB = NK // LOTS
DVE_LOTS = [0, 3, 4, 4]
DRING = 5


class Step:

    def __init__(self, eng, sem):
        self.eng, self.sem, self.total, self.local, self.it, self.per = eng, sem, 0, 0, None, 0

    def link(self, ins):
        ins.then_inc(self.sem, 1)
        self.local += 1
        if self.it is None:
            self.total, self.local = self.total + 1, 0
            self.eng.wait_ge(self.sem, self.total)
        else:
            self.eng.wait_ge(self.sem, self.it * self.per + (self.total + self.local))

    def enter(self, it, per):
        self.it, self.per, self.local = it, per, 0

    def leave(self, iterations):
        assert self.local == self.per, (self.local, self.per)
        self.total += iterations * self.per
        self.it, self.local = None, 0


def gnn(nc, x, src, src_t, dst, attr3, attr64, w0, attn_l, attn_r, gamma, beta,
        w1, mu, inv_sigma, bias1, w3, att_src, att_dst, bias3, out):
    with ExitStack() as ctx:
        def sb(name, shape, dt=F32):
            return ctx.enter_context(nc.sbuf_tensor(name, shape, dt))

        def dram(name, shape, dt=F32):
            return nc.dram_tensor(name, shape, dt, kind="Internal").ap()

        def sem(name):
            return ctx.enter_context(nc.semaphore(name))

        dst_rows = dram("dst_rows", [P, J])
        start_tab = dram("start_tab", [N + 1, 1], I32)
        er_tab = dram("er_tab", [N, 2])
        er_edges = dram("er_edges", [EP + N, 2])
        x_tab = [x] + [dram(f"x_tab{l}", [N, D]) for l in (1, 2, 3)]
        run_tab = [dram(f"run_tab{l}", [EP + 1, ROWW[l]]) for l in range(4)]

        ring_big = sb("ring_big", [P, U * G * 65 + 2 * G * D])
        ring = ring_big[:, 0:U * G * 65].rearrange("p (s j f) -> p s j f", s=U, j=G)
        prod = ring_big[:, U * G * 65:].rearrange("p (h j f) -> p h j f", h=2, j=G)
        corr = ring_big[0:NP, 0:NK * 132]
        proj_t = ring_big[:, NK * 256:NK * 256 + 8 * NP].rearrange("p (b n) -> p b n", b=2)
        wz = sb("wz", [P, 4, 65 * (G + 1)])
        pseudo = wz[:, :, :].rearrange("p a c -> p (a c)")[:, 0:3 * J].rearrange("p (j d) -> p j d", d=3)
        before_loops = ring_big[:, U * G * 65:]
        dst_f = before_loops[:, 0:J + 1]
        prod_tail = ring_big[:, NK * 256 + 8 * NP:NK * 256 + 8 * NP + 4 * D]
        attb = before_loops[:, J + 1:J + 1 + 6 * P].rearrange("p (v c) -> p v c", v=6)
        dec_run = sb("dec_run", [P, 4, 65 * (G + 1)])
        dec = dec_run[:, 0:2, :]
        run = dec_run[:, 2:4, :]
        squares = dec_run[:, :, :].rearrange("p a c -> p (a c)")[:, 0:6 * J].rearrange(
            "p (b d j) -> p b d j", b=2, d=3)
        RROW = 2 * G * 132
        rows_big = sb("rows_big", [P, max(RROW + U * G * D, 2 * G * 256)])
        bond = rows_big[:, RROW:RROW + U * G * D].rearrange("p (s c) -> p s c", s=U)
        drows = rows_big[0:NP, 0:DRING * J].rearrange("p (s c) -> p s c", s=DRING)

        def hot(l, i):
            n = LB * C[l] * P // 2
            if l == 1:
                space, o = (before_loops, i * n) if i < 3 else (rows_big, 2 * G * 256 + (i - 3) * n)
            else:
                space, o = rows_big, 2400 + i * n
            return space[0:NP, o:o + n].bitcast(BF16).rearrange("p (b e) -> p b e", b=LB)

        ends = rows_big[0:NP, 0:NK * 256]
        er_mx = sb("er_mx", [P, 2 * J + 2 * (J + 1)])
        er = er_mx[:, 0:2 * J].rearrange("p (h j) -> p h j", h=2)
        mx = er_mx[:, 2 * J:]
        mxv = mx[:, :].rearrange("p (h j) -> p h j", h=2)
        er_raw = mx[:, 0:2 * J].rearrange("p (j h) -> p j h", h=2)
        neg = sb("neg", [P, J])
        keep = sb("keep", [P, J])
        gauss = sb("gauss", [P, 4, J])
        dot = sb("dot", [P, 2, G])

        def spare(l):
            return er_mx[0:NP, :] if l == 1 else gauss[0:NP, :, :].rearrange("p k j -> p (k j)")

        def split(l):
            return spare(l)[:, 0:NK * 96].bitcast(BF16).rearrange("p (k t f) -> p k t f", k=NK, t=3)

        def srow16(l, slot):
            n = C[l] * 65
            o = slot % U % 3 * n
            return xw[:, :, :].rearrange("p k f -> p (k f)")[:, o:o + n].bitcast(I16).rearrange("p (c e) -> p c e", c=C[l])[:, :, 0:P]

        def srow32(l):
            if l == 1:
                return spare(1)[:, NK * 96:NK * 96 + C[1] * P].bitcast(I32)
            return er[0:NP, 1, 0:C[l] * P].bitcast(I32)

        logit = sb("logit", [P, 2, G])
        wexp_in = sb("wexp_in", [P, U, 2, 2, G])
        wexp = sb("wexp", [P, U, 2, 2, G])
        idx = sb("idx", [P, U, G], I32)
        dst_i = sb("dst_i", [P, J + 1], I32)
        nxt_i = sb("nxt_i", [P, 1], I32)
        nxt_f = sb("nxt_f", [P, 1])
        flags = sb("flags", [P, 8])
        sel = sb("sel", [P, N])
        ident = sb("ident", [P, P])
        ones = sb("ones", [P, P])
        diag = sb("diag", [P, 2, P])
        last_row = sb("last_row", [P, P])
        pass_b = sb("pass_b", [P, P])
        negpass_b = sb("negpass_b", [P, P])
        xs = sb("xs", [NP, NK, D])
        xw = sb("xw", [NP, NK, D])
        xt = sb("xt", [NP, NK, D])
        nid = sb("nid", [NP, NK])
        cross = sb("cross", [NP, NK])
        below = sb("below", [NP, NK])
        start_i = sb("start_i", [NP, NK], I32)
        next_i = sb("next_i", [NP, NK], I32)
        bound_i = sb("bound_i", [NP, NK], I32)
        startf = sb("startf", [NP, NK])
        nextf = sb("nextf", [NP, NK])
        has = sb("has", [NP, NK])
        norm = sb("norm", [NP, NK])
        end_i = sb("end_i", [NP, NK], I32)
        put_i = sb("put_i", [NP, NK], I32)
        negc = sb("negc", [NP, NK])
        nege = sb("nege", [NP, NK])
        small = sb("small", [NP, 3, 2, NK])
        er_n = sb("er_n", [NP, NK, 2])
        er_first = sb("er_first", [P, 2])
        total_i = sb("total_i", [1, 1], I32)
        w03 = sb("w03", [D, 192])
        wst0 = sb("wst0", [P, D])
        wst0h = sb("wst0h", [P, D])
        w1a = sb("w1a", [D, 4 * D])
        wst1 = sb("wst1", [P, 2, D])
        w1t = sb("w1t", [D, 4, D])
        w0t = sb("w0t", [P, D])
        w3t = sb("w3t", [D, D])
        att0 = sb("att0", [P, 2])
        att3 = sb("att3", [D, 2])
        vecs = sb("vecs", [P, 6, D])
        feat_b = sb("feat_b", [NP, 4, D])
        mu_b = sb("mu_b", [P, 12])
        inv_b = sb("inv_b", [P, 12])
        mi_b = sb("mi_b", [P, 12])
        carry_t = sb("carry_t", [P, 4, P + 1])
        mc = sb("mc", [P, 2, P + 1])
        cexp_in = sb("cexp_in", [P, 2, 2, P])
        cexp = sb("cexp", [P, 2, 2, P])
        tail_s = sb("tail_s", [P, 2, P])
        carry = sb("carry", [P, 256])
        st = sb("st", [NP, 12, NK])
        bn = sb("bn", [NP, 3, D])
        parts = prod_tail[0:NP, :].rearrange("p (c f) -> p c f", f=D)
        eps = sb("eps", [P, 1])
        zero = sb("zero", [P, 1])
        nexp_in = sb("nexp_in", [NP, 3, 2, NK])
        nexp = sb("nexp", [NP, 3, 2, NK])
        loop_logit = sb("loop_logit", [NP, NK])

        pt = [ctx.enter_context(nc.psum_tensor(f"pt{i}", [P, 512], F32)) for i in range(2)]
        pa = [ctx.enter_context(nc.psum_tensor(f"pa{i}", [P, 512], F32)) for i in range(4)]
        pb = [ctx.enter_context(nc.psum_tensor(f"pb{i}", [P, 512], F32)) for i in range(2)]

        dve_step = sem("dve_step")
        preset, dst_loaded, w_loaded, x_loaded, attr3_loaded = (sem(n) for n in (
            "preset", "dst_loaded", "w_loaded", "x_loaded", "attr3_loaded"))
        iota_done, total_ready, ident_ready = sem("iota_done"), sem("total_ready"), sem("ident_ready")
        dstf_ready, dst_stored, cross_ready = sem("dstf_ready"), sem("dst_stored"), sem("cross_ready")
        drow = [sem(f"drow{i}") for i in range(DRING)]
        drow_used, starts_ready, starts_stored, next_loaded, put_ready = (sem(n) for n in (
            "drow_used", "starts_ready", "starts_stored", "next_loaded", "put_ready"))
        zero_ready, zeroed, diag_ready, rows_bcast = (sem(n) for n in (
            "zero_ready", "zeroed", "diag_ready", "rows_bcast"))
        wt_psum, wt_copied, att_ready, vec_psum, vec_ready = (sem(n) for n in (
            "wt_psum", "wt_copied", "att_ready", "vec_psum", "vec_ready"))
        gauss_in, gauss_sq, gauss_sum, gauss_ready = (sem(n) for n in (
            "gauss_in", "gauss_sq", "gauss_sum", "gauss_ready"))
        ern_ready, ern_stored, er_first_in, er_put, er_loaded = (sem(n) for n in (
            "ern_ready", "ern_stored", "er_first_in", "er_put", "er_loaded"))
        x_ready, x_stored, sel_ready, negc_psum = (sem(n) for n in (
            "x_ready", "x_stored", "sel_ready", "negc_psum"))
        idx_loaded = [sem(f"idx_loaded{s}") for s in range(U)]
        gathered = [sem(f"gathered{s}") for s in range(U)]
        bond_loaded = [sem(f"bond_loaded{s}") for s in range(U)]
        slot_free = [sem(f"slot_free{l}") for l in range(4)]
        logits_ready = {l: sem(f"logits_ready{l}") for l in (0, 3)}
        w_ready = {l: sem(f"w_ready{l}") for l in (0, 3)}
        dec_ready = [sem(f"dec_ready{l}") for l in range(4)]
        scanned = [sem(f"scanned{l}") for l in range(4)]
        rows_copied = [sem(f"rows_copied{l}") for l in range(4)]
        row_free = [[sem(f"row_free{l}_{r}") for r in range(2)] for l in range(4)]
        tail_ready, tails_t, exp_in, exp_ready, carry_scanned, carry_back, carry_ready = (sem(n) for n in (
            "tail_ready", "tails_t", "exp_in", "exp_ready", "carry_scanned", "carry_back", "carry_ready"))
        corr_psum, corr_copied = sem("corr_psum"), sem("corr_copied")
        ends_in = [sem(f"ends_in{c}") for c in range(len(CHUNKS))]
        proj_read = sem("proj_read")
        agg_ready, agg_t, agg_tc, proj_done, stat_ready, stat_sum, sqrt_in, sqrt_out = (sem(n) for n in (
            "agg_ready", "agg_t", "agg_tc", "proj_done", "stat_ready", "stat_sum", "sqrt_in", "sqrt_out"))
        out_stored = sem("out_stored")
        split_ready = {l: sem(f"split_ready{l}") for l in (1, 2, 3)}
        srow_loaded = {l: sem(f"srow_loaded{l}") for l in (1, 2, 3)}
        srow_ready = {l: sem(f"srow_ready{l}") for l in (1, 2, 3)}
        hot_ready = {l: sem(f"hot_ready{l}") for l in (1, 2, 3)}
        hot_diff = {l: sem(f"hot_diff{l}") for l in (1, 2, 3)}
        hot_made = {l: sem(f"hot_made{l}") for l in (1, 2, 3)}
        hot_used = {l: sem(f"hot_used{l}") for l in (1, 2, 3)}
        filled = {l: sem(f"filled{l}") for l in (1, 2, 3)}

        assert NG == U * IT and J == G * NG

        def wz3(k, ch=65):
            return wz[:, k, :].rearrange("p (f j) -> p f j", f=65)[:, 0:ch, :]

        def dec3(k, ch=65):
            return dec[:, k, :].rearrange("p (f j) -> p f j", f=65)[:, 0:ch, :]

        def run3(k, ch=65):
            return run[:, k, :].rearrange("p (f j) -> p f j", f=65)[:, 0:ch, :]

        def row_slot(l, r):
            w = ROWW[l]
            return rows_big[:, r * G * w:(r + 1) * G * w].rearrange("p (j c) -> p j c", c=w)

        def run_store(l, g):
            return run_tab[l][0:EP, :].rearrange("(p j) c -> p j c", j=J)[:, bass.ds(g * G, G), :]

        def bank_blocks(l):
            per = 512 // CORRW[l]
            return [(b, min(b + per, NK)) for b in range(0, NK, per)]

        def chunk_of(k):
            return next(c for c, (b0, b1) in enumerate(CHUNKS) if b0 <= k < b1)

        ROUNDS = [sum(len(bank_blocks(m)) for m in range(l)) for l in range(5)]
        NPROJ = [1, 2, 0, 1]
        PROJ_READS = [0, len(CHUNKS), 2 * len(CHUNKS), 2 * len(CHUNKS)]
        SOFT = (0, 3)
        BATCHES, BATCH0 = [], []
        for l in range(4):
            BATCH0.append(BATCHES[-1][-1][1] if BATCHES else 0)
            BATCHES.append([])
            n = BATCH0[-1]
            for b0, b1 in CHUNKS:
                pieces = [(b, c) for b in range(b0, b1) for c in range(NPROJ[l])]
                lots = [pieces[i:i + 4] for i in range(0, len(pieces), 4)]
                BATCHES[-1].append((lots, n + len(lots)))
                n += len(lots)
        COPIES = [2, 1, 1, 2]
        CREDIT = [4, 2, 1, 2]
        ROW_USES = [(0, 3), (0, 2), (1, 3), (1, 2), (2, 3)]

        def fetch_bank(c):
            return (pa + pb)[c]

        def rows_in(l):
            return 16 * (IT * sum(GP[:l]) + GP[l])

        def agg_of(l):
            if l == 1:
                return ends[:, :].rearrange("p (k c) -> p k c", k=NK)
            w = 128 if l == 0 else 64
            return wz[0:NP, :, :].rearrange("p a c -> p (a c)")[:, 0:NK * w].rearrange("p (k c) -> p k c", k=NK)

        block = ctx.enter_context(nc.Block())

        @block.sync
        def _(sp):
            def load_indices(l, g, s):
                sp.wait_ge(slot_free[l], g + 1)
                sp.dma_start(idx[:, s, :], src.rearrange("(p j) -> p j", j=J)[:, bass.ds(g * G, G)]
                             ).then_inc(idx_loaded[s], 16)
                if l == 0:
                    sp.dma_start(bond[:, s, :],
                                 attr64.rearrange("(p j) f -> p (j f)", j=J)[:, bass.ds(g * (G * D), G * D)]
                                 ).then_inc(bond_loaded[s], 16)

            dst2 = dst.rearrange("(p j) -> p j", j=J)
            sp.dma_start(dst_i[:, 1:J + 1], dst2).then_inc(dst_loaded, 16)
            sp.wait_ge(preset, 1)
            sp.dma_start(dst_i[1:P, 0:1], dst2[0:P - 1, J - 1:J],
                         allow_slow_non_contiguous=True).then_inc(dst_loaded, 16)
            sp.dma_start(nxt_i[0:P - 1, :], dst2[1:P, 0:1], allow_slow_non_contiguous=True).then_inc(dst_loaded, 16)
            load_indices(0, 0, 0)
            load_indices(0, 1, 1)
            sp.dma_start(xs[:, :, :], x.rearrange("(p k) f -> p k f", k=NK)).then_inc(x_loaded, 16)
            for t, a in ((w03[:, 0:128], w0), (w03[:, 128:192], w3),
                         (att0[:, 0:1], attn_l.rearrange("h (d a) -> (h d) a", a=1)),
                         (att0[:, 1:2], attn_r.rearrange("h (d a) -> (h d) a", a=1)),
                         (att3[:, 0:1], att_src.rearrange("(d a) -> d a", a=1)),
                         (att3[:, 1:2], att_dst.rearrange("(d a) -> d a", a=1)),
                         (wst0[0:D, :], w0[:, 0:D]), (wst0[D:P, :], w0[:, D:2 * D]),
                         (w1a[:, :].rearrange("o (k i) -> o k i", k=4), w1.rearrange("(k o) i -> o k i", k=4)),
                         (mu_b[:, :], mu.rearrange("k d -> (k d)").partition_broadcast(P)),
                         (inv_b[:, :], inv_sigma.rearrange("k d -> (k d)").partition_broadcast(P)),
                         (feat_b[:, 0, :], gamma.partition_broadcast(NP)),
                         (feat_b[:, 1, :], beta.partition_broadcast(NP)),
                         (feat_b[:, 2, :], bias1.partition_broadcast(NP)),
                         (feat_b[:, 3, :], bias3.partition_broadcast(NP))):
                sp.dma_start(t, a).then_inc(w_loaded, 16)
            sp.wait_ge(dstf_ready, 1)
            sp.dma_start(dst_rows, dst_f[:, 1:J + 1]).then_inc(dst_stored, 16)
            sp.wait_ge(zero_ready, 1)
            sp.dma_start(er_edges[0:EP, :].rearrange("(p j) h -> p (j h)", j=J),
                         mx[:, 0:2 * J]).then_inc(zeroed, 16)
            for l in range(4):
                sp.dma_start(run_tab[l][EP:EP + 1, :], mx[0:1, 0:ROWW[l]]).then_inc(zeroed, 16)
            sp.wait_ge(cross_ready, 1)
            sp.dma_start(pseudo[:, :, :], attr3.rearrange("(p j) d -> p j d", j=J)).then_inc(attr3_loaded, 16)
            sp.wait_ge(total_ready, 1)
            sp.dma_start(start_tab[N:N + 1, :], total_i[:, :]).then_inc(starts_stored, 16)

            def store_er():
                sp.dma_start(er_tab.rearrange("(p k) h -> p k h", k=NK), er_n[:, :, :]).then_inc(ern_stored, 16)

            def load_er(n):
                sp.wait_ge(er_put, 16 * NK * n)
                sp.dma_start(er_raw, er_edges[0:EP, :].rearrange("(p j) h -> p j h", j=J)).then_inc(er_loaded, 16)

            for s in range(2, U):
                load_indices(0, s, s)
            sp.wait_ge(ern_ready, 1)
            store_er()
            sp.wait_ge(starts_ready, 1)
            sp.dma_start(start_tab[0:N, :].rearrange("(p k) a -> p (k a)", k=NK), start_i[:, :]
                         ).then_inc(starts_stored, 16)
            sp.wait_ge(starts_stored, 32)
            sp.dma_start(next_i[:, :], start_tab[1:N + 1, :].rearrange("(p k) a -> p (k a)", k=NK)
                         ).then_inc(next_loaded, 16)
            load_er(1)
            for l in range(4):
                if l == 3:
                    for s in range(U):
                        load_indices(l, s, s)
                    sp.wait_ge(ern_ready, 2)
                    store_er()
                    load_er(2)
                with nc.sync.Fori(1 if l in SOFT else 0, IT) as it:
                    for s in range(U):
                        load_indices(l, it * U + s, s)
                if l < 3:
                    sp.wait_ge(x_ready, l + 1)
                    sp.dma_start(x_tab[l + 1].rearrange("(p k) f -> p k f", k=NK),
                                 (xt if l == 1 else xs)[:, :, :]).then_inc(x_stored, 16)
            sp.wait_ge(x_ready, 4)
            sp.dma_start(out.rearrange("(p k) f -> p k f", k=NK), xs[:, :, :]).then_inc(out_stored, 16)
            sp.wait_ge(out_stored, 16)
            sp.wait_ge(x_stored, 48)
            sp.wait_ge(dst_stored, 16)
            sp.wait_ge(zeroed, 80)
            sp.wait_ge(ern_stored, 32)
            sp.wait_ge(starts_stored, 32)
            sp.wait_ge(er_put, 32 * NK)
            for l in range(4):
                sp.wait_ge(row_free[l][0], 16 * (3 * IT + 1))
                sp.wait_ge(row_free[l][1], 16 * (2 * IT + 1))

        @block.gpsimd
        def _(pool):
            nc.gpsimd.iota(nid[:, :], [[1, NK]], base=0, channel_multiplier=NK,
                           allow_small_or_imprecise_dtypes=True).then_inc(iota_done, 1)
            nc.gpsimd.iota(ident[:, :], [[1, P]], base=0, channel_multiplier=-1,
                           allow_small_or_imprecise_dtypes=True).then_inc(iota_done, 1)
            nc.gpsimd.iota(total_i[:, :], [[1, 1]], base=E, channel_multiplier=0).then_inc(total_ready, 1)
            nc.gpsimd.iota(sel[:, :], [[1, N]], base=0, channel_multiplier=0,
                           allow_small_or_imprecise_dtypes=True).then_inc(iota_done, 1)

            def fetch_dst_rows():
                pool.wait_ge(dst_stored, 16)
                pool.wait_ge(cross_ready, 1)
                for k in range(NK):
                    if k >= DRING:
                        pool.wait_ge(drow_used, k - DRING + 1)
                    nc.gpsimd.indirect_dma_start(
                        drows[:, k % DRING, :], None, dst_rows,
                        bass.IndirectOffsetOnAxis(ap=bound_i[:, k:k + 1], axis=0)).then_inc(drow[k % DRING], 16)

            def gather_group(l, loads, s):
                pool.wait_ge(idx_loaded[s], loads + 16 * IT * l)
                nc.gpsimd.nop(nofuse=True)
                for j in range(GP[l]):
                    nc.gpsimd.indirect_dma_start(
                        ring[:, s, j, 0:D], None, x_tab[l],
                        bass.IndirectOffsetOnAxis(ap=idx[:, s, j:j + 1], axis=0)).then_inc(gathered[s], 16)

            def scatter_er(n):
                pool.wait_ge(ern_stored, 16 * n)
                if n == 1:
                    pool.wait_ge(put_ready, 1)
                    pool.wait_ge(zeroed, 80)
                for k in range(NK):
                    nc.gpsimd.indirect_dma_start(
                        er_edges, bass.IndirectOffsetOnAxis(ap=put_i[:, k:k + 1], axis=0),
                        er_n[:, k, :], None).then_inc(er_put, 16)
                nc.gpsimd.indirect_dma_start(
                    er_first[:, :], None, er_tab,
                    bass.IndirectOffsetOnAxis(ap=dst_i[:, 1:2], axis=0)).then_inc(er_first_in, 16)

            for l in range(4):
                if l > 0:
                    pool.wait_ge(x_stored, 16 * l)
                if l in SOFT:
                    gather_group(l, 16, 0)
                    if l == 0:
                        fetch_dst_rows()
                        gather_group(l, 16, 1)
                    scatter_er(1 if l == 0 else 2)
                    for s in range(2 if l == 0 else 1, U):
                        gather_group(l, 16, s)
                with nc.gpsimd.Fori(1 if l in SOFT else 0, IT) as it:
                    for s in range(U):
                        gather_group(l, it * 16 + 16, s)
                pool.wait_ge(row_free[l][0], 16 * (3 * IT + 1))
                pool.wait_ge(row_free[l][1], 16 * (2 * IT + 1))
                for k in range(NK):
                    nc.gpsimd.indirect_dma_start(
                        ends[:, k * ROWW[l]:(k + 1) * ROWW[l]], None, run_tab[l],
                        bass.IndirectOffsetOnAxis(ap=end_i[:, k:k + 1], axis=0)).then_inc(ends_in[chunk_of(k)], 16)

        @block.scalar
        def _(act):
            act.wait_ge(w_loaded, 16 * 15)
            nc.scalar.mul(wst0h[:, :], wst0[:, :], 0.5).then_inc(wt_copied, 1)
            act.wait_ge(wt_psum, 1)
            nc.scalar.copy(w0t[:, :], pb[0][:, 0:D]).then_inc(wt_copied, 1)
            nc.scalar.copy(w3t[:, :], pb[0][0:D, D:2 * D]).then_inc(wt_copied, 1)
            nc.scalar.copy(wst1[:, :, :], pb[0][:, 2 * D:4 * D].rearrange("p (a o) -> p a o", a=2)
                           ).then_inc(wt_copied, 1)
            nc.scalar.copy(w1t[:, :, :], pb[0][0:D, 4 * D:8 * D].rearrange("p (k o) -> p k o", k=4)).then_inc(wt_copied, 1)
            act.wait_ge(vec_psum, 1)
            nc.scalar.copy(vecs[:, :, :], pb[1][:, 0:6 * D].rearrange("p (v f) -> p v f", v=6)).then_inc(vec_ready, 1)

            act.wait_ge(gauss_in, 1)
            act.wait_ge(attr3_loaded, 16)
            for k in range(4):
                if k >= 2:
                    act.wait_ge(gauss_sum, k - 1)
                for d in range(3):
                    nc.scalar.activation(squares[:, k % 2, d, :], pseudo[:, :, d], ACT.Square,
                                         bias=mi_b[:, 3 * k + d:3 * k + d + 1],
                                         scale=inv_b[:, 3 * k + d:3 * k + d + 1]).then_inc(gauss_sq, 1)
            act.wait_ge(gauss_sum, 4)
            nc.scalar.activation(gauss[:, :, :], gauss[:, :, :], ACT.Exp, scale=-0.5).then_inc(gauss_ready, 1)

            def decays(l, g, s):
                act.wait_ge(scanned[l], g * UNITS[l] + 1)
                if l in SOFT:
                    for h in range(UNITS[l]):
                        nc.scalar.copy(dec3(h)[:, :, 1:G + 1],
                                       wexp[:, s, 1, h:h + 1, :].broadcast_to([P, 65, G])).then_inc(dec_ready[l], 1)
                else:
                    flag = keep if l == 1 else neg
                    nc.scalar.copy(dec3(s % 2, D)[:, :, 1:G + 1],
                                   flag[:, bass.ds(g * G, G)].rearrange("p (a j) -> p a j", a=1)
                                   .broadcast_to([P, D, G])).then_inc(dec_ready[l], 1)

            def store_rows(l, g, it, s):
                before, per = ROW_USES[s]
                units, ch, stride = UNITS[l], CH[l], ROWW[l] // UNITS[l]
                slot = row_slot(l, s % 2)
                act.wait_ge(row_free[l][s % 2], it * (16 * per) + 16 * (before + 1))
                for k in range(units):
                    act.wait_ge(scanned[l], g * units + (k + 2))
                    nc.scalar.copy(slot[:, :, k * stride:k * stride + ch],
                                   run3(k % 2, ch)[:, :, 1:G + 1].rearrange("p f j -> p j f")
                                   ).then_inc(rows_copied[l], 1)
                    if l in SOFT:
                        nc.scalar.copy(slot[:, :, k * stride + 65:k * stride + 66],
                                       mxv[:, k, bass.ds(g * G + 1, G)].rearrange("p (j a) -> p j a", a=1)
                                       ).then_inc(rows_copied[l], 1)
                act.wait_ge(rows_copied[l], g * (units * COPIES[l]) + (units * COPIES[l] + CREDIT[l]))
                act.dma_start(run_store(l, g), slot).then_inc(row_free[l][s % 2], 16)

            def load_srow(l, n):
                act.dma_start(srow32(l), src_t[bass.ds(n * G + GP[l], C[l]), :].rearrange("c e -> (c e)")
                              .partition_broadcast(NP)).then_inc(srow_loaded[l], 16)

            def convert_srow(l, n, slot):
                act.wait_ge(srow_loaded[l], n * 16 + 16)
                act.wait_ge(hot_ready[l], n * DVE_LOTS[l] + DVE_LOTS[l])
                nc.scalar.copy(srow16(l, slot), srow32(l).rearrange("p (c e) -> p c e", c=C[l])
                               ).then_inc(srow_ready[l], 1)
                act.wait_ge(srow_ready[l], n + 1)
                if not isinstance(n, int) or n + 1 < NG:
                    load_srow(l, n + 1)

            def hot_lots(l, n, slot):
                for i in range(DVE_LOTS[l], LOTS):
                    act.wait_ge(hot_used[l], n * LOTS + (i + 1))
                    for b in range(LB):
                        k = i * LB + b
                        nc.scalar.activation(hot(l, i)[:, b, :].rearrange("p (c e) -> p c e", c=C[l]),
                                             srow16(l, slot), ACT.Abs, bias=nid[:, k:k + 1],
                                             scale=-1.0).then_inc(hot_diff[l], 1)
                    done = (LOTS - DVE_LOTS[l]) * LB
                    act.wait_ge(hot_diff[l], n * done + (i - DVE_LOTS[l] + 1) * LB)
                    nc.scalar.activation(hot(l, i), hot(l, i), ACT.Relu, bias=ones[0:NP, 0:1],
                                         scale=-1.0).then_inc(hot_made[l], 1)

            rounds = exps = roots = batch = 0

            def node_exp(t, shape_in):
                act.wait_ge(exp_in, exps + 1)
                nc.scalar.activation(t, shape_in, ACT.Exp).then_inc(exp_ready, 1)

            def node_sqrt(t, sums=None, scale=1.0 / D, bias=eps):
                act.wait_ge(sqrt_in, roots + 1)
                nc.scalar.activation(t, t if sums is None else sums, ACT.Sqrt, scale=scale,
                                     bias=bias[0:NP, :]).then_inc(sqrt_out, 1)

            for l in range(4):
                units = UNITS[l]
                nc.scalar.sem_inc(row_free[l][0], 16)
                nc.scalar.sem_inc(row_free[l][1], 16)
                nc.scalar.sem_inc(rows_copied[l], CREDIT[l])
                ahead = AHEAD[l]
                if ahead:
                    nc.scalar.sem_inc(hot_ready[l], 2 * DVE_LOTS[l])
                    load_srow(l, 0)
                    act.wait_ge(split_ready[l], 1)
                    for n in range(ahead + 1):
                        convert_srow(l, n, n)
                        hot_lots(l, n, n)

                def act_group(it, s):
                    g = it * U + s
                    more = ahead and (not isinstance(g, int) or g + ahead + 1 < NG)
                    if more:
                        convert_srow(l, g + (ahead + 1), s + ahead + 1)
                    if l in SOFT:
                        act.wait_ge(logits_ready[l], g + 1)
                        nc.scalar.activation(wexp[:, s, :, 0:units, :], wexp_in[:, s, :, 0:units, :],
                                             ACT.Exp).then_inc(w_ready[l], 1)
                        act.wait_ge(w_ready[l], g + 1)
                    if l in SOFT:
                        decays(l, g, s)
                    if l == 2:
                        act.wait_ge(gathered[s], it * (16 * GP[l]) + rows_in(l))
                        act.wait_ge(filled[2], g + 2)
                        nc.scalar.copy(wz3(s % 2, D)[:, :, 1:G + 1],
                                       ring[:, s, :, 0:D].rearrange("p j f -> p f j")).then_inc(slot_free[2], 1)
                    store_rows(l, g, it, s)
                    if l not in SOFT and (not isinstance(g, int) or g + 1 < NG):
                        decays(l, g + 1, (s + 1) % U)
                    if more:
                        hot_lots(l, g + (ahead + 1), s + ahead + 1)

                if l not in SOFT:
                    decays(l, 0, 0)
                with nc.scalar.Fori(0, IT - 1) as it:
                    for s in range(U):
                        act_group(it, s)
                for s in range(U):
                    act_group(IT - 1, s)

                if l in SOFT:
                    node_exp(cexp[:, :, 0:units, :], cexp_in[:, :, 0:units, :])
                    exps += 1
                act.wait_ge(carry_back, l + 1)
                width = CORRW[l]
                nc.scalar.copy(carry[:, 0:width], pb[1][:, 0:width]).then_inc(carry_ready, 1)
                for b0, b1 in bank_blocks(l):
                    act.wait_ge(corr_psum, rounds + 1)
                    nc.scalar.copy(corr[:, b0 * width:b1 * width],
                                   pa[rounds % 4][0:NP, 0:(b1 - b0) * width]).then_inc(corr_copied, 1)
                    rounds += 1
                width = 64 if l == 3 else 128
                for b0, b1 in CHUNKS:
                    if l in SOFT:
                        parts = 2 if l == 0 else 3
                        node_exp(nexp[:, 0:parts, 0:units, b0:b1], nexp_in[:, 0:parts, 0:units, b0:b1])
                        exps += 1
                    for lot in BATCHES[l][chunk_of(b0)][0]:
                        act.wait_ge(agg_t, batch + 1)
                        if batch >= 2:
                            act.wait_ge(proj_done, batch - 1)
                        nc.scalar.copy(proj_t[0:width, batch % 2, 0:len(lot) * NP],
                                       pt[batch % 2][0:width, 0:len(lot) * NP]).then_inc(agg_tc, 1)
                        batch += 1
                    if l in (1, 3) and b0:
                        node_sqrt(st[:, 1, last[0]:last[1]])
                        roots += 1
                    elif l == 2:
                        node_sqrt(st[:, 1, b0:b1])
                        roots += 1
                    last = b0, b1
                if l in (1, 3):
                    node_sqrt(st[:, 1, last[0]:last[1]])
                    roots += 1
                if l == 0:
                    node_sqrt(norm[:, :], scale=1.0, bias=zero)
                    roots += 1
                    act.wait_ge(stat_sum, 2)
                    node_sqrt(bn[:, 2, :], pb[0][0:NP, 0:D], 1.0 / N)
                    roots += 1
                    node_sqrt(st[:, 1, :])
                    roots += 1

        @block.tensor
        def _(pe):
            pe.wait_ge(diag_ready, 1)
            nc.tensor.matmul(pa[0][:, 0:256], ones[:, :], diag[:, 0:2, :].rearrange("p a b -> p (a b)"),
                             start=True, stop=True).then_inc(rows_bcast, 1)
            pe.wait_ge(w_loaded, 16 * 15)
            nc.tensor.transpose(pb[0][:, 0:D], w03[:, 0:128], ident[0:D, 0:D])
            nc.tensor.transpose(pb[0][0:D, D:2 * D], w03[:, 128:192], ident[0:D, 0:D])
            for a in range(2):
                last = nc.tensor.transpose(pb[0][:, (2 + a) * D:(3 + a) * D], w1a[:, a * 128:(a + 1) * 128],
                                           ident[0:D, 0:D])
            for k in range(4):
                last = nc.tensor.transpose(pb[0][0:D, (4 + k) * D:(5 + k) * D], w1a[:, k * D:(k + 1) * D], ident[0:D, 0:D])
            last.then_inc(wt_psum, 1)
            pe.wait_ge(wt_copied, 5)
            pe.wait_ge(att_ready, 1)
            for v in range(4):
                nc.tensor.matmul(pb[1][:, v * D:(v + 1) * D], attb[:, v, :], w0t[:, :], start=True, stop=True)
            for v in range(4, 6):
                last = nc.tensor.matmul(pb[1][:, v * D:(v + 1) * D], attb[0:D, v, :], w3t[:, :], start=True, stop=True)
            last.then_inc(vec_psum, 1)
            pe.wait_ge(sel_ready, 1)
            for b in range(NK):
                last = nc.tensor.matmul(pt[1][0:NP, b:b + 1], sel[:, b::NK], ones[:, 0:1], start=True, stop=True)
            last.then_inc(negc_psum, 1)

            rounds = 0
            for l in range(4):
                units, ch, w = UNITS[l], CH[l], CORRW[l]
                stride = ROWW[l] // units
                if AHEAD[l]:
                    pe.wait_ge(split_ready[l], 1)

                    def fetch(it, s):
                        g = it * U + s
                        pe.wait_ge(filled[l], g + 1)
                        for i in range(LOTS):
                            made = DVE_LOTS[l]
                            if i < made:
                                pe.wait_ge(hot_ready[l], g * made + (2 * made + i + 1))
                            else:
                                pe.wait_ge(hot_made[l], g * (LOTS - made) + (i - made + 1))
                            for b in range(LB):
                                for c in range(C[l]):
                                    last = nc.tensor.matmul(
                                        fetch_bank(c)[:, 0:3 * D], hot(l, i)[:, b, c * P:(c + 1) * P],
                                        split(l)[:, i * LB + b, :, :].rearrange("p t f -> p (t f)"),
                                        start=(i == 0 and b == 0), stop=(i == LOTS - 1 and b == LB - 1))
                            last.then_inc(hot_used[l], 1)

                    with nc.tensor.Fori(0, IT) as it:
                        for s in range(U):
                            fetch(it, s)
                pe.wait_ge(tail_ready, l + 1)
                if l in SOFT:
                    nc.tensor.matmul(pt[0][:, 0:units * P], ones[:, :],
                                     diag[:, 0:units, :].rearrange("p a b -> p (a b)"), start=True, stop=True)
                for k in range(units):
                    last = nc.tensor.transpose(pb[0][0:ch, k * P:(k + 1) * P],
                                               wz3(k, ch)[:, :, 0:1].rearrange("p f a -> p (f a)"), ident[:, :])
                last.then_inc(tails_t, 1)
                pe.wait_ge(carry_scanned, l + 1)
                if l == 1:
                    for k in range(4):
                        last = nc.tensor.matmul(pb[1][:, 0:D], carry_t[0:D, k, 0:P], w1t[:, k, :],
                                                start=(k == 0), stop=(k == 3))
                else:
                    for k in range(units):
                        last = nc.tensor.transpose(pb[1][:, k * stride:k * stride + ch], carry_t[0:ch, k, 0:P],
                                                   ident[0:ch, 0:ch])
                        if l in SOFT:
                            last = nc.tensor.transpose(pb[1][:, k * stride + 65:k * stride + 66], mc[0:1, k, 0:P],
                                                       ident[0:1, 0:1])
                last.then_inc(carry_back, 1)
                pe.wait_ge(carry_ready, l + 1)
                for b0, b1 in bank_blocks(l):
                    if rounds >= 4:
                        pe.wait_ge(corr_copied, rounds - 3)
                    for b in range(b0, b1):
                        last = nc.tensor.matmul(pa[rounds % 4][0:NP, (b - b0) * w:(b - b0 + 1) * w],
                                                sel[:, b::NK], carry[:, 0:w], start=True, stop=True)
                    last.then_inc(corr_psum, 1)
                    rounds += 1
                if not NPROJ[l]:
                    continue
                width = 64 if l == 3 else 128
                agg = agg_of(l)
                if l > 0:
                    pe.wait_ge(proj_read, PROJ_READS[l])
                pe.wait_ge(corr_copied, ROUNDS[l + 1])

                def arrived(c):
                    if l == 1:
                        b0, b1 = CHUNKS[c]
                        pe.wait_ge(ends_in[c], 16 * 2 * (b1 - b0))
                    else:
                        pe.wait_ge(agg_ready, (0 if l == 0 else len(CHUNKS)) + c + 1)

                def turn(n, lot):
                    if n >= 2:
                        pe.wait_ge(agg_tc, n - 1)
                    for i, (b, c) in enumerate(lot):
                        last = nc.tensor.transpose(pt[n % 2][0:width, i * NP:(i + 1) * NP],
                                                   agg[:, b, c * 128:c * 128 + width], ident[0:NP, 0:NP])
                    last.then_inc(agg_t, 1)

                for chunk, (b0, b1) in enumerate(CHUNKS):
                    lots = BATCHES[l][chunk][0]
                    n0 = BATCHES[l][chunk][1] - len(lots)
                    arrived(chunk)
                    turn(n0, lots[0])
                    for n, lot in enumerate(lots, n0):
                        if n - n0 + 1 < len(lots):
                            turn(n + 1, lots[n - n0 + 1])
                        pe.wait_ge(agg_tc, n + 1)
                        for i, (b, c) in enumerate(lot):
                            rhs = wst0h[:, :] if l == 0 else wst1[:, c, :] if l == 1 else w03[:, 128:192]
                            product = pa[chunk][0:NP, (b - b0) * D:(b - b0 + 1) * D]
                            last = nc.tensor.matmul(product, proj_t[0:width, n % 2, i * NP:(i + 1) * NP], rhs,
                                                    start=(c == 0), stop=(c == NPROJ[l] - 1))
                        last.then_inc(proj_done, 1)
                if l == 0:
                    for c in range(len(CHUNKS)):
                        pe.wait_ge(stat_ready, c + 1)
                        last = nc.tensor.matmul(pb[0][0:NP, 0:D], ones[0:NP, 0:NP], parts[:, c, :],
                                                start=(c == 0), stop=(c == len(CHUNKS) - 1))
                    last.then_inc(stat_sum, 1)
                    pe.wait_ge(stat_ready, len(CHUNKS) + 1)
                    nc.tensor.matmul(pb[0][0:NP, 0:D], ones[0:NP, 0:NP], bn[:, 0, :],
                                     start=True, stop=True).then_inc(stat_sum, 1)

        @block.vector
        def _(dve):
            v = nc.vector
            step = Step(dve, dve_step)
            link = step.link

            v.memset(dst_i[:, 0:1], -1)
            v.memset(nxt_i[:, :], -1).then_inc(preset, 1)
            v.sem_inc(slot_free[0], U)
            v.memset(ones[:, :], 1.0)
            v.memset(eps[:, :], EPS)
            v.memset(zero[:, :], 0.0)
            v.memset(carry_t[:, :, 0:1], 0.0)
            v.memset(mc[:, :, 0:1], -BIG)
            v.memset(ring[:, :, :, D:D + 1], 1.0)
            v.memset(attb[:, :, :], 0.0)
            link(v.memset(mx[:, :], 0.0))
            v.sem_inc(zero_ready, 1)
            dve.wait_ge(iota_done, 2)
            link(v.tensor_scalar(ident[:, :], ident[:, :], 0.0, None, ALU.is_equal))
            dve.wait_ge(dst_loaded, 48)
            v.tensor_copy(nxt_f[:, :], nxt_i[:, :])
            link(v.tensor_copy(dst_f[:, :], dst_i[:, :]))
            v.sem_inc(dstf_ready, 1)
            first, last = dst_f[:, 1:2], dst_f[:, J:J + 1]
            CONT, SINGLE, NEXT, PASS, STOP, TAKE = range(6)

            def fl(i):
                return flags[:, i:i + 1]
            v.tensor_tensor(keep[:, :], dst_f[:, 1:J + 1], dst_f[:, 0:J], ALU.is_equal)
            v.tensor_tensor(fl(CONT), first, dst_f[:, 0:1], ALU.is_equal)
            v.tensor_tensor(fl(SINGLE), first, last, ALU.is_equal)
            link(v.tensor_tensor(fl(NEXT), nxt_f[:, :], last, ALU.is_equal))
            v.tensor_tensor(fl(PASS), fl(CONT), fl(SINGLE), ALU.mult)
            link(v.tensor_tensor(fl(STOP), fl(SINGLE), fl(NEXT), ALU.mult))
            v.tensor_scalar(neg[:, :], keep[:, :], -1.0, BIG, ALU.add, ALU.mult)
            v.tensor_scalar(diag[:, 0, :], ident[:, :], last, None, ALU.mult)
            link(v.tensor_scalar(diag[:, 1, :], ident[:, :], fl(PASS), None, ALU.mult))
            v.sem_inc(diag_ready, 1)
            link(v.tensor_scalar(fl(TAKE), fl(STOP), -1.0, 1.0, ALU.mult, ALU.add))
            link(v.tensor_tensor(fl(TAKE), fl(TAKE), fl(CONT), ALU.mult))
            dve.wait_ge(rows_bcast, 1)
            v.tensor_copy(pass_b[:, :], pa[0][:, P:2 * P])
            v.tensor_scalar(negpass_b[:, :], pa[0][:, P:2 * P], -1.0, BIG, ALU.add, ALU.mult)
            link(v.tensor_copy(last_row[:, :], pa[0][:, 0:P]))
            less = wz[0:NP, :, :].rearrange("p a c -> p (a c)")[:, 0:NK * P].rearrange("p (k b) -> p k b", k=NK)
            dve.wait_ge(iota_done, 3)
            link(v.tensor_tensor(less, last_row[0:NP, :].rearrange("p (a b) -> p a b", a=1).broadcast_to([NP, NK, P]),
                                 nid[:, :].rearrange("p (k a) -> p k a", a=1).broadcast_to([NP, NK, P]), ALU.is_lt))
            link(v.tensor_reduce(cross[:, :], less, AX, ALU.add))
            link(v.tensor_scalar(cross[:, :], cross[:, :], float(P - 1), None, ALU.min))
            link(v.tensor_copy(bound_i[:, :], cross[:, :]))
            v.sem_inc(cross_ready, 1)
            dve.wait_ge(w_loaded, 16 * 15)
            for a, (p0, p1) in ((0, (0, D)), (1, (D, P))):
                v.tensor_scalar(attb[p0:p1, a, :], ones[p0:p1, :], att0[p0:p1, 0:1], None, ALU.mult)
                v.tensor_scalar(attb[p0:p1, 2 + a, :], ones[p0:p1, :], att0[p0:p1, 1:2], None, ALU.mult)
            v.tensor_scalar(attb[0:D, 4, :], ones[0:D, :], att3[:, 0:1], None, ALU.mult)
            link(v.tensor_scalar(attb[0:D, 5, :], ones[0:D, :], att3[:, 1:2], None, ALU.mult))
            v.sem_inc(att_ready, 1)
            link(v.scalar_tensor_tensor(mi_b[:, :], mu_b[:, :], -1.0, inv_b[:, :], ALU.mult, ALU.mult))
            v.sem_inc(gauss_in, 1)
            link(v.tensor_scalar(sel[:, :], sel[:, :], first, fl(TAKE), ALU.is_equal, ALU.mult))
            v.sem_inc(sel_ready, 1)

            def node_dot(dst_ap, vec):
                link(v.tensor_tensor(xt[:, :, :], xs[:, :, :], vec.rearrange("p (a f) -> p a f", a=1)
                                     .broadcast_to([NP, NK, D]), ALU.mult))
                link(v.tensor_reduce(dst_ap, xt[:, :, :], AX, ALU.add))

            dve.wait_ge(vec_ready, 1)
            dve.wait_ge(x_loaded, 16)
            node_dot(er_n[:, :, 0], vecs[0:NP, 2, :])
            node_dot(er_n[:, :, 1], vecs[0:NP, 3, :])
            v.sem_inc(ern_ready, 1)
            for k in range(NK):
                dve.wait_ge(drow[k % DRING], 16 * (k // DRING + 1))
                v.tensor_scalar(drows[:, k % DRING, :], drows[:, k % DRING, :], nid[:, k:k + 1], None,
                                ALU.is_lt, ALU.add, accum_out=below[:, k:k + 1]).then_inc(drow_used, 1)
            dve.wait_ge(drow_used, NK)
            link(v.scalar_tensor_tensor(startf[:, :], cross[:, :], float(J), below[:, :], ALU.mult, ALU.add))
            link(v.tensor_copy(start_i[:, :], startf[:, :]))
            v.sem_inc(starts_ready, 1)
            dve.wait_ge(next_loaded, 16)
            link(v.tensor_copy(nextf[:, :], next_i[:, :]))
            deg, t0, t1 = st[:, 2, :], st[:, 3, :], st[:, 4, :]
            v.tensor_scalar(t1, nextf[:, :], -1.0 - EP, None, ALU.add)
            link(v.tensor_tensor(deg, nextf[:, :], startf[:, :], ALU.subtract))
            v.tensor_scalar(norm[:, :], deg, 1.0, None, ALU.max)
            link(v.tensor_scalar(has[:, :], deg, 1.0, None, ALU.min))
            link(v.tensor_scalar(nege[:, :], has[:, :], -1.0, BIG, ALU.add, ALU.mult))
            link(v.tensor_tensor(t1, t1, has[:, :], ALU.mult))
            link(v.tensor_scalar(t1, t1, float(EP), None, ALU.add))
            v.tensor_copy(end_i[:, :], t1)
            link(v.tensor_scalar(t0, nid[:, :], float(EP), None, ALU.add))
            link(v.tensor_tensor(t1, startf[:, :], t0, ALU.subtract))
            link(v.tensor_tensor(t1, t1, has[:, :], ALU.mult))
            link(v.tensor_tensor(t0, t0, t1, ALU.add))
            link(v.tensor_copy(put_i[:, :], t0))
            v.sem_inc(put_ready, 1)
            for k in range(4):
                dve.wait_ge(gauss_sq, 3 * (k + 1))
                link(v.tensor_tensor(gauss[:, k, :], squares[:, k % 2, 0, :], squares[:, k % 2, 1, :], ALU.add))
                link(v.tensor_tensor(gauss[:, k, :], gauss[:, k, :], squares[:, k % 2, 2, :], ALU.add))
                v.sem_inc(gauss_sum, 1)

            def expand_er(n, heads):
                dve.wait_ge(er_loaded, 16 * n)
                dve.wait_ge(er_first_in, 16 * n)
                for h in range(heads):
                    last_scan = v.tensor_tensor_scan(er[:, h, :], keep[:, :], er_raw[:, :, h], er_first[:, h:h + 1],
                                                     ALU.mult, ALU.add)
                link(last_scan)
                link(v.memset(mxv[:, :, 0:1], -BIG))

            def split_features(l, t):
                link(v.tensor_copy(split(l)[:, :, 0, :], t))
                link(v.tensor_tensor(xw[:, :, :], t, split(l)[:, :, 0, :], ALU.subtract))
                link(v.tensor_copy(split(l)[:, :, 1, :], xw[:, :, :]))
                link(v.tensor_tensor(xw[:, :, :], xw[:, :, :], split(l)[:, :, 1, :], ALU.subtract))
                link(v.tensor_copy(split(l)[:, :, 2, :], xw[:, :, :]))
                v.sem_inc(split_ready[l], 1)
                v.sem_inc(hot_used[l], LOTS)
                v.sem_inc(filled[l], 1)

            def make_hot(l, g, slot):
                if isinstance(g, int) and g >= NG:
                    return
                dve.wait_ge(srow_ready[l], g + 1)
                for i in range(DVE_LOTS[l]):
                    dve.wait_ge(hot_used[l], g * LOTS + (i + 1))
                    for b in range(LB):
                        k = i * LB + b
                        last_hot = v.tensor_scalar(hot(l, i)[:, b, :].rearrange("p (c e) -> p c e", c=C[l]),
                                                   srow16(l, slot), nid[:, k:k + 1], None, ALU.is_equal)
                    last_hot.then_inc(hot_ready[l], 1)

            def fill(l, g, slot):
                if isinstance(g, int) and g >= NG:
                    return
                slot = slot % U
                dve.wait_ge(hot_used[l], g * LOTS + 2 * LOTS)
                dve.wait_ge(slot_free[l], g + 1)
                for c in range(C[l]):
                    ins = v.tensor_reduce(ring[:, slot, GP[l] + c, 0:D],
                                          fetch_bank(c)[:, 0:3 * D].rearrange("p (t f) -> p f t", t=3),
                                          AX, ALU.add)
                ins.then_inc(filled[l], 1)

            def prepare(l):
                op_max = l == 2
                for k in range(4):
                    v.memset(wz3(k)[:, :, 0:1], -BIG if op_max else 0.0)
                for k in range(2):
                    ins = v.memset(dec3(k)[:, :, 0:1], -BIG if op_max else 0.0)
                link(ins)
                v.sem_inc(scanned[l], 1)

            def logits(l, g, it, s):
                heads = UNITS[l]
                vec0 = 0 if l == 0 else 4
                dve.wait_ge(gathered[s], it * (16 * GP[l]) + rows_in(l))
                if l == 3:
                    dve.wait_ge(filled[l], g + 2)
                if l == 0:
                    dve.wait_ge(bond_loaded[s], it * 16 + 16)
                    link(v.tensor_tensor(ring[:, s, :, 0:D], ring[:, s, :, 0:D],
                                         bond[:, s, :].rearrange("p (j f) -> p j f", j=G), ALU.add))
                for h in range(heads):
                    ins = v.tensor_tensor(prod[:, h, :, :], ring[:, s, :, 0:D],
                                          vecs[:, vec0 + h:vec0 + h + 1, :].broadcast_to([P, G, D]), ALU.mult)
                link(ins)
                link(v.tensor_reduce(dot[:, 0:heads, :], prod[:, 0:heads, :, :], AX, ALU.add))
                link(v.tensor_tensor(dot[:, 0:heads, :], dot[:, 0:heads, :], er[:, 0:heads, bass.ds(g * G, G)], ALU.add))
                link(v.scalar_tensor_tensor(logit[:, 0:heads, :], dot[:, 0:heads, :], SLOPE, dot[:, 0:heads, :],
                                            ALU.mult, ALU.max))
                for h in range(heads):
                    ins = v.tensor_tensor_scan(mxv[:, h, bass.ds(g * G + 1, G)], neg[:, bass.ds(g * G, G)],
                                               logit[:, h, :], mxv[:, h, bass.ds(g * G, 1)], ALU.add, ALU.max)
                link(ins)
                now, before = mxv[:, 0:heads, bass.ds(g * G + 1, G)], mxv[:, 0:heads, bass.ds(g * G, G)]
                link(v.tensor_tensor(wexp_in[:, s, 1, 0:heads, :], before,
                                     neg[:, bass.ds(g * G, G)].rearrange("p (a j) -> p a j", a=1)
                                     .broadcast_to([P, heads, G]), ALU.add))
                v.tensor_tensor(wexp_in[:, s, 0, 0:heads, :], logit[:, 0:heads, :], now, ALU.subtract)
                v.tensor_tensor(wexp_in[:, s, 1, 0:heads, :], wexp_in[:, s, 1, 0:heads, :], now,
                                ALU.subtract).then_inc(logits_ready[l], 1)

            def scans(l, g, s):
                units, ch = UNITS[l], CH[l]
                if l in SOFT:
                    dve.wait_ge(w_ready[l], g + 1)
                if l != 2:
                    for k in range(units):
                        weight = wexp[:, s, 0, k:k + 1, :] if l in SOFT else gauss[:, k:k + 1, bass.ds(g * G, G)]
                        ins = v.tensor_tensor(wz3(k, ch)[:, :, 1:G + 1], ring[:, s, :, 0:ch].rearrange("p j f -> p f j"),
                                              weight.broadcast_to([P, ch, G]), ALU.mult)
                    link(ins)
                    v.sem_inc(slot_free[l], 1)
                else:
                    dve.wait_ge(slot_free[2], g + (U + 1))

                def keep_last(k):
                    to = wz3((s + 1) % U % 2 if l == 2 else k, ch)
                    dve.wait_ge(scanned[l], g * units + (k + 2))
                    return v.tensor_copy(to[:, :, 0:1], run3(k % 2, ch)[:, :, G:G + 1])

                for k in range(units):
                    if l in SOFT or k == 0:
                        dve.wait_ge(dec_ready[l], g * (units if l in SOFT else 1) + ((k if l in SOFT else 0) + 1))
                    dve.wait_ge(rows_copied[l], g * (units * COPIES[l]) + (k * COPIES[l] + 1))
                    d = dec[:, k if l in SOFT else s % 2, 0:ch * (G + 1)]
                    z = wz[:, s % 2 if l == 2 else k, 0:ch * (G + 1)]
                    ops = (ALU.add, ALU.max) if l == 2 else (ALU.mult, ALU.add)
                    v.tensor_tensor_scan(run[:, k % 2, 0:ch * (G + 1)], d, z, 0.0, *ops).then_inc(scanned[l], 1)
                    if 0 < k < units - 1:
                        link(keep_last(k - 1))
                    elif k > 0:
                        keep_last(k - 1)
                link(keep_last(units - 1))

            def loop_soft(l):
                a, f = (7, 2) if l == 0 else (6, 2)

                def group(it, s):
                    g = it * U + s
                    nxt = it + 1 if s == U - 1 else it
                    if l == 3:
                        fill(l, g + 1, s + 1)
                        make_hot(l, g + 2, s + 2)
                    if not isinstance(g, int) or g + 1 < NG:
                        logits(l, g + 1, nxt, (s + 1) % U)
                    scans(l, g, s)

                if l == 3:
                    make_hot(l, 0, 0)
                    fill(l, 0, 0)
                    make_hot(l, 1, 1)
                    expand_er(2, 1)
                logits(l, 0, 0, 0)
                with nc.vector.Fori(0, IT - 1) as it:
                    step.enter(it, U * (a + f))
                    for s in range(U):
                        group(it, s)
                step.leave(IT - 1)
                for s in range(U):
                    group(IT - 1, s)

            def loop_plain(l):
                def group(it, s):
                    g = it * U + s
                    fill(l, g, s)
                    make_hot(l, g + 1, s + 1)
                    if l == 1:
                        dve.wait_ge(gathered[s], it * (16 * GP[l]) + rows_in(l))
                        dve.wait_ge(filled[1], g + 2)
                    scans(l, g, s)

                make_hot(l, 0, 0)
                with nc.vector.Fori(0, IT - 1) as it:
                    step.enter(it, U * (1 if l == 2 else 4))
                    for s in range(U):
                        group(it, s)
                step.leave(IT - 1)
                for s in range(U):
                    group(IT - 1, s)

            n_exp = n_root = 0

            def carries(l):
                nonlocal n_exp
                units, ch = UNITS[l], CH[l]
                if l in SOFT:
                    for h in range(units):
                        ins = v.tensor_scalar(diag[:, h, :], ident[:, :], mxv[:, h, J:J + 1], None, ALU.mult)
                    link(ins)
                v.sem_inc(tail_ready, 1)
                dve.wait_ge(tails_t, l + 1)
                tails = pb[0]
                if l in SOFT:
                    mrow = pt[0][:, 0:units * P].rearrange("p (h b) -> p h b", h=units)
                    for h in range(units):
                        ins = v.tensor_tensor_scan(mc[:, h, 1:P + 1], negpass_b[:, :], mrow[:, h, :], -BIG,
                                                   ALU.add, ALU.max)
                    link(ins)
                    v.tensor_tensor(cexp_in[:, 1, 0:units, :], mrow, mc[:, 0:units, 1:P + 1], ALU.subtract)
                    link(v.tensor_tensor(cexp_in[:, 0, 0:units, :], mc[:, 0:units, 0:P],
                                         negpass_b[:, :].rearrange("p (a b) -> p a b", a=1)
                                         .broadcast_to([P, units, P]), ALU.add))
                    v.tensor_tensor(cexp_in[:, 0, 0:units, :], cexp_in[:, 0, 0:units, :], mc[:, 0:units, 1:P + 1],
                                    ALU.subtract).then_inc(exp_in, 1)
                    n_exp += 1
                    dve.wait_ge(exp_ready, n_exp)
                    for h in range(units):
                        ins = v.tensor_tensor(tail_s[0:ch, h, :], tails[0:ch, h * P:(h + 1) * P], cexp[0:ch, 1, h, :],
                                              ALU.mult)
                    link(ins)
                    for h in range(units):
                        ins = v.tensor_tensor_scan(carry_t[0:ch, h, 1:P + 1], cexp[0:ch, 0, h, :], tail_s[0:ch, h, :],
                                                   0.0, ALU.mult, ALU.add)
                else:
                    for k in range(units):
                        ins = v.tensor_tensor_scan(
                            carry_t[0:ch, k, 1:P + 1], (negpass_b if l == 2 else pass_b)[0:ch, :],
                            tails[0:ch, k * P:(k + 1) * P], -BIG if l == 2 else 0.0,
                            *((ALU.add, ALU.max) if l == 2 else (ALU.mult, ALU.add)))
                ins.then_inc(carry_scanned, 1)

            def bk(ap, n):
                return ap.rearrange("p (k a) -> p k a", a=1).broadcast_to([NP, ap.shape[1], n])

            def bf(ap, n=NK):
                return ap.rearrange("p (a f) -> p a f", a=1).broadcast_to([NP, n, D])

            def merge_soft(l, b0, b1):
                nonlocal n_exp
                heads, nk = UNITS[l], b1 - b0
                e4 = ends[:, b0 * ROWW[l]:b1 * ROWW[l]].rearrange("p (k h c) -> p k h c", k=nk, h=heads)
                c4 = corr[:, b0 * ROWW[l]:b1 * ROWW[l]].rearrange("p (k h c) -> p k h c", k=nk, h=heads)
                agg = agg_of(l)[:, b0:b1, :]
                x0, x1, x2 = (nexp_in[:, i, :, b0:b1] for i in range(3))
                f0, f1, f2 = (nexp[:, i, :, b0:b1] for i in range(3))
                m_all, den = small[:, 0, :, b0:b1], small[:, 1, :, b0:b1]
                m_ends = e4[:, :, :, 65].rearrange("p k h -> p h k")
                m_corr = c4[:, :, :, 65].rearrange("p k h -> p h k")
                d_ends = e4[:, :, :, 64].rearrange("p k h -> p h k")
                d_corr = c4[:, :, :, 64].rearrange("p k h -> p h k")

                def both(ap):
                    return ap[:, b0:b1].rearrange("p (a k) -> p a k", a=1).broadcast_to([NP, heads, nk])
                s0, s1 = x0[:, 0:heads, :], x1[:, 0:heads, :]
                m_all, den = m_all[:, 0:heads, :], den[:, 0:heads, :]
                link(v.tensor_tensor(s0, m_ends, both(nege), ALU.add))
                link(v.tensor_tensor(s1, m_corr, both(negc), ALU.add))
                link(v.tensor_tensor(m_all, s0, s1, ALU.max))
                if l == 3:
                    link(v.tensor_tensor(m_all, m_all, both(loop_logit), ALU.max))
                    v.tensor_tensor(x2[:, 0:heads, :], both(loop_logit), m_all, ALU.subtract)
                v.tensor_tensor(s0, s0, m_all, ALU.subtract)
                link(v.tensor_tensor(s1, s1, m_all, ALU.subtract))
                v.sem_inc(exp_in, 1)
                n_exp += 1
                dve.wait_ge(exp_ready, n_exp)
                s0, s1, s2 = f0[:, 0:heads, :], f1[:, 0:heads, :], f2[:, 0:heads, :]
                tmp = small[:, 2, 0:heads, b0:b1]
                v.tensor_tensor(den, d_ends, s0, ALU.mult)
                link(v.tensor_tensor(tmp, d_corr, s1, ALU.mult))
                link(v.tensor_tensor(den, den, tmp, ALU.add))
                if l == 3:
                    link(v.tensor_tensor(den, den, s2, ALU.add))
                link(v.tensor_scalar(den, den, 1e-16 if l == 3 else 0.0, 1e-30, ALU.add, ALU.max))
                link(v.reciprocal(den, den))
                if l == 3:
                    v.tensor_tensor(s2, s2, den, ALU.mult)
                v.tensor_tensor(s0, s0, den, ALU.mult)
                link(v.tensor_tensor(s1, s1, den, ALU.mult))
                for h in range(heads):
                    to = agg[:, :, h * D:(h + 1) * D]
                    v.tensor_tensor(to, e4[:, :, h, 0:D], bk(f0[:, h, :], D), ALU.mult)
                    link(v.tensor_tensor(c4[:, :, h, 0:D], c4[:, :, h, 0:D], bk(f1[:, h, :], D), ALU.mult))
                    ins = v.tensor_tensor(to, to, c4[:, :, h, 0:D], ALU.add)
                    if l == 3:
                        link(ins)
                        link(v.tensor_tensor(xt[:, b0:b1, :], xs[:, b0:b1, :], bk(f2[:, h, :], D), ALU.mult))
                        ins = v.tensor_tensor(to, to, xt[:, b0:b1, :], ALU.add)
                link(ins)
                v.sem_inc(agg_ready, 1)

            def root(t):
                nonlocal n_root
                v.sem_inc(sqrt_in, 1)
                n_root += 1
                dve.wait_ge(sqrt_out, n_root)
                link(v.reciprocal(t, t))

            def free_slots(l):
                if l == 3:
                    link(v.memset(ring[:, :, :, D:D + 1], 1.0))
                v.sem_inc(slot_free[l], U)

            def projected(l, b0, b1):
                dve.wait_ge(proj_done, BATCHES[l][chunk_of(b0)][1])
                p = pa[chunk_of(b0)][0:NP, 0:(b1 - b0) * D].rearrange("p (k f) -> p k f", f=D)
                w = xw[:, b0:b1, :]
                if l == 0:
                    ins = v.tensor_copy(w, p)
                else:
                    ins = v.tensor_tensor(w, w, p, ALU.add)
                link(ins)
                v.sem_inc(proj_read, 1)

            def layer_norm(l, b0, b1):
                mean, var = st[:, 0, b0:b1], st[:, 1, b0:b1]
                w, t = xw[:, b0:b1, :], xt[:, b0:b1, :]
                link(v.tensor_reduce(mean, w, AX, ALU.add))
                link(v.scalar_tensor_tensor(w, bk(mean, D), -1.0 / D, w, ALU.mult, ALU.add))
                link(v.tensor_tensor(t, w, w, ALU.mult))
                link(v.tensor_reduce(var, t, AX, ALU.add))
                root(var)
                if l == 1:
                    link(v.tensor_tensor(mean, var, norm[:, b0:b1], ALU.mult))
                    link(v.tensor_tensor(t, w, bk(mean, D), ALU.mult))
                else:
                    link(v.tensor_tensor(xs[:, b0:b1, :], w, bk(var, D), ALU.mult))

            expand_er(1, 2)
            prepare(0)
            loop_soft(0)
            carries(0)
            dve.wait_ge(negc_psum, 1)
            link(v.tensor_scalar(negc[:, :], pt[1][0:NP, 0:NK], -1.0, BIG, ALU.add, ALU.mult))
            by_f = "p k f -> p f k"

            def part_sum(c):
                b0, b1 = CHUNKS[c]
                projected(0, b0, b1)
                link(v.tensor_reduce(parts[:, c, :], xw[:, b0:b1, :].rearrange(by_f), AX, ALU.add))
                v.sem_inc(stat_ready, 1)

            dve.wait_ge(corr_copied, ROUNDS[1])
            for c, (b0, b1) in enumerate(CHUNKS):
                dve.wait_ge(ends_in[c], 16 * (b1 - b0))
                merge_soft(0, b0, b1)
                if c:
                    part_sum(c - 1)
            free_slots(1)
            part_sum(len(CHUNKS) - 1)
            root(norm[:, :])
            dve.wait_ge(stat_sum, 1)
            link(v.scalar_tensor_tensor(xw[:, :, :], bf(pb[0][0:NP, 0:D]), -1.0 / N, xw[:, :, :], ALU.mult, ALU.add))
            link(v.tensor_tensor(xt[:, :, :], xw[:, :, :], xw[:, :, :], ALU.mult))
            link(v.tensor_reduce(bn[:, 0, :], xt[:, :, :].rearrange(by_f), AX, ALU.add))
            v.sem_inc(stat_ready, 1)
            root(bn[:, 2, :])
            link(v.tensor_tensor(bn[:, 2, :], bn[:, 2, :], feat_b[:, 0, :], ALU.mult))
            link(v.tensor_tensor(xw[:, :, :], xw[:, :, :], bf(bn[:, 2, :]), ALU.mult))
            link(v.tensor_tensor(xw[:, :, :], xw[:, :, :], bf(feat_b[:, 1, :]), ALU.add))
            link(v.scalar_tensor_tensor(xw[:, :, :], xw[:, :, :], 0.0, xs[:, :, :], ALU.max, ALU.add))
            layer_norm(0, 0, NK)
            v.sem_inc(x_ready, 1)

            prepare(1)
            split_features(1, xs[:, :, :])
            dve.wait_ge(gauss_ready, 1)
            loop_plain(1)
            carries(1)
            dve.wait_ge(x_stored, 16)
            link(v.tensor_scalar(xw[:, :, :], xs[:, :, :], 2.0, None, ALU.mult))
            link(v.tensor_tensor(xw[:, :, :], xw[:, :, :], bf(feat_b[:, 2, :]), ALU.add))
            dve.wait_ge(corr_copied, ROUNDS[2])
            link(v.tensor_tensor(xw[:, :, :], xw[:, :, :], corr[:, 0:NK * D].rearrange("p (k f) -> p k f", k=NK),
                                 ALU.add))
            free_slots(2)
            for b0, b1 in CHUNKS:
                projected(1, b0, b1)
                layer_norm(1, b0, b1)
            v.sem_inc(x_ready, 1)
            link(v.tensor_tensor(xs[:, :, :], xw[:, :, :], bk(st[:, 1, :], D), ALU.mult))

            prepare(2)
            split_features(2, xt[:, :, :])
            loop_plain(2)
            carries(2)
            corr2 = corr[:, 0:NK * D].rearrange("p (k f) -> p k f", k=NK)
            ends2 = ends[:, 0:NK * D].rearrange("p (k f) -> p k f", k=NK)
            dve.wait_ge(corr_copied, ROUNDS[3])
            link(v.tensor_tensor(corr2, corr2, bk(negc[:, :], D), ALU.add))
            dve.wait_ge(x_stored, 32)
            for c, (b0, b1) in enumerate(CHUNKS):
                dve.wait_ge(ends_in[c], 16 * 3 * (b1 - b0))
                w = xw[:, b0:b1, :]
                link(v.tensor_tensor(w, corr2[:, b0:b1, :], ends2[:, b0:b1, :], ALU.max))
                link(v.tensor_tensor(w, w, bk(norm[:, b0:b1], D), ALU.mult))
                link(v.tensor_tensor(w, w, xs[:, b0:b1, :], ALU.add))
                layer_norm(2, b0, b1)
            free_slots(3)
            v.sem_inc(x_ready, 1)

            node_dot(er_n[:, :, 0], vecs[0:NP, 5, :])
            v.sem_inc(ern_ready, 1)
            node_dot(st[:, 2, :], vecs[0:NP, 4, :])
            link(v.tensor_tensor(st[:, 2, :], st[:, 2, :], er_n[:, :, 0], ALU.add))
            link(v.scalar_tensor_tensor(loop_logit[:, :], st[:, 2, :], SLOPE, st[:, 2, :], ALU.mult, ALU.max))
            split_features(3, xs[:, :, :])
            prepare(3)
            loop_soft(3)
            carries(3)
            dve.wait_ge(x_stored, 48)
            link(v.tensor_tensor(xw[:, :, :], xs[:, :, :], bf(feat_b[:, 3, :]), ALU.add))
            dve.wait_ge(corr_copied, ROUNDS[4])
            for c, (b0, b1) in enumerate(CHUNKS):
                dve.wait_ge(ends_in[c], 16 * 4 * (b1 - b0))
                merge_soft(3, b0, b1)
                if c:
                    projected(3, *CHUNKS[c - 1])
                    layer_norm(3, *CHUNKS[c - 1])
            projected(3, *CHUNKS[-1])
            layer_norm(3, *CHUNKS[-1])

            v.sem_inc(x_ready, 1)


_INS = ["x", "src", "src_t", "dst", "edge_attr_3", "edge_attr_64", "L0_gnn_W", "L0_gnn_attn_l", "L0_gnn_attn_r",
        "L0_gnn_bn_gamma", "L0_gnn_bn_beta", "L1_gnn_W_fc", "L1_gnn_mu", "L1_gnn_inv_sigma", "L1_gnn_bias",
        "L3_gnn_W", "L3_gnn_att_src", "L3_gnn_att_dst", "L3_gnn_bias"]


def kernel(**inputs):
    import numpy as _np
    import concourse.bacc as _bacc
    from concourse.bass_utils import run_bass_kernel_spmd as _run

    nc = _bacc.Bacc("TRN2", target_bir_lowering=False, num_devices=1)
    arrays, args = {}, []
    for name in _INS:
        a = _np.ascontiguousarray(inputs["src" if name == "src_t" else name])
        if a.shape[0] == E:
            padded = _np.full((EP,) + a.shape[1:], N if name == "dst" else 0, a.dtype)
            padded[:E] = a
            a = padded
        if name == "src_t":
            a = _np.ascontiguousarray(a.reshape(P, J).T)
        arrays[f"in_{name}"] = a
        args.append(nc.dram_tensor(f"in_{name}", a.shape, mybir.dt.from_np(a.dtype), kind="ExternalInput").ap())
    args.append(nc.dram_tensor("out_0", (N, D), F32, kind="ExternalOutput").ap())
    gnn(nc, *args)
    return _run(nc, [arrays], core_ids=[0]).results[0]["out_0"]
```
